# Optimizing a Trainium2 kernel written in Bass

```python
import numpy as np
import jax
import jax.numpy as jnp

def _softmax(x, axis=-1):
    return jax.nn.softmax(x, axis=axis)

def _gelu(x):
    return jax.nn.gelu(x, approximate=True)

def _silu(x):
    return jax.nn.silu(x)

def _sigmoid(x):
    return jax.nn.sigmoid(x)

def _layernorm(x, axis=-1, eps=1e-05):
    m = jnp.mean(x, axis=axis, keepdims=True)
    v = jnp.var(x, axis=axis, keepdims=True)
    return (x - m) / jnp.sqrt(v + eps)

def _scatter_add(tgt, idx, src, axis=0):
    return tgt.at[idx].add(src)

def _segment_sum(src, seg, n):
    return jax.ops.segment_sum(src, seg, n)
kernel_name = 'mk_gnn_preln_d2_gnn_r64_13b90e'

def setup_inputs(seed: int=0):
    np.random.seed(seed)
    _w = jnp.asarray

    def _rec_inputs():
        import jax
        import jax.numpy as jnp
        _gk = jax.random.key(seed)
        x = -0.000202 + 1 * jax.random.normal(jax.random.fold_in(_gk, 1), (50000, 128), jnp.float32)
        src = jax.random.randint(jax.random.fold_in(_gk, 2), (25000,), 0, 50000, jnp.int32)
        dst = jax.random.randint(jax.random.fold_in(_gk, 3), (25000,), 0, 50000, jnp.int32)
        _o = jnp.argsort(dst, stable=True)
        src = src[_o]
        dst = dst[_o]
        edge_attr_16 = jax.random.uniform(jax.random.fold_in(_gk, 12), (25000, 16), jnp.float32, 0.0, 1)
        return (x, src, dst, edge_attr_16)
    x, src, dst, edge_attr_16 = _rec_inputs()

    def _L0_gnn_setup():
        import jax, jax.numpy as jnp
        import numpy as np
        N, E = (50000, 12500)
        F_IN, D, H, FE = (128, 32, 4, 16)
        ALPHA = 0.2
        key = jax.random.key(seed)
        k1, k2, k3, k4, k5 = jax.random.split(key, 5)
        h = jax.random.normal(k1, (N, F_IN), dtype=jnp.float32)
        edge_index = jax.random.randint(k2, (2, E), 0, N, dtype=jnp.int64)
        edge_attr = jax.random.uniform(k3, (E, FE), dtype=jnp.float32)
        W = jax.random.normal(k4, (F_IN, H * D), dtype=jnp.float32) * 0.1
        a = jax.random.normal(k5, (H, 2 * D + FE), dtype=jnp.float32) * 0.1
        return {'h': h, 'edge_attr': edge_attr, 'W': W, 'a': a, 'edge_index': edge_index}
    _L0_gnn_all = _L0_gnn_setup()
    _L0_gnn_in = {k: v for k, v in _L0_gnn_all.items() if k in ('W', 'a')}
    del _L0_gnn_all

    def _L1_gnn_setup():
        import jax, jax.numpy as jnp
        import numpy as np
        N, E, D, H, L = (50000, 12500, 128, 8, 3)
        HD = D // H

        def _layernorm(h, gamma, beta, eps=1e-05):
            mu = h.mean(-1, keepdims=True)
            var = ((h - mu) ** 2).mean(-1, keepdims=True)
            return (h - mu) * jax.lax.rsqrt(var + eps) * gamma + beta

        def _forward(x, src, dst, Wemb, Wq, bq, Wk, bk, Wv, bv, Wo, bo, ln1_g, ln1_b, W1, b1, W2, b2, ln2_g, ln2_b):
            n = x.shape[0]
            scale = np.float32(np.sqrt(HD))
            h = x @ Wemb
            for l in range(L):
                Q = (h @ Wq[l] + bq[l]).reshape(n, H, HD)
                K = (h @ Wk[l] + bk[l]).reshape(n, H, HD)
                V = (h @ Wv[l] + bv[l]).reshape(n, H, HD)
                score = jnp.einsum('ehd,ehd->eh', K[src], Q[dst]) / scale
                score = jnp.exp(jnp.clip(score, -5.0, 5.0))
                wV = jax.ops.segment_sum(V[src] * score[:, :, None], dst, num_segments=n)
                z = jax.ops.segment_sum(score, dst, num_segments=n)
                attn = (wV / (z[:, :, None] + 1e-06)).reshape(n, D)
                h = _layernorm(h + attn @ Wo[l] + bo[l], ln1_g[l], ln1_b[l])
                ffn = jax.nn.relu(h @ W1[l] + b1[l]) @ W2[l] + b2[l]
                h = _layernorm(h + ffn, ln2_g[l], ln2_b[l])
            return h
        key = jax.random.key(seed)
        ks = jax.random.split(key, 16)
        s = 1.0 / np.sqrt(D)
        g = lambda k, shape, sc: jax.random.normal(k, shape, jnp.float32) * sc
        return {'x': g(ks[0], (N, D), 1.0), 'src': jax.random.randint(ks[1], (E,), 0, N, jnp.int32), 'dst': jax.random.randint(ks[2], (E,), 0, N, jnp.int32), 'Wemb': g(ks[3], (D, D), s), 'Wq': g(ks[4], (L, D, D), s), 'bq': jnp.zeros((L, D), jnp.float32), 'Wk': g(ks[5], (L, D, D), s), 'bk': jnp.zeros((L, D), jnp.float32), 'Wv': g(ks[6], (L, D, D), s), 'bv': jnp.zeros((L, D), jnp.float32), 'Wo': g(ks[7], (L, D, D), s), 'bo': jnp.zeros((L, D), jnp.float32), 'ln1_g': jnp.ones((L, D), jnp.float32), 'ln1_b': jnp.zeros((L, D), jnp.float32), 'W1': g(ks[8], (L, D, 2 * D), s), 'b1': jnp.zeros((L, 2 * D), jnp.float32), 'W2': g(ks[9], (L, 2 * D, D), 1.0 / np.sqrt(2 * D)), 'b2': jnp.zeros((L, D), jnp.float32), 'ln2_g': jnp.ones((L, D), jnp.float32), 'ln2_b': jnp.zeros((L, D), jnp.float32)}
    _L1_gnn_all = _L1_gnn_setup()
    _L1_gnn_in = {k: v for k, v in _L1_gnn_all.items() if k in ('Wemb', 'Wq', 'bq', 'Wk', 'bk', 'Wv', 'bv', 'Wo', 'bo', 'ln1_g', 'ln1_b', 'W1', 'b1', 'W2', 'b2', 'ln2_g', 'ln2_b')}
    del _L1_gnn_all
    return {'x': x, 'src': src, 'dst': dst, 'edge_attr_16': edge_attr_16, 'L0_gnn_W': _L0_gnn_in['W'], 'L0_gnn_a': _L0_gnn_in['a'], 'L1_gnn_Wemb': _L1_gnn_in['Wemb'], 'L1_gnn_Wq': _L1_gnn_in['Wq'], 'L1_gnn_bq': _L1_gnn_in['bq'], 'L1_gnn_Wk': _L1_gnn_in['Wk'], 'L1_gnn_bk': _L1_gnn_in['bk'], 'L1_gnn_Wv': _L1_gnn_in['Wv'], 'L1_gnn_bv': _L1_gnn_in['bv'], 'L1_gnn_Wo': _L1_gnn_in['Wo'], 'L1_gnn_bo': _L1_gnn_in['bo'], 'L1_gnn_ln1_g': _L1_gnn_in['ln1_g'], 'L1_gnn_ln1_b': _L1_gnn_in['ln1_b'], 'L1_gnn_W1': _L1_gnn_in['W1'], 'L1_gnn_b1': _L1_gnn_in['b1'], 'L1_gnn_W2': _L1_gnn_in['W2'], 'L1_gnn_b2': _L1_gnn_in['b2'], 'L1_gnn_ln2_g': _L1_gnn_in['ln2_g'], 'L1_gnn_ln2_b': _L1_gnn_in['ln2_b']}

def reference(x, src, dst, edge_attr_16, L0_gnn_W, L0_gnn_a, L1_gnn_Wemb, L1_gnn_Wq, L1_gnn_bq, L1_gnn_Wk, L1_gnn_bk, L1_gnn_Wv, L1_gnn_bv, L1_gnn_Wo, L1_gnn_bo, L1_gnn_ln1_g, L1_gnn_ln1_b, L1_gnn_W1, L1_gnn_b1, L1_gnn_W2, L1_gnn_b2, L1_gnn_ln2_g, L1_gnn_ln2_b):
    import jax
    import jax.numpy as jnp

    def _L0_gnn_ref(h, edge_attr, W, a, edge_index):
        import jax, jax.numpy as jnp
        import numpy as np
        N, E = (50000, 12500)
        F_IN, D, H, FE = (128, 32, 4, 16)
        ALPHA = 0.2
        src = edge_index[0]
        dst = edge_index[1]
        Wh = (h @ W).reshape(N, H, D)
        Wh_i = Wh[src]
        Wh_j = Wh[dst]
        a_i, a_j, a_e = (a[:, :D], a[:, D:2 * D], a[:, 2 * D:])
        e = jnp.einsum('ehd,hd->eh', Wh_i, a_i) + jnp.einsum('ehd,hd->eh', Wh_j, a_j) + jnp.einsum('ef,hf->eh', edge_attr, a_e)
        e = jnp.where(e > 0, e, ALPHA * e)
        attention = jax.nn.softmax(e, axis=1)
        msg = attention[:, :, None] * Wh_j
        h_prime = jax.ops.segment_sum(msg, src, num_segments=N)
        out = h_prime.reshape(N, H * D)
        return jax.nn.elu(out)

    def _L1_gnn_ref(x, src, dst, Wemb, Wq, bq, Wk, bk, Wv, bv, Wo, bo, ln1_g, ln1_b, W1, b1, W2, b2, ln2_g, ln2_b):
        import jax, jax.numpy as jnp
        import numpy as np
        N, E, D, H, L = (50000, 12500, 128, 8, 3)
        HD = D // H

        def _layernorm(h, gamma, beta, eps=1e-05):
            mu = h.mean(-1, keepdims=True)
            var = ((h - mu) ** 2).mean(-1, keepdims=True)
            return (h - mu) * jax.lax.rsqrt(var + eps) * gamma + beta

        def _forward(x, src, dst, Wemb, Wq, bq, Wk, bk, Wv, bv, Wo, bo, ln1_g, ln1_b, W1, b1, W2, b2, ln2_g, ln2_b):
            n = x.shape[0]
            scale = np.float32(np.sqrt(HD))
            h = x @ Wemb
            for l in range(L):
                Q = (h @ Wq[l] + bq[l]).reshape(n, H, HD)
                K = (h @ Wk[l] + bk[l]).reshape(n, H, HD)
                V = (h @ Wv[l] + bv[l]).reshape(n, H, HD)
                score = jnp.einsum('ehd,ehd->eh', K[src], Q[dst]) / scale
                score = jnp.exp(jnp.clip(score, -5.0, 5.0))
                wV = jax.ops.segment_sum(V[src] * score[:, :, None], dst, num_segments=n)
                z = jax.ops.segment_sum(score, dst, num_segments=n)
                attn = (wV / (z[:, :, None] + 1e-06)).reshape(n, D)
                h = _layernorm(h + attn @ Wo[l] + bo[l], ln1_g[l], ln1_b[l])
                ffn = jax.nn.relu(h @ W1[l] + b1[l]) @ W2[l] + b2[l]
                h = _layernorm(h + ffn, ln2_g[l], ln2_b[l])
            return h
        return _forward(x, src, dst, Wemb, Wq, bq, Wk, bk, Wv, bv, Wo, bo, ln1_g, ln1_b, W1, b1, W2, b2, ln2_g, ln2_b)
    edge_index = jnp.stack([src, dst])
    h = jnp.maximum(_layernorm(x, axis=-1), 0.0)
    x = x + _L0_gnn_ref(h, edge_attr_16, L0_gnn_W, L0_gnn_a, edge_index)
    h = jnp.maximum(_layernorm(x, axis=-1), 0.0)
    x = x + _L1_gnn_ref(h, src, dst, L1_gnn_Wemb, L1_gnn_Wq, L1_gnn_bq, L1_gnn_Wk, L1_gnn_bk, L1_gnn_Wv, L1_gnn_bv, L1_gnn_Wo, L1_gnn_bo, L1_gnn_ln1_g, L1_gnn_ln1_b, L1_gnn_W1, L1_gnn_b1, L1_gnn_W2, L1_gnn_b2, L1_gnn_ln2_g, L1_gnn_ln2_b)
    return x

_drawn_inputs = setup_inputs


def setup_inputs(seed=0):
    import zlib

    import numpy as np

    out = dict(_drawn_inputs(seed))
    spreads = {'L1_gnn_bq': (0.0, 0.8),
     'L1_gnn_bk': (0.0, 0.8),
     'L1_gnn_bv': (0.0, 0.1),
     'L1_gnn_bo': (0.0, 0.1),
     'L1_gnn_ln1_g': (1.0, 0.2),
     'L1_gnn_ln1_b': (0.0, 0.1),
     'L1_gnn_b1': (0.0, 0.1),
     'L1_gnn_b2': (0.0, 0.1),
     'L1_gnn_ln2_g': (1.0, 0.2),
     'L1_gnn_ln2_b': (0.0, 0.1)}
    factors = {'edge_attr_16': 4.865}
    for name, (base, spread) in spreads.items():
        noise = np.random.default_rng([zlib.crc32(name.encode()), seed]).standard_normal(out[name].shape)
        drawn = base * np.exp(spread * noise) if base else spread * noise
        out[name] = jnp.asarray(drawn.astype(out[name].dtype))
    for name, factor in factors.items():
        out[name] = (out[name] * factor).astype(out[name].dtype)
    return out
```

```python
from contextlib import ExitStack

import numpy as np
import concourse.bass as bass
from concourse import mybir

P = 128
TE = 2
TN = 4
D = 128
H0, D0 = 4, 32
FE = 16
H1, D1 = 8, 16
MW = D + H1
LAYERS = 3
ALPHA = 0.2
LN_EPS = 1e-5
Z_EPS = 1e-6
CLIP = 5.0
SCALE = float(np.sqrt(D1))

ALU = mybir.AluOpType
ACT = mybir.ActivationFunctionType
AX = mybir.AxisListType
F32 = mybir.dt.float32
BF16 = mybir.dt.bfloat16
I32 = mybir.dt.int32
U32 = mybir.dt.uint32


class Step:

    def __init__(self, pair, slot, steps, layer):
        self.pair, self.slot, self.steps, self.layer = pair, slot, steps, layer
        self.index = pair * 2 + slot
        self.reused = not (isinstance(pair, int) and pair == 0 and layer == 0)

    def done(self, n=1):
        return (self.index + (self.layer * self.steps + 1)) * n

    def before(self, n=1):
        return (self.index + (self.layer * self.steps - 1)) * n

    def landed(self, n=16):
        return (self.pair + (self.layer * self.steps // 2 + 1)) * n

    def landed_before(self, n=16):
        return (self.pair + self.layer * self.steps // 2) * n


def run_steps(engine, steps, stages, layer=0):
    least, most = min(a for a, _ in stages), max(a for a, _ in stages)
    first, last = -most, steps - least
    start = max(2 - least, -most)
    start += start % 2
    end = (steps - most) // 2 * 2

    def plain(rounds):
        for r in rounds:
            for ahead, emit in stages:
                if 0 <= r + ahead < steps:
                    emit(Step((r + ahead) // 2, (r + ahead) % 2, steps, layer))

    if end - start < 4:
        plain(range(first, last))
        return
    plain(range(first, start))
    with engine.Fori(start // 2, end // 2) as i:
        for half in range(2):
            for ahead, emit in stages:
                emit(Step(i + (half + ahead) // 2, (half + ahead) % 2, steps, layer))
    plain(range(end, last))


class Core:

    def __init__(self, nc, ctx):
        self.nc, self.ctx, self.kept = nc, ctx, {}

    def sb(self, name, shape, dt=F32):
        if name not in self.kept:
            self.kept[name] = self.ctx.enter_context(self.nc.sbuf_tensor(name, shape, dt))
        return self.kept[name]

    def sem(self, name):
        if name not in self.kept:
            self.kept[name] = self.ctx.enter_context(self.nc.semaphore(name))
        return self.kept[name]

    def count(self, engine, n, value):
        if isinstance(value, int):
            return value
        key = f"count_{engine.engine.name}_{n}"
        if key not in self.kept:
            self.kept[key] = engine.alloc_register(key)
        engine.reg_mov(self.kept[key], value)
        return self.kept[key]

    def sems(self, name):
        return [self.sem(f"{name}_{k}") for k in range(2)]


def held(core, engine, *counts):
    kept = [core.count(engine, n, v) for n, v in enumerate(counts)]
    engine.wait_ge(core.sem("consts_made"), 5)
    return kept


def over_tiles(row, tiles):
    return row.unsqueeze(1).to_broadcast([P, tiles, row.shape[-1]])


def over_lanes(heads, width):
    return heads.unsqueeze(2).to_broadcast([P, heads.shape[-1], width])


def setup_phase(core, w, tables):
    nc = core.nc
    psum = core.psum
    loaded, zeroed = core.sem("weights_loaded"), core.sem("tables_zeroed")
    pool_made, dve_made, pe_made = core.sem("consts_made"), core.sem("prep_dve"), core.sem("prep_pe")
    ident, later, trash_i = core.sb("ident", [P, P]), core.sb("later", [P, P]), core.sb("trash_i", [P, 1], I32)
    trash, eps, ones3 = core.sb("trash", [P, 1]), core.sb("ln_eps", [P, 1]), core.sb("ones3", [3, P], BF16)
    w0, wi = core.sb("w0_ext", [P, D + H0]), core.sb("w0_src", [P, H0])
    a_rows = core.sb("a_rows", [P, H0, 2 * D0 + FE])
    ae = core.sb("a_edge", [FE, H0])
    aw = core.sb("a_times_w", [P, D])
    wemb = core.sb("wemb", [P, D])
    wkvq = core.sb("wkvq", [P, LAYERS, 3 * D])
    wo = core.sb("wo", [P, LAYERS, D])
    w1 = core.sb("w1", [P, LAYERS, 2 * D])
    w2 = core.sb("w2", [P, LAYERS, 2, D])
    g1col, b1lncol = core.sb("ln1_g_col", [P, LAYERS]), core.sb("ln1_b_col", [P, LAYERS])
    b1col = core.sb("b1_col", [P, LAYERS, 2])
    diag = core.sb("ln1_g_diag", [P, LAYERS, P])
    g2rows, b2rows = core.sb("ln2_g_rows", [P, LAYERS, D]), core.sb("ln2_b_rows", [P, LAYERS, D])
    nb = 5 * D
    bias3 = core.sb("bias3", [3, LAYERS, nb])
    lnb3 = core.sb("lnb3", [3, LAYERS, D])
    part = core.sb("bias_part", [3, 3, LAYERS * nb], BF16)
    rest = core.sb("bias_rest", [3, LAYERS * nb])
    picked = core.sb("bias_picked", [3, LAYERS * nb])
    bias_b = core.sb("bias_b", [3, LAYERS * nb], BF16)
    zeros = core.sb("zeros", [P, tables[1].shape[0] * MW // P // 8])

    loads = [(w0[:, 0:D], w["L0_gnn_W"]), (wemb[:], w["L1_gnn_Wemb"]),
             (a_rows[:].rearrange("p h a -> p (h a)"), w["L0_gnn_a"].rearrange("h a -> (h a)").partition_broadcast(P)),
             (ae[:], w["a_T"][2 * D0:, :]),
             (wkvq[:, :, 0:D], w["L1_gnn_Wk"].rearrange("l p n -> p l n")),
             (wkvq[:, :, D:2 * D], w["L1_gnn_Wv"].rearrange("l p n -> p l n")),
             (wkvq[:, :, 2 * D:], w["L1_gnn_Wq"].rearrange("l p n -> p l n")),
             (wo[:], w["L1_gnn_Wo"].rearrange("l p n -> p l n")),
             (w1[:], w["L1_gnn_W1"].rearrange("l p n -> p l n")),
             (g1col[:], w["ln1_g_T"]), (b1lncol[:], w["ln1_b_T"]), (b1col[:].rearrange("p l c -> p (l c)"), w["b1_T"]),
             (g2rows[:].rearrange("p l n -> p (l n)"), w["L1_gnn_ln2_g"].rearrange("l n -> (l n)").partition_broadcast(P)),
             (b2rows[:].rearrange("p l n -> p (l n)"), w["L1_gnn_ln2_b"].rearrange("l n -> (l n)").partition_broadcast(P)),
             (lnb3[:].rearrange("p l n -> p (l n)"), w["L1_gnn_ln1_b"].rearrange("l n -> (l n)").partition_broadcast(3))]
    loads += [(w2[:, l], w["L1_gnn_W2"][l].rearrange("(c p) n -> p c n", p=P)) for l in range(LAYERS)]
    loads += [(bias3[:, :, c * D:(c + 1) * D], w[f"L1_gnn_{b}"].partition_broadcast(3))
              for c, b in enumerate(("bk", "bv", "bq", "bo", "b2"))]

    with nc.Block() as block:
        @block.sync
        def _(sp):
            for dst, src in loads:
                sp.dma_start(dst, src).then_inc(loaded, 16)

        @block.scalar
        def _(act):
            act.wait_ge(dve_made, 1)
            n = 0
            for table in tables:
                size = table.shape[0] * table.shape[1] // P // 8
                view = table.rearrange("r d -> (r d)").rearrange("(c p n) -> c p n", p=P, n=size)
                for c in range(8):
                    act.dma_start(view[c], zeros[:, 0:size]).then_inc(zeroed, 16)
                    n += 16
            act.wait_ge(zeroed, n)

        @block.gpsimd
        def _(pool):
            nc.gpsimd.memset(ident[:], 0.0).then_inc(pool_made, 1)
            nc.gpsimd.memset(later[:], 1.0).then_inc(pool_made, 1)
            pool.wait_ge(pool_made, 2)
            nc.gpsimd.affine_select(out=ident[:], in_=ident[:], compare_op=ALU.not_equal, fill=1.0, base=0,
                                    pattern=[[-1, P]], channel_multiplier=1).then_inc(pool_made, 1)
            nc.gpsimd.affine_select(out=later[:], in_=later[:], compare_op=ALU.is_gt, fill=0.0, base=0,
                                    pattern=[[1, P]], channel_multiplier=-1).then_inc(pool_made, 1)
            nc.gpsimd.iota(trash_i[:], [[0, 1]], base=tables[0].shape[0] - P, channel_multiplier=1).then_inc(pool_made, 1)

        @block.vector
        def _(dve):
            made = [0]

            def then(instruction):
                instruction.then_inc(dve_made, 1)
                made[0] += 1
                dve.wait_ge(dve_made, made[0])

            then(nc.vector.memset(zeros[:], 0.0))
            then(nc.vector.memset(eps[:], LN_EPS))
            then(nc.vector.memset(ones3[:], 1.0))
            dve.wait_ge(pool_made, 5)
            then(nc.vector.tensor_copy(trash[:], trash_i[:]))
            dve.wait_ge(loaded, 16 * len(loads))
            w_heads = w0[:, 0:D].rearrange("p (h d) -> p h d", h=H0)
            for out, lo in ((wi[:], 0), (w0[:, D:D + H0], D0)):
                then(nc.vector.tensor_tensor(aw[:].rearrange("p (h d) -> p h d", h=H0), w_heads,
                                             a_rows[:, :, lo:lo + D0], ALU.mult))
                then(nc.vector.tensor_reduce(out, aw[:].rearrange("p (h d) -> p h d", h=H0), AX.X, ALU.add))
            then(nc.vector.tensor_tensor(bias3[:, :, 4 * D:], bias3[:, :, 4 * D:], lnb3[:], ALU.add))
            flat = bias3[:].rearrange("p l n -> p (l n)")
            then(nc.vector.tensor_copy(rest[:], flat))
            for c in range(3):
                then(nc.vector.tensor_copy(part[:, c], rest[:]))
                then(nc.vector.tensor_tensor(rest[:], rest[:], part[:, c], ALU.subtract))
            then(nc.vector.tensor_scalar(picked[:], part[:, 0], ident[0:3, 0:1], None, ALU.mult))
            for c in range(1, 3):
                then(nc.vector.scalar_tensor_tensor(out=picked[:], in0=part[:, c], scalar=ident[0:3, c:c + 1],
                                                    in1=picked[:], op0=ALU.mult, op1=ALU.add))
            then(nc.vector.tensor_copy(bias_b[:], picked[:]))
            dve.wait_ge(pe_made, 1)
            for l in range(LAYERS):
                then(nc.vector.tensor_tensor(b1col[:, l], b1col[:, l], psum[:, 0, 2 * l:2 * l + 2], ALU.add))
                then(nc.vector.tensor_scalar(w1[:, l], w1[:, l], g1col[:, l:l + 1], None, ALU.mult))
                then(nc.vector.tensor_scalar(diag[:, l], ident[:], g1col[:, l:l + 1], None, ALU.mult))

        @block.tensor
        def _(pe):
            pe.wait_ge(loaded, 16 * len(loads))
            for l in range(LAYERS):
                for c in range(2):
                    mm = nc.tensor.matmul(psum[:, 0, 2 * l + c:2 * l + c + 1], w1[:, l, c * D:(c + 1) * D],
                                          b1lncol[:, l:l + 1], start=True, stop=True)
            mm.then_inc(pe_made, 1)


def pick_targets(core, nc, dve, st, prefix, ids, rows, match, others, target):
    later, trash = core.sb("later", [P, P]), core.sb("trash", [P, 1])
    scratch, lone, moved = (core.sb(f"{prefix}_scratch", [P, TE, P]), core.sb(f"{prefix}_lone", [P, TE]),
                            core.sb(f"{prefix}_moved", [P, TE]))
    matched, counted = core.sem(f"{prefix}_matched"), core.sem(f"{prefix}_counted")
    chained, picked = core.sem(f"{prefix}_chained"), core.sem(f"{prefix}_picked")
    k = st.slot
    for t in range(TE):
        nc.vector.tensor_scalar(match[:, k, t], rows[:, k, t * P:(t + 1) * P], ids[:, k, t:t + 1], None,
                                ALU.is_equal).then_inc(matched, 1)
    dve.wait_ge(matched, st.done(TE))
    for t in range(TE):
        nc.vector.tensor_tensor_reduce(out=scratch[:, t], in0=match[:, k, t], in1=later[:], scale=1.0, scalar=0.0,
                                       op0=ALU.mult, op1=ALU.add, accum_out=others[:, t:t + 1]).then_inc(counted, 1)
    dve.wait_ge(counted, st.done(TE))
    nc.vector.tensor_scalar(lone[:], others[:], 0.0, None, ALU.is_equal).then_inc(chained, 1)
    nc.vector.tensor_scalar(moved[:], ids[:, k, 0:TE], trash[:, 0:1], None, ALU.subtract).then_inc(chained, 1)
    dve.wait_ge(chained, st.done(3) - 1)
    nc.vector.tensor_tensor(moved[:], moved[:], lone[:], ALU.mult).then_inc(chained, 1)
    dve.wait_ge(chained, st.done(3))
    nc.vector.tensor_scalar(target[:, k], moved[:], trash[:, 0:1], None, ALU.add).then_inc(picked, 1)


def gather_and_add(core, nc, pool, steps, layer, prefix, source, table, ends, rows_in, sums, target):
    ends_landed, gathered = core.sems(f"{prefix}_ends_landed"), core.sems(f"{prefix}_gathered")
    added = core.sems("sums_added" if layer is None else f"{prefix}_added")
    rows_used = core.sem(f"{prefix}_rows_used")
    summed, picked = core.sem(f"{prefix}_summed"), core.sem(f"{prefix}_picked")

    def gather(st, t):
        k = st.slot
        if t == 0:
            landed, used = held(core, pool, st.landed(), st.before() if st.reused else 0)
            pool.wait_ge(ends_landed[k], landed)
            pool.wait_ge(rows_used, used)
        for c in (t, TE + t):
            nc.gpsimd.indirect_dma_start(
                rows_in[:, k, c], None, source, bass.IndirectOffsetOnAxis(ap=ends[:, k, c:c + 1].bitcast(U32), axis=0)
            ).then_inc(gathered[k], 16)

    def add(st, t):
        k = st.slot
        if t == 0:
            done, previous = held(core, pool, st.done(), st.landed(16 * TE) if k == 1 else st.landed_before(16 * TE))
            pool.wait_ge(summed, done)
            pool.wait_ge(picked, done)
            pool.wait_ge(added[1 - k], previous)
        else:
            previous, = held(core, pool, st.landed_before(16 * TE) + 16 * t)
            pool.wait_ge(added[k], previous)
        nc.gpsimd.indirect_dma_start(
            table, bass.IndirectOffsetOnAxis(ap=target[:, k, t:t + 1].bitcast(U32), axis=0), sums[:, k, t], None,
            compute_op=ALU.add).then_inc(added[k], 16)

    stages = []
    for t in range(TE):
        stages += [(0, lambda st, t=t: gather(st, t)), (-2, lambda st, t=t: add(st, t))]
    run_steps(pool, steps, stages, layer)
    end = Step(steps // 2 - 1, 1, steps, layer)
    for k in range(2):
        pool.wait_ge(added[k], end.landed(16 * TE))


def l0_edge_phase(core, w, steps, x, table):
    nc, psum = core.nc, core.psum
    ident, eps = core.sb("ident", [P, P]), core.sb("ln_eps", [P, 1])
    w0, wi, ae = core.sb("w0_ext", [P, D + H0]), core.sb("w0_src", [P, H0]), core.sb("a_edge", [FE, H0])
    ends, ids = core.sb("ends", [P, 2, 2 * TE], I32), core.sb("ids", [P, 2, TE])
    equal_rows = core.sb("equal_rows", [P, 2, TE * P], I32)
    attr = core.sb("attr", [FE, 2, TE * P])
    x_in = core.sb("rows_in", [P, 2, 2 * TE, D])
    n_in, x_t = core.sb("normed", [P, 2, 2 * TE, D]), core.sb("rows_t", [P, 2, 2 * TE * P])
    stats, mv = core.sb("e_stats", [P, 2 * TE, 6]), core.sb("e_mv", [P, 2, 2 * TE, 2])
    sd, rs = core.sb("e_sd", [P, 2 * TE]), core.sb("e_rs", [P, 2 * TE])
    match, others = core.sb("match", [P, 2, TE, P]), core.sb("others", [P, TE])
    target = core.sb("target", [P, 2, TE], I32)
    logit, leaky = core.sb("logit", [P, 2, TE, H0]), core.sb("leaky", [P, TE, H0])
    top, centred = core.sb("top", [P, TE]), core.sb("centred", [P, 2, TE, H0])
    grown, total = core.sb("grown", [P, 2, TE, H0]), core.sb("total", [P, TE])
    share = core.sb("share", [P, TE, H0])
    msg, sums = core.sb("msg0", [P, 2, TE, D]), core.sb("sums0", [P, 2, TE, D])

    ps_t = lambda k: psum[:, k]
    ps_w = lambda k: psum[:, 2 + k].rearrange("p (t n) -> p t n", t=TE)
    ps_m = lambda k: psum[:, 4 + k, 0:TE * D].rearrange("p (t n) -> p t n", t=TE)

    ends_landed, rows_landed = core.sems("e0_ends_landed"), core.sems("e0_rows_landed")
    attr_landed, gathered, added = core.sems("e0_attr_landed"), core.sems("e0_gathered"), core.sems("e0_added")
    (cast, rows_used, stated, aggregated, rooted, inverted, normed, turned, relued, projected, logits_out, matched,
     picked, chain, centre_done, exped, weighed, merged, summed) = (
        core.sem("e0_" + n) for n in
        ("cast", "rows_used", "stated", "aggregated", "rooted", "inverted", "normed", "turned", "relued",
         "projected", "logits_out", "matched", "picked", "softmaxed", "centred", "exped", "weighed", "merged",
         "summed"))

    with nc.Block() as block:
        @block.sync
        def _(sp):
            def load(st):
                k = st.slot
                if st.reused:
                    used, previous = held(core, sp, st.landed_before(16 * 2 * TE), st.before())
                    sp.wait_ge(gathered[k], used)
                    sp.wait_ge(cast, previous)
                sp.dma_start(ends[:, k], w["ends"][st.index]).then_inc(ends_landed[k], 16)
                if st.reused:
                    before, = held(core, sp, st.before(TE))
                    sp.wait_ge(matched, before)
                sp.dma_start(equal_rows[:, k], w["src_rows"][st.index].partition_broadcast(P)).then_inc(rows_landed[k], 16)
                if st.reused:
                    before, = held(core, sp, st.before())
                    sp.wait_ge(projected, before)
                sp.dma_start(attr[:, k], w["attr_T"][:, bass.ds(st.index * (TE * P), TE * P)]).then_inc(attr_landed[k], 16)

            run_steps(sp, steps, [(0, load)])

        @block.gpsimd
        def _(pool):
            gather_and_add(core, nc, pool, steps, 0, "e0", x, table, ends, x_in, sums, target)

        @block.vector
        def _(dve):
            def normalise(st):
                k = st.slot
                dve.wait_ge(ends_landed[k], st.landed())
                if st.reused:
                    dve.wait_ge(picked, st.before())
                nc.vector.tensor_copy(ids[:, k], ends[:, k, 0:TE]).then_inc(cast, 1)
                dve.wait_ge(gathered[k], st.landed(16 * 2 * TE))
                for c in range(2 * TE):
                    nc.vector.bn_stats(stats[:, c], x_in[:, k, c]).then_inc(stated, 1)
                all_stated, = held(core, dve, st.done(2 * TE))
                dve.wait_ge(stated, all_stated)
                for c in range(2 * TE):
                    nc.vector.bn_aggr(mv[:, k, c], stats[:, c]).then_inc(aggregated, 1)
                dve.wait_ge(aggregated, st.done(2 * TE))
                dve.wait_ge(rooted, st.done())
                nc.vector.reciprocal(rs[:], sd[:]).then_inc(inverted, 1)
                dve.wait_ge(inverted, st.done())
                if st.reused:
                    dve.wait_ge(turned, st.before())
                for c in range(2 * TE):
                    ins = nc.vector.tensor_scalar(n_in[:, k, c], x_in[:, k, c], mv[:, k, c, 0:1], rs[:, c:c + 1],
                                                  ALU.subtract, ALU.mult).then_inc(normed, 1)
                dve.wait_ge(normed, st.done(2 * TE))
                nc.vector.tensor_copy(others[:, 0:1], rs[:, 0:1]).then_inc(rows_used, 1)
                dve.wait_ge(rows_used, st.done())

            def softmax(st):
                k = st.slot
                dve.wait_ge(cast, st.done())
                dve.wait_ge(rows_landed[k], st.landed())
                if st.reused:
                    dve.wait_ge(merged, st.before())
                    dve.wait_ge(added[k], st.landed_before(16 * TE))
                pick_targets(core, nc, dve, st, "e0", ids, equal_rows, match, others, target)
                dve.wait_ge(logits_out, st.done())
                nc.vector.scalar_tensor_tensor(out=leaky[:], in0=logit[:, k], scalar=ALPHA, in1=logit[:, k],
                                               op0=ALU.mult, op1=ALU.max).then_inc(chain, 1)
                dve.wait_ge(chain, st.done(5) - 4)
                nc.vector.tensor_reduce(top[:], leaky[:], AX.X, ALU.max).then_inc(chain, 1)
                dve.wait_ge(chain, st.done(5) - 3)
                nc.vector.tensor_tensor(centred[:, k], leaky[:], over_lanes(top[:], H0), ALU.subtract).then_inc(centre_done, 1)
                dve.wait_ge(exped, st.done())
                nc.vector.tensor_reduce(total[:], grown[:, k], AX.X, ALU.add).then_inc(chain, 1)
                dve.wait_ge(chain, st.done(5) - 2)
                nc.vector.reciprocal(total[:], total[:]).then_inc(chain, 1)
                dve.wait_ge(chain, st.done(5) - 1)
                nc.vector.tensor_tensor(share[:], grown[:, k], over_lanes(total[:], H0), ALU.mult).then_inc(chain, 1)
                dve.wait_ge(chain, st.done(5))
                for t in range(TE):
                    nc.vector.tensor_tensor(msg[:, k, t].rearrange("p (h d) -> p h d", h=H0),
                                            ps_w(k)[:, t, 0:D].rearrange("p (h d) -> p h d", h=H0),
                                            over_lanes(share[:, t], D0), ALU.mult).then_inc(weighed, 1)
                dve.wait_ge(weighed, st.done(TE))

            run_steps(dve, steps, [(0, normalise), (-1, softmax)])

        @block.scalar
        def _(act):
            def root(st):
                act.wait_ge(aggregated, st.done(2 * TE))
                if st.reused:
                    act.wait_ge(inverted, st.done() - 1)
                nc.scalar.activation(sd[:], mv[:, st.slot, :, 1], ACT.Sqrt, bias=eps[:, 0:1]).then_inc(rooted, 1)

            def relu_turned(st):
                act.wait_ge(turned, st.done())
                if st.reused:
                    act.wait_ge(projected, st.before())
                nc.scalar.activation(x_t[:, st.slot], ps_t(st.slot), ACT.Relu).then_inc(relued, 1)

            def logits(st):
                act.wait_ge(projected, st.done())
                nc.scalar.copy(logit[:, st.slot], ps_w(st.slot)[:, :, D:D + H0]).then_inc(logits_out, 1)

            def exp(st):
                act.wait_ge(centre_done, st.done())
                nc.scalar.activation(grown[:, st.slot], centred[:, st.slot], ACT.Exp).then_inc(exped, 1)

            def sums_out(st):
                act.wait_ge(merged, st.done())
                if st.reused:
                    act.wait_ge(added[st.slot], st.landed_before(16 * TE))
                nc.scalar.copy(sums[:, st.slot], ps_m(st.slot)).then_inc(summed, 1)

            run_steps(act, steps, [(0, root), (0, relu_turned), (0, logits), (-1, exp), (-1, sums_out)])

        @block.tensor
        def _(pe):
            def turn(st):
                k = st.slot
                pe.wait_ge(normed, st.done(2 * TE))
                if st.reused:
                    pe.wait_ge(relued, st.before())
                for c in range(2 * TE):
                    mm = nc.tensor.transpose(ps_t(k)[:, c * P:(c + 1) * P], n_in[:, k, c], ident[:])
                mm.then_inc(turned, 1)

            def project(st):
                k = st.slot
                pe.wait_ge(relued, st.done())
                pe.wait_ge(attr_landed[k], st.landed())
                if st.reused:
                    pe.wait_ge(weighed, st.before(TE))
                    pe.wait_ge(logits_out, st.before())
                for t in range(TE):
                    nc.tensor.matmul(ps_w(k)[:, t, 0:D + H0], x_t[:, k, (TE + t) * P:(TE + t + 1) * P], w0[:],
                                     start=True, stop=False)
                    nc.tensor.matmul(ps_w(k)[:, t, D:D + H0], x_t[:, k, t * P:(t + 1) * P], wi[:],
                                     start=False, stop=False)
                    mm = nc.tensor.matmul(ps_w(k)[:, t, D:D + H0], attr[:, k, t * P:(t + 1) * P], ae[:],
                                          start=False, stop=True)
                mm.then_inc(projected, 1)

            def merge(st):
                k = st.slot
                pe.wait_ge(weighed, st.done(TE))
                pe.wait_ge(matched, st.done(TE))
                if st.reused:
                    pe.wait_ge(summed, st.before())
                for t in range(TE):
                    mm = nc.tensor.matmul(ps_m(k)[:, t], match[:, k, t], msg[:, k, t], start=True, stop=True)
                mm.then_inc(merged, 1)

            run_steps(pe, steps, [(0, turn), (0, project), (-1, merge)])


def l0_node_phase(core, w, steps, x, table, x1_table, h_table):
    nc, psum = core.nc, core.psum
    ident, eps, wemb = core.sb("ident", [P, P]), core.sb("ln_eps", [P, 1]), core.sb("wemb", [P, D])
    node = lambda name: core.sb(name, [P, 2, TN, D])
    o_in, x_in, low, e_low, high = node("n_a"), node("n_b"), node("n_c"), node("n_d"), node("n_e")
    x1, n1, n1t, h_out = node("n_f"), node("n_g"), node("n_h"), node("n_i")
    stats, mv = core.sb("n_stats", [P, TN, 6]), core.sb("n_mv", [P, 2, TN, 2])
    sd, rs = core.sb("n_sd", [P, TN]), core.sb("n_rs", [P, TN])
    ps_t = lambda k: psum[:, k].rearrange("p (t n) -> p t n", t=TN)
    ps_h = lambda k: psum[:, 2 + k].rearrange("p (t n) -> p t n", t=TN)
    per_step = lambda t: t[0:steps * TN * P, :].rearrange("(s p j) d -> s p j d", p=P, j=TN)

    o_landed, x_landed = core.sems("n0_o_landed"), core.sems("n0_x_landed")
    x1_stored, h_stored = core.sems("n0_x1_stored"), core.sems("n0_h_stored")
    lowed, highed, exped, x1_made, stated, aggregated, rooted, inverted, normed, turned, relued, embedded, h_made = (
        core.sem("n0_" + n) for n in ("lowed", "highed", "exped", "x1_made", "stated", "aggregated", "rooted",
                                      "inverted", "normed", "turned", "relued", "embedded", "h_made"))

    with nc.Block() as block:
        @block.sync
        def _(sp):
            def load(st):
                k = st.slot
                if st.reused:
                    before, = held(core, sp, st.before())
                    sp.wait_ge(highed, before)
                    sp.wait_ge(lowed, before)
                sp.dma_start(o_in[:, k], per_step(table)[st.index]).then_inc(o_landed[k], 16)
                sp.dma_start(x_in[:, k], per_step(x)[st.index]).then_inc(x_landed[k], 16)

            def store(st):
                k = st.slot
                ready, = held(core, sp, st.done())
                sp.wait_ge(x1_made, ready)
                sp.dma_start(per_step(x1_table)[st.index], x1[:, k]).then_inc(x1_stored[k], 16)
                ready, = held(core, sp, st.done())
                sp.wait_ge(h_made, ready)
                sp.dma_start(per_step(h_table)[st.index], h_out[:, k]).then_inc(h_stored[k], 16)

            run_steps(sp, steps, [(1, load), (-1, store)])
            end = Step(steps // 2 - 1, 1, steps, 0)
            for k in range(2):
                sp.wait_ge(x1_stored[k], end.landed())
                sp.wait_ge(h_stored[k], end.landed())

        @block.vector
        def _(dve):
            def split(st):
                k = st.slot
                dve.wait_ge(o_landed[k], st.landed())
                if st.reused:
                    dve.wait_ge(exped, st.before())
                nc.vector.tensor_scalar(low[:, k], o_in[:, k], 0.0, None, ALU.min).then_inc(lowed, 1)
                dve.wait_ge(x_landed[k], st.landed())
                if st.reused:
                    dve.wait_ge(x1_made, st.before())
                nc.vector.scalar_tensor_tensor(out=high[:, k], in0=o_in[:, k], scalar=0.0, in1=x_in[:, k],
                                               op0=ALU.max, op1=ALU.add).then_inc(highed, 1)

            def normalise(st):
                k = st.slot
                dve.wait_ge(exped, st.done())
                dve.wait_ge(highed, st.done())
                if st.reused:
                    dve.wait_ge(x1_stored[k], st.landed_before())
                nc.vector.scalar_tensor_tensor(out=x1[:, k], in0=e_low[:, k], scalar=-1.0, in1=high[:, k],
                                               op0=ALU.add, op1=ALU.add).then_inc(x1_made, 1)
                dve.wait_ge(x1_made, st.done())
                for j in range(TN):
                    nc.vector.bn_stats(stats[:, j], x1[:, k, j]).then_inc(stated, 1)
                all_stated, = held(core, dve, st.done(TN))
                dve.wait_ge(stated, all_stated)
                for j in range(TN):
                    nc.vector.bn_aggr(mv[:, k, j], stats[:, j]).then_inc(aggregated, 1)
                dve.wait_ge(aggregated, st.done(TN))
                dve.wait_ge(rooted, st.done())
                nc.vector.reciprocal(rs[:], sd[:]).then_inc(inverted, 1)
                dve.wait_ge(inverted, st.done())
                if st.reused:
                    dve.wait_ge(turned, st.before())
                for j in range(TN):
                    nc.vector.tensor_scalar(n1[:, k, j], x1[:, k, j], mv[:, k, j, 0:1], rs[:, j:j + 1],
                                            ALU.subtract, ALU.mult).then_inc(normed, 1)
                dve.wait_ge(normed, st.done(TN))

            run_steps(dve, steps, [(1, split), (0, normalise)])

        @block.scalar
        def _(act):
            def exp(st):
                act.wait_ge(lowed, st.done())
                if st.reused:
                    act.wait_ge(x1_made, st.before())
                nc.scalar.activation(e_low[:, st.slot], low[:, st.slot], ACT.Exp).then_inc(exped, 1)

            def root(st):
                act.wait_ge(aggregated, st.done(TN))
                if st.reused:
                    act.wait_ge(inverted, st.done() - 1)
                nc.scalar.activation(sd[:], mv[:, st.slot, :, 1], ACT.Sqrt, bias=eps[:, 0:1]).then_inc(rooted, 1)

            def relu_turned(st):
                act.wait_ge(turned, st.done())
                if st.reused:
                    act.wait_ge(embedded, st.before())
                nc.scalar.activation(n1t[:, st.slot], ps_t(st.slot), ACT.Relu).then_inc(relued, 1)

            def h_ready(st):
                act.wait_ge(embedded, st.done())
                if st.reused:
                    act.wait_ge(h_stored[st.slot], st.landed_before())
                nc.scalar.copy(h_out[:, st.slot], ps_h(st.slot)).then_inc(h_made, 1)

            run_steps(act, steps, [(1, exp), (0, root), (0, relu_turned), (0, h_ready)])

        @block.tensor
        def _(pe):
            def turn(st):
                k = st.slot
                pe.wait_ge(normed, st.done(TN))
                if st.reused:
                    pe.wait_ge(relued, st.before())
                for j in range(TN):
                    mm = nc.tensor.transpose(ps_t(k)[:, j], n1[:, k, j], ident[:])
                mm.then_inc(turned, 1)

            def embed(st):
                k = st.slot
                pe.wait_ge(relued, st.done())
                if st.reused:
                    pe.wait_ge(h_made, st.before())
                for j in range(TN):
                    mm = nc.tensor.matmul(ps_h(k)[:, j], n1t[:, k, j], wemb[:], start=True, stop=True)
                mm.then_inc(embedded, 1)

            run_steps(pe, steps, [(0, turn), (0, embed)])


def l1_edge_phase(core, w, steps, layer, h_table, table):
    nc, psum = core.nc, core.psum
    ident, ones3 = core.sb("ident", [P, P]), core.sb("ones3", [3, P], BF16)
    wkvq = core.sb("wkvq", [P, LAYERS, 3 * D])[:, layer]
    bias = core.sb("bias_b", [3, LAYERS * 5 * D], BF16)[:].rearrange("p (l n) -> p l n", l=LAYERS)[:, layer]
    ends, ids = core.sb("ends", [P, 2, 2 * TE], I32), core.sb("ids", [P, 2, TE])
    equal_rows = core.sb("equal_rows", [P, 2, TE * P], I32)
    h_in, h_t = core.sb("rows_in", [P, 2, 2 * TE, D]), core.sb("rows_t", [P, 2, 2 * TE * P])
    match, others = core.sb("match", [P, 2, TE, P]), core.sb("others", [P, TE])
    target = core.sb("target", [P, 2, TE], I32)
    q, prod = core.sb("q", [P, 2, TE, D]), core.sb("prod", [P, TE, D])
    score, clipped = core.sb("score", [P, TE, H1]), core.sb("clipped", [P, 2, TE, H1])
    msg, sums = core.sb("msg1", [P, 2, TE, MW]), core.sb("sums1", [P, 2, TE, MW])

    ps_t = lambda k: psum[:, k]
    ps_kv = lambda k: psum[:, 2 + k].rearrange("p (t n) -> p t n", t=TE)
    ps_q = lambda k: psum[:, 4 + k, 0:TE * D].rearrange("p (t n) -> p t n", t=TE)
    ps_m = lambda k: psum[:, 6 + k, 0:TE * MW].rearrange("p (t n) -> p t n", t=TE)

    ends_landed, rows_landed = core.sems("e1_ends_landed"), core.sems("e1_rows_landed")
    gathered, added = core.sems("e1_gathered"), core.sems("e1_added")
    (cast, rows_used, turned_out, projected, q_out, matched, picked, multiplied, scored, clip_done, exped, weighed,
     merged, summed) = (core.sem("e1_" + n) for n in
                        ("cast", "rows_used", "turned_out", "projected", "q_out", "matched", "picked",
                         "multiplied", "scored", "clipped", "exped", "weighed", "merged", "summed"))

    with nc.Block() as block:
        @block.sync
        def _(sp):
            def load(st):
                k = st.slot
                if st.reused:
                    used, previous = held(core, sp, st.landed_before(16 * 2 * TE), st.before())
                    sp.wait_ge(gathered[k], used)
                    sp.wait_ge(cast, previous)
                sp.dma_start(ends[:, k], w["ends"][st.index]).then_inc(ends_landed[k], 16)
                if st.reused:
                    before, = held(core, sp, st.before(TE))
                    sp.wait_ge(matched, before)
                sp.dma_start(equal_rows[:, k], w["dst_rows"][st.index].partition_broadcast(P)).then_inc(rows_landed[k], 16)

            run_steps(sp, steps, [(0, load)], layer)

        @block.gpsimd
        def _(pool):
            gather_and_add(core, nc, pool, steps, layer, "e1", h_table, table, ends, h_in, sums, target)

        @block.vector
        def _(dve):
            def message(st):
                k = st.slot
                dve.wait_ge(ends_landed[k], st.landed())
                if st.reused:
                    dve.wait_ge(picked, st.before())
                nc.vector.tensor_copy(ids[:, k], ends[:, k, TE:]).then_inc(cast, 1)
                dve.wait_ge(q_out, st.done())
                nc.vector.tensor_tensor(prod[:], ps_kv(k)[:, :, 0:D], q[:, k], ALU.mult).then_inc(multiplied, 1)
                dve.wait_ge(multiplied, st.done())
                nc.vector.tensor_reduce(score[:], prod[:].rearrange("p t (h d) -> p t h d", h=H1), AX.X,
                                        ALU.add).then_inc(scored, 1)
                dve.wait_ge(scored, st.done())
                nc.vector.tensor_scalar(clipped[:, k], score[:], CLIP * SCALE, -CLIP * SCALE, ALU.min,
                                        ALU.max).then_inc(clip_done, 1)
                dve.wait_ge(cast, st.done())
                dve.wait_ge(rows_landed[k], st.landed())
                if st.reused:
                    dve.wait_ge(merged, st.before())
                    dve.wait_ge(added[k], st.landed_before(16 * TE))
                pick_targets(core, nc, dve, st, "e1", ids, equal_rows, match, others, target)
                dve.wait_ge(exped, st.done())
                for t in range(TE):
                    nc.vector.tensor_tensor(msg[:, k, t, 0:D].rearrange("p (h d) -> p h d", h=H1),
                                            ps_kv(k)[:, t, D:].rearrange("p (h d) -> p h d", h=H1),
                                            over_lanes(msg[:, k, t, D:], D1), ALU.mult).then_inc(weighed, 1)

            run_steps(dve, steps, [(0, message)], layer)

        @block.scalar
        def _(act):
            def turned_to_sbuf(st):
                act.wait_ge(rows_used, st.done())
                if st.reused:
                    act.wait_ge(projected, st.before())
                nc.scalar.copy(h_t[:, st.slot], ps_t(st.slot)).then_inc(turned_out, 1)

            def q_to_sbuf(st):
                act.wait_ge(projected, st.done())
                if st.reused:
                    act.wait_ge(multiplied, st.before())
                nc.scalar.copy(q[:, st.slot], ps_q(st.slot)).then_inc(q_out, 1)

            def exp(st):
                act.wait_ge(clip_done, st.done())
                if st.reused:
                    act.wait_ge(merged, st.before())
                nc.scalar.activation(msg[:, st.slot, :, D:], clipped[:, st.slot], ACT.Exp,
                                     scale=1.0 / SCALE).then_inc(exped, 1)

            def sums_out(st):
                act.wait_ge(merged, st.done())
                if st.reused:
                    act.wait_ge(added[st.slot], st.landed_before(16 * TE))
                nc.scalar.copy(sums[:, st.slot], ps_m(st.slot)).then_inc(summed, 1)

            run_steps(act, steps, [(0, turned_to_sbuf), (-1, sums_out), (0, q_to_sbuf), (0, exp)], layer)

        @block.tensor
        def _(pe):
            def turn(st):
                k = st.slot
                pe.wait_ge(gathered[k], st.landed(16 * 2 * TE))
                if st.reused:
                    pe.wait_ge(turned_out, st.before())
                for c in range(2 * TE):
                    mm = nc.tensor.transpose(ps_t(k)[:, c * P:(c + 1) * P], h_in[:, k, c], ident[:])
                mm.then_inc(rows_used, 1)

            def merge(st):
                k = st.slot
                pe.wait_ge(weighed, st.done(TE))
                pe.wait_ge(matched, st.done(TE))
                pe.wait_ge(exped, st.done())
                if st.reused:
                    pe.wait_ge(summed, st.before())
                for t in range(TE):
                    mm = nc.tensor.matmul(ps_m(k)[:, t], match[:, k, t], msg[:, k, t], start=True, stop=True)
                mm.then_inc(merged, 1)

            def project(st):
                k = st.slot
                pe.wait_ge(turned_out, st.done())
                if st.reused:
                    pe.wait_ge(weighed, st.before(TE))
                    pe.wait_ge(q_out, st.before())
                for t in range(TE):
                    nc.tensor.matmul(ps_kv(k)[:, t], h_t[:, k, t * P:(t + 1) * P], wkvq[:, 0:2 * D],
                                     start=True, stop=False)
                    nc.tensor.matmul(ps_kv(k)[:, t], ones3[:], bias[:, 0:2 * D], start=False, stop=True)
                    nc.tensor.matmul(ps_q(k)[:, t], h_t[:, k, (TE + t) * P:(TE + t + 1) * P], wkvq[:, 2 * D:],
                                     start=True, stop=False)
                    mm = nc.tensor.matmul(ps_q(k)[:, t], ones3[:], bias[:, 2 * D:3 * D], start=False, stop=True)
                mm.then_inc(projected, 1)

            run_steps(pe, steps, [(0, turn), (-1, merge), (0, project)], layer)


def l1_node_phase(core, w, steps, layer, table, h_table, x1_table, out):
    nc, psum = core.nc, core.psum
    ident, eps, ones3 = core.sb("ident", [P, P]), core.sb("ln_eps", [P, 1]), core.sb("ones3", [3, P], BF16)
    wo = core.sb("wo", [P, LAYERS, D])[:, layer]
    w1 = core.sb("w1", [P, LAYERS, 2 * D])[:, layer]
    w2 = core.sb("w2", [P, LAYERS, 2, D])[:, layer]
    b1col = core.sb("b1_col", [P, LAYERS, 2])[:, layer]
    diag = core.sb("ln1_g_diag", [P, LAYERS, P])[:, layer]
    g2rows, b2rows = core.sb("ln2_g_rows", [P, LAYERS, D])[:, layer], core.sb("ln2_b_rows", [P, LAYERS, D])[:, layer]
    bias = core.sb("bias_b", [3, LAYERS * 5 * D], BF16)[:].rearrange("p (l n) -> p l n", l=LAYERS)[:, layer]
    last = layer == LAYERS - 1

    node = lambda name: core.sb(name, [P, 2, TN, D])
    h_in, att, att_t, r1, n1, n1t = node("n_a"), node("n_b"), node("n_c"), node("n_d"), node("n_e"), node("n_f")
    n2, h_out, x1_in = node("n_g"), node("n_h"), node("n_i")
    agg = core.sb("agg", [P, 2, TN, MW])
    hidden = core.sb("hidden", [P, 2, 2, TN * P])
    z = core.sb("z", [P, TN, H1])
    rz = core.sb("rz", [P, 2, TN, H1])
    stats, mv = core.sb("n_stats", [P, TN, 6]), core.sb("n_mv", [P, 2, TN, 2])
    sd, rs = core.sb("n_sd", [P, TN]), core.sb("n_rs", [P, TN])
    stats2, mv2 = core.sb("n_stats2", [P, TN, 6]), core.sb("n_mv2", [P, 2, TN, 2])
    sd2, rs2, shift2 = core.sb("n_sd2", [P, TN]), core.sb("n_rs2", [P, 2, TN]), core.sb("n_shift2", [P, 2, TN])

    by_tile = lambda b: psum[:, b].rearrange("p (t n) -> p t n", t=TN)
    ps_at = by_tile(0)
    ps_nt = by_tile(1)
    ps_o = lambda k: by_tile(2 + k)
    ps_h = lambda c: psum[:, 4 + c]
    ps_f = lambda k: by_tile(6 + k)
    per_step = lambda t: t[0:steps * TN * P, :].rearrange("(s p j) d -> s p j d", p=P, j=TN)

    agg_landed, h_landed, x1_landed = core.sems("n1_agg_landed"), core.sems("n1_h_landed"), core.sems("n1_x1_landed")
    stored = core.sems("n1_stored")
    (z_made, rz_made, att_made, att_turned, att_out, o_made, r_made, stated, aggregated, rooted, inverted, normed,
     n1_turned, n1_out, up, relued, ffn_made, stated2, aggregated2, rooted2, inverted2, shifted2, normed2, scaled,
     h_made) = (core.sem("n1_" + n) for n in
                ("z_made", "rz_made", "att_made", "att_turned", "att_out", "o_made", "r_made", "stated",
                 "aggregated", "rooted", "inverted", "normed", "n1_turned", "n1_out", "up", "relued", "ffn_made",
                 "stated2", "aggregated2", "rooted2", "inverted2", "shifted2", "normed2", "scaled", "h_made"))

    with nc.Block() as block:
        @block.sync
        def _(sp):
            def load(st):
                k = st.slot
                if st.reused:
                    before, = held(core, sp, st.before())
                    sp.wait_ge(att_made, before)
                sp.dma_start(agg[:, k], per_step(table)[st.index]).then_inc(agg_landed[k], 16)
                if st.reused:
                    before, = held(core, sp, st.before())
                    sp.wait_ge(r_made, before)
                sp.dma_start(h_in[:, k], per_step(h_table)[st.index]).then_inc(h_landed[k], 16)

            def store(st):
                k = st.slot
                ready, = held(core, sp, st.done())
                sp.wait_ge(h_made, ready)
                if not last:
                    sp.dma_start(per_step(h_table)[st.index], h_out[:, k]).then_inc(stored[k], 16)
                elif isinstance(st.index, int) and (st.index + 1) * TN * P > out.shape[0]:
                    rows = out.shape[0] - st.index * TN * P
                    sp.dma_start(out[st.index * TN * P:, :].rearrange("(p j) d -> p j d", j=TN),
                                 h_out[0:rows // TN, k]).then_inc(stored[k], 16)
                else:
                    whole = out[0:out.shape[0] // (TN * P) * (TN * P), :]
                    sp.dma_start(whole.rearrange("(s p j) d -> s p j d", p=P, j=TN)[st.index],
                                 h_out[:, k]).then_inc(stored[k], 16)

            def load_x1(st):
                k = st.slot
                if not (isinstance(st.pair, int) and st.pair == 0):
                    before, = held(core, sp, st.before())
                    sp.wait_ge(h_made, before)
                sp.dma_start(x1_in[:, k], per_step(x1_table)[st.index]).then_inc(x1_landed[k], 16)

            run_steps(sp, steps, [(2, load), (-3, store)] + [(-1, load_x1)] * last, layer)
            end = Step(steps // 2 - 1, 1, steps, layer)
            for k in range(2):
                sp.wait_ge(stored[k], end.landed())

        @block.gpsimd
        def _(pool):
            def attend(st):
                k = st.slot
                pool.wait_ge(agg_landed[k], st.landed())
                pool.wait_ge(rz_made, st.done())
                if st.reused:
                    pool.wait_ge(att_turned, st.before())
                for j in range(TN):
                    ins = nc.gpsimd.tensor_tensor(att[:, k, j].rearrange("p (h d) -> p h d", h=H1),
                                                  agg[:, k, j, 0:D].rearrange("p (h d) -> p h d", h=H1),
                                                  over_lanes(rz[:, k, j], D1), ALU.mult)
                    if j == TN - 1:
                        ins.then_inc(att_made, 1)

            def finish(st):
                k = st.slot
                pool.wait_ge(normed2, st.done(TN))
                if st.reused:
                    pool.wait_ge(stored[k], st.landed_before())
                nc.gpsimd.tensor_tensor(h_out[:, k], n2[:, k], over_tiles(g2rows, TN), ALU.mult).then_inc(scaled, 1)
                pool.wait_ge(scaled, st.done())
                nc.gpsimd.tensor_tensor(h_out[:, k], h_out[:, k], over_tiles(b2rows, TN), ALU.add).then_inc(
                    scaled if last else h_made, 1)

            def finish_last(st):
                k = st.slot
                pool.wait_ge(normed2, st.done(TN))
                if st.reused:
                    pool.wait_ge(stored[k], st.landed_before())
                base = st.index * 2 + layer * steps
                nc.gpsimd.tensor_tensor(h_out[:, k], n2[:, k], over_tiles(g2rows, TN), ALU.mult).then_inc(scaled, 1)
                pool.wait_ge(scaled, base + 1)
                nc.gpsimd.tensor_tensor(h_out[:, k], h_out[:, k], over_tiles(b2rows, TN), ALU.add).then_inc(scaled, 1)
                pool.wait_ge(scaled, base + 2)
                pool.wait_ge(x1_landed[k], (st.pair + 1) * 16)
                nc.gpsimd.tensor_tensor(h_out[:, k], h_out[:, k], x1_in[:, k], ALU.add).then_inc(h_made, 1)

            run_steps(pool, steps, [(1, attend), (-2, finish_last if last else finish)], layer)

        @block.vector
        def _(dve):
            def weights_inverse(st):
                k = st.slot
                dve.wait_ge(agg_landed[k], st.landed())
                nc.vector.tensor_scalar(z[:], agg[:, k, :, D:], Z_EPS, None, ALU.add).then_inc(z_made, 1)
                dve.wait_ge(z_made, st.done())
                if st.reused:
                    dve.wait_ge(att_made, st.before())
                nc.vector.reciprocal(rz[:, k], z[:]).then_inc(rz_made, 1)
                dve.wait_ge(rz_made, st.done())

            def residual(st):
                k = st.slot
                dve.wait_ge(o_made, st.done())
                dve.wait_ge(h_landed[k], st.landed())
                if st.reused:
                    dve.wait_ge(normed, st.before(TN))
                nc.vector.tensor_tensor(r1[:, k], ps_o(k), h_in[:, k], ALU.add).then_inc(r_made, 1)
                dve.wait_ge(r_made, st.done())
                for j in range(TN):
                    nc.vector.bn_stats(stats[:, j], r1[:, k, j]).then_inc(stated, 1)
                all_stated, = held(core, dve, st.done(TN))
                dve.wait_ge(stated, all_stated)
                for j in range(TN):
                    nc.vector.bn_aggr(mv[:, k, j], stats[:, j]).then_inc(aggregated, 1)

            def normalise(st):
                k = st.slot
                dve.wait_ge(aggregated, st.done(TN))
                dve.wait_ge(rooted, st.done())
                nc.vector.reciprocal(rs[:], sd[:]).then_inc(inverted, 1)
                dve.wait_ge(inverted, st.done())
                if st.reused:
                    dve.wait_ge(n1_turned, st.before())
                for j in range(TN):
                    nc.vector.tensor_scalar(n1[:, k, j], r1[:, k, j], mv[:, k, j, 0:1], rs[:, j:j + 1],
                                            ALU.subtract, ALU.mult).then_inc(normed, 1)

            def statistics2(st):
                k = st.slot
                dve.wait_ge(ffn_made, st.done())
                for j in range(TN):
                    nc.vector.bn_stats(stats2[:, j], ps_f(k)[:, j]).then_inc(stated2, 1)
                all_stated, used = held(core, dve, st.done(TN), st.before() if st.reused else 0)
                dve.wait_ge(stated2, all_stated)
                dve.wait_ge(shifted2, used)
                for j in range(TN):
                    nc.vector.bn_aggr(mv2[:, k, j], stats2[:, j]).then_inc(aggregated2, 1)

            def shift(st):
                k = st.slot
                dve.wait_ge(aggregated2, st.done(TN))
                dve.wait_ge(rooted2, st.done())
                if st.reused:
                    dve.wait_ge(normed2, st.before(TN))
                nc.vector.reciprocal(rs2[:, k], sd2[:]).then_inc(inverted2, 1)
                dve.wait_ge(inverted2, st.done())
                nc.vector.scalar_tensor_tensor(out=shift2[:, k], in0=mv2[:, k, :, 0], scalar=-1.0, in1=rs2[:, k],
                                               op0=ALU.mult, op1=ALU.mult).then_inc(shifted2, 1)

            run_steps(dve, steps, [(1, weights_inverse), (0, residual), (-2, statistics2), (0, normalise), (-2, shift)],
                      layer)

        @block.scalar
        def _(act):
            def n1_to_sbuf(st):
                act.wait_ge(n1_turned, st.done())
                if st.reused:
                    act.wait_ge(ffn_made, st.before())
                nc.scalar.copy(n1t[:, st.slot], ps_nt).then_inc(n1_out, 1)

            def att_to_sbuf(st):
                act.wait_ge(att_turned, st.done())
                if st.reused:
                    act.wait_ge(o_made, st.before())
                nc.scalar.copy(att_t[:, st.slot], ps_at).then_inc(att_out, 1)

            def root(st):
                act.wait_ge(aggregated, st.done(TN))
                if st.reused:
                    act.wait_ge(inverted, st.done() - 1)
                nc.scalar.activation(sd[:], mv[:, st.slot, :, 1], ACT.Sqrt, bias=eps[:, 0:1]).then_inc(rooted, 1)

            def relu(st):
                act.wait_ge(up, st.done())
                if st.reused:
                    act.wait_ge(ffn_made, st.before())
                for c in range(2):
                    nc.scalar.activation(hidden[:, st.slot, c], ps_h(c), ACT.Relu,
                                         bias=b1col[:, c:c + 1]).then_inc(relued, 1)

            def root2(st):
                act.wait_ge(aggregated2, st.done(TN))
                if st.reused:
                    act.wait_ge(inverted2, st.done() - 1)
                nc.scalar.activation(sd2[:], mv2[:, st.slot, :, 1], ACT.Sqrt, bias=eps[:, 0:1]).then_inc(rooted2, 1)

            def normalise2(st):
                k = st.slot
                act.wait_ge(shifted2, st.done())
                if st.reused:
                    act.wait_ge(h_made, st.before())
                for j in range(TN):
                    nc.scalar.activation(n2[:, k, j], ps_f(k)[:, j], ACT.Identity, bias=shift2[:, k, j:j + 1],
                                         scale=rs2[:, k, j:j + 1]).then_inc(normed2, 1)

            run_steps(act, steps, [(-1, n1_to_sbuf), (0, root), (-1, relu), (1, att_to_sbuf), (-2, root2),
                                   (-2, normalise2)], layer)

        @block.tensor
        def _(pe):
            def turn_n1(st):
                pe.wait_ge(normed, st.done(TN))
                if st.reused:
                    pe.wait_ge(n1_out, st.done() - 1)
                for j in range(TN):
                    mm = nc.tensor.transpose(ps_nt[:, j], n1[:, st.slot, j], ident[:])
                mm.then_inc(n1_turned, 1)

            def turn_att(st):
                pe.wait_ge(att_made, st.done())
                if st.reused:
                    pe.wait_ge(att_out, st.done() - 1)
                for j in range(TN):
                    mm = nc.tensor.transpose(ps_at[:, j], att[:, st.slot, j], ident[:])
                mm.then_inc(att_turned, 1)

            def output(st):
                k = st.slot
                pe.wait_ge(att_out, st.done())
                if st.reused:
                    pe.wait_ge(r_made, st.before())
                for j in range(TN):
                    nc.tensor.matmul(ps_o(k)[:, j], att_t[:, k, j], wo, start=True, stop=False)
                    mm = nc.tensor.matmul(ps_o(k)[:, j], ones3[:], bias[:, 3 * D:4 * D], start=False, stop=True)
                mm.then_inc(o_made, 1)

            def widen(st):
                k = st.slot
                pe.wait_ge(n1_out, st.done())
                if st.reused:
                    pe.wait_ge(relued, (st.done() - 1) * 2)
                for c in range(2):
                    mm = nc.tensor.matmul(ps_h(c), w1[:, c * D:(c + 1) * D], n1t[:, k].rearrange("p j n -> p (j n)"),
                                          start=True, stop=True)
                mm.then_inc(up, 1)

            def narrow(st):
                k = st.slot
                pe.wait_ge(relued, st.done(2))
                if st.reused:
                    pe.wait_ge(normed2, st.before(TN))
                    pe.wait_ge(stated2, st.before(TN))
                for j in range(TN):
                    out_j = ps_f(k)[:, j]
                    for c in range(2):
                        nc.tensor.matmul(out_j, hidden[:, k, c, j * P:(j + 1) * P], w2[:, c], start=(c == 0), stop=False)
                    nc.tensor.matmul(out_j, n1t[:, k, j], diag, start=False, stop=False)
                    mm = nc.tensor.matmul(out_j, ones3[:], bias[:, 4 * D:], start=False, stop=True)
                mm.then_inc(ffn_made, 1)

            run_steps(pe, steps, [(-1, turn_n1), (0, output), (-1, widen), (1, turn_att), (-2, narrow)], layer)


def build(nc, w, out):
    node_rows = w["x"].shape[0]
    node_steps, edge_steps = node_rows // (TN * P), w["ends"].shape[0]
    assert node_steps % 2 == 0 and edge_steps % 2 == 0
    scratch = lambda name, rows, cols: nc.dram_tensor(name, (rows, cols), F32).ap()
    sums0 = scratch("l0_sums", node_rows + P, D)
    sums1 = [scratch(f"l1_sums_{l}", node_rows + P, MW) for l in range(LAYERS)]
    x1_table, h_table = scratch("x1_table", node_rows, D), scratch("h_table", node_rows, D)
    with ExitStack() as ctx:
        core = Core(nc, ctx)
        core.psum = ctx.enter_context(nc.psum_tensor("psum", [P, 8, 512], F32))
        setup_phase(core, w, [sums0, *sums1])
        l0_edge_phase(core, w, edge_steps, w["x"], sums0)
        l0_node_phase(core, w, node_steps, w["x"], sums0, x1_table, h_table)
        for layer in range(LAYERS):
            l1_edge_phase(core, w, edge_steps, layer, h_table, sums1[layer])
            l1_node_phase(core, w, node_steps, layer, sums1[layer], h_table, x1_table, out)


def kernel(**inputs):
    import numpy as _np
    import concourse.bacc as _bacc
    from concourse import mybir as _mybir
    from concourse.bass_utils import run_bass_kernel_spmd as _run

    a = {k: _np.asarray(v) for k, v in inputs.items()}
    nodes, edges = a["x"].shape[0], a["src"].shape[0]
    node_steps = -(-nodes // (TN * P * 2)) * 2
    edge_steps = -(-edges // (TE * P * 2)) * 2
    rows, slots = node_steps * TN * P, edge_steps * TE * P
    assert rows > nodes
    src = _np.full(slots, nodes, _np.int32)
    src[:edges] = a["src"]
    dst = _np.full(slots, nodes, _np.int32)
    dst[:edges] = a["dst"]
    x = _np.zeros((rows, D), _np.float32)
    x[:nodes] = a["x"]
    attr_t = _np.zeros((FE, slots), _np.float32)
    attr_t[:, :edges] = a["edge_attr_16"].T
    by_partition = lambda v: v.reshape(edge_steps, TE, P).transpose(0, 2, 1)
    arrays = {
        "x": x, "attr_T": attr_t,
        "ends": _np.concatenate([by_partition(src), by_partition(dst)], axis=2),
        "src_rows": src.reshape(edge_steps, TE * P), "dst_rows": dst.reshape(edge_steps, TE * P),
        "a_T": a["L0_gnn_a"].T, "ln1_g_T": a["L1_gnn_ln1_g"].T, "ln1_b_T": a["L1_gnn_ln1_b"].T,
        "b1_T": a["L1_gnn_b1"].reshape(LAYERS, 2, P).transpose(2, 0, 1).reshape(P, LAYERS * 2),
    }
    for name in ("L0_gnn_W", "L0_gnn_a", "L1_gnn_Wemb", "L1_gnn_Wq", "L1_gnn_bq", "L1_gnn_Wk", "L1_gnn_bk", "L1_gnn_Wv",
                 "L1_gnn_bv", "L1_gnn_Wo", "L1_gnn_bo", "L1_gnn_ln1_b", "L1_gnn_W1", "L1_gnn_W2", "L1_gnn_b2",
                 "L1_gnn_ln2_g", "L1_gnn_ln2_b"):
        arrays[name] = a[name]
    nc = _bacc.Bacc("TRN2", target_bir_lowering=False, num_devices=1)
    given, w = {}, {}
    for name, v in arrays.items():
        v = _np.ascontiguousarray(v)
        given[f"in_{name}"] = v
        w[name] = nc.dram_tensor(f"in_{name}", v.shape, _mybir.dt.from_np(v.dtype), kind="ExternalInput").ap()
    out = nc.dram_tensor("out", (nodes, D), _mybir.dt.float32, kind="ExternalOutput").ap()
    build(nc, w, out)
    r = _run(nc, [given], core_ids=[0])
    return r.results[0]["out"]
```

```python
from contextlib import ExitStack

import numpy as np
import concourse.bass as bass
from concourse import mybir

P = 128
TE = 2
TN = 4
TURN = 4
D = 128
H0, D0 = 4, 32
FE = 16
H1, D1 = 8, 16
MW = D + H1
LAYERS = 3
ALPHA = 0.2
LN_EPS = 1e-5
Z_EPS = 1e-6
CLIP = 5.0
EXP_AND_LN = "natural_log_exp_and_others"
SCALE = float(np.sqrt(D1))

ALU = mybir.AluOpType
ACT = mybir.ActivationFunctionType
AX = mybir.AxisListType
F32 = mybir.dt.float32
BF16 = mybir.dt.bfloat16
I32 = mybir.dt.int32
U32 = mybir.dt.uint32


class Step:

    def __init__(self, turn, place, steps, layer):
        self.turn, self.place, self.steps, self.layer = turn, place, steps, layer
        self.slot = place % 2
        self.pair = turn * 2 + place // 2
        self.index = turn * TURN + place
        self.reused = not (isinstance(turn, int) and turn == 0 and place < 2 and layer == 0)
        self.place_reused = not (isinstance(turn, int) and turn == 0 and layer == 0)

    def done(self, n=1):
        return (self.index + (self.layer * self.steps + 1)) * n

    def before(self, n=1):
        return (self.index + (self.layer * self.steps - 1)) * n

    def landed(self, n=16):
        return (self.pair + (self.layer * self.steps // 2 + 1)) * n

    def landed_before(self, n=16):
        return (self.pair + self.layer * self.steps // 2) * n

    def turn_before(self, n=1):
        return self.before(n) - 2 * n

    def place_landed(self, n=16):
        return (self.turn + (self.layer * ((self.steps - self.place + TURN - 1) // TURN) + 1)) * n

    def place_landed_before(self, n=16):
        return (self.turn + self.layer * ((self.steps - self.place + TURN - 1) // TURN)) * n


def last_step(steps, layer):
    return Step((steps - 1) // TURN, (steps - 1) % TURN, steps, layer)


def run_steps(engine, steps, stages, layer=0):
    least, most = min(a for a, _ in stages), max(a for a, _ in stages)
    first, last = -most, steps - least
    start = -(least - TURN) // TURN * TURN + TURN * ((least - TURN) % TURN > 0)
    end = start + (steps - most - start) // TURN * TURN

    def plain(rounds):
        for r in rounds:
            for ahead, emit in stages:
                if 0 <= r + ahead < steps:
                    emit(Step((r + ahead) // TURN, (r + ahead) % TURN, steps, layer))

    if end - start < 2 * TURN:
        plain(range(first, last))
        return
    plain(range(first, start))
    with engine.Fori(start // TURN, end // TURN) as turn:
        for r in range(TURN):
            for ahead, emit in stages:
                emit(Step(turn + (r + ahead) // TURN, (r + ahead) % TURN, steps, layer))
    plain(range(end, last))


class Core:

    def __init__(self, nc, ctx):
        self.nc, self.ctx, self.kept = nc, ctx, {}

    def sb(self, name, shape, dt=F32):
        if name not in self.kept:
            self.kept[name] = self.ctx.enter_context(self.nc.sbuf_tensor(name, shape, dt))
        return self.kept[name]

    def sem(self, name):
        if name not in self.kept:
            self.kept[name] = self.ctx.enter_context(self.nc.semaphore(name))
        return self.kept[name]

    def count(self, engine, n, value):
        if isinstance(value, int):
            return value
        key = f"count_{engine.engine.name}_{n}"
        if key not in self.kept:
            self.kept[key] = engine.alloc_register(key)
        engine.reg_mov(self.kept[key], value)
        return self.kept[key]

    def sems(self, name):
        return [self.sem(f"{name}_{k}") for k in range(2)]

    def place_sems(self, name):
        return [self.sem(f"{name}_{k}") for k in range(TURN)]


def held(core, engine, *counts):
    kept = [core.count(engine, n, v) for n, v in enumerate(counts)]
    engine.wait_ge(core.sem("consts_made"), 5)
    return kept


def over_tiles(row, tiles):
    return row.unsqueeze(1).to_broadcast([P, tiles, row.shape[-1]])


def over_lanes(heads, width):
    return heads.unsqueeze(len(heads.shape)).to_broadcast([*heads.shape, width])


def setup_phase(core, w, table, trash_row, zero_width):
    nc = core.nc
    psum = core.psum
    loaded = core.sem("weights_loaded")
    pool_made, dve_made, pe_made = core.sem("consts_made"), core.sem("prep_dve"), core.sem("prep_pe")
    ident, later, trash_i = core.sb("ident", [P, P]), core.sb("later", [P, P]), core.sb("trash_i", [P, 1], I32)
    trash, eps, ones = core.sb("trash", [P, 1]), core.sb("ln_eps", [P, 1]), core.sb("ones", [P, P], BF16)
    w0, wi = core.sb("w0_ext", [P, D + H0]), core.sb("w0_src", [P, H0])
    a_rows = core.sb("a_rows", [P, H0, 2 * D0 + FE])
    ae, attr = core.sb("a_edge", [P, H0]), core.sb("attr", [P, 2, TE * P])
    aw = core.sb("a_times_w", [P, D])
    wemb = core.sb("wemb", [P, D])
    wkvq = core.sb("wkvq", [P, LAYERS, 3 * D])
    wo = core.sb("wo", [P, LAYERS, D])
    w1 = core.sb("w1", [P, LAYERS, 2 * D])
    w2 = core.sb("w2", [P, LAYERS, 2, D])
    g1col, b1lncol = core.sb("ln1_g_col", [P, LAYERS]), core.sb("ln1_b_col", [P, LAYERS])
    b1col = core.sb("b1_col", [P, LAYERS, 2])
    g1rows, g2rows, b2rows = (core.sb(f"{n}_rows", [P, LAYERS, D]) for n in ("ln1_g", "ln2_g", "ln2_b"))
    nb = 5 * D
    bias3 = core.sb("bias3", [3, LAYERS, nb])
    lnb3 = core.sb("lnb3", [3, LAYERS, D])
    part = core.sb("bias_part", [3, 3, LAYERS * nb], BF16)
    rest = core.sb("bias_rest", [3, LAYERS * nb])
    picked = core.sb("bias_picked", [3, LAYERS * nb])
    bias_b = core.sb("bias_b", [P, LAYERS * nb], BF16)
    zeros = core.sb("zeros", [P, zero_width])

    loads = [(w0[:, 0:D], w["L0_gnn_W"]), (wemb[:], w["L1_gnn_Wemb"]),
             (a_rows[:].rearrange("p h a -> p (h a)"), w["L0_gnn_a"].rearrange("h a -> (h a)").partition_broadcast(P)),
             (wkvq[:, :, 0:D], w["L1_gnn_Wk"].rearrange("l p n -> p l n")),
             (wkvq[:, :, D:2 * D], w["L1_gnn_Wv"].rearrange("l p n -> p l n")),
             (wkvq[:, :, 2 * D:], w["L1_gnn_Wq"].rearrange("l p n -> p l n")),
             (wo[:], w["L1_gnn_Wo"].rearrange("l p n -> p l n")),
             (w1[:], w["L1_gnn_W1"].rearrange("l p n -> p l n")),
             (g1col[:], w["ln1_g_T"]), (b1lncol[:], w["ln1_b_T"]), (b1col[:].rearrange("p l c -> p (l c)"), w["b1_T"]),
             (g1rows[:].rearrange("p l n -> p (l n)"), w["L1_gnn_ln1_g"].rearrange("l n -> (l n)").partition_broadcast(P)),
             (g2rows[:].rearrange("p l n -> p (l n)"), w["L1_gnn_ln2_g"].rearrange("l n -> (l n)").partition_broadcast(P)),
             (b2rows[:].rearrange("p l n -> p (l n)"), w["L1_gnn_ln2_b"].rearrange("l n -> (l n)").partition_broadcast(P)),
             (lnb3[:].rearrange("p l n -> p (l n)"), w["L1_gnn_ln1_b"].rearrange("l n -> (l n)").partition_broadcast(3))]
    loads += [(w2[:, l], w["L1_gnn_W2"][l].rearrange("(c p) n -> p c n", p=P)) for l in range(LAYERS)]
    loads += [(bias3[:, :, c * D:(c + 1) * D], w[f"L1_gnn_{b}"].partition_broadcast(3))
              for c, b in enumerate(("bk", "bv", "bq", "bo", "b2"))]

    with nc.Block() as block:
        @block.sync
        def _(sp):
            for dst, src in loads:
                sp.dma_start(dst, src).then_inc(loaded, 16)
            sp.wait_ge(dve_made, 5)
            sp.dma_start(ae[0:FE, :], w["a_T"][2 * D0:, :]).then_inc(loaded, 16)

        @block.scalar
        def _(act):
            act.wait_ge(dve_made, 1)
            view = table.rearrange("r d -> (r d)").rearrange("(c p n) -> c p n", c=8, p=P)
            part_width = view.shape[-1]
            source = core.sb("zeros_0", [P, part_width])
            for c in range(8):
                act.dma_start(view[c], source[:]).then_inc(core.sem("zeroed_0"), 16)

        @block.gpsimd
        def _(pool):
            nc.gpsimd.memset(ident[:], 0.0).then_inc(pool_made, 1)
            nc.gpsimd.memset(later[:], 1.0).then_inc(pool_made, 1)
            pool.wait_ge(pool_made, 2)
            nc.gpsimd.affine_select(out=ident[:], in_=ident[:], compare_op=ALU.not_equal, fill=1.0, base=0,
                                    pattern=[[-1, P]], channel_multiplier=1).then_inc(pool_made, 1)
            nc.gpsimd.affine_select(out=later[:], in_=later[:], compare_op=ALU.is_gt, fill=0.0, base=0,
                                    pattern=[[1, P]], channel_multiplier=-1).then_inc(pool_made, 1)
            nc.gpsimd.iota(trash_i[:], [[0, 1]], base=trash_row, channel_multiplier=1).then_inc(pool_made, 1)

        @block.vector
        def _(dve):
            made = [0]

            def then(instruction):
                instruction.then_inc(dve_made, 1)
                made[0] += 1
                dve.wait_ge(dve_made, made[0])

            then(nc.vector.memset(core.sb("zeros_0", [P, table.shape[0] * D // P // 8])[:], 0.0))
            then(nc.vector.memset(eps[:], LN_EPS))
            then(nc.vector.memset(ones[:], 1.0))
            then(nc.vector.memset(bias_b[:], 0.0))
            then(nc.vector.memset(ae[:], 0.0))
            then(nc.vector.memset(attr[:], 0.0))
            then(nc.vector.memset(zeros[:], 0.0))
            dve.wait_ge(pool_made, 5)
            then(nc.vector.tensor_copy(trash[:], trash_i[:]))
            dve.wait_ge(loaded, 16 * (len(loads) + 1))
            w_heads = w0[:, 0:D].rearrange("p (h d) -> p h d", h=H0)
            for out, lo in ((wi[:], 0), (w0[:, D:D + H0], D0)):
                then(nc.vector.tensor_tensor(aw[:].rearrange("p (h d) -> p h d", h=H0), w_heads,
                                             a_rows[:, :, lo:lo + D0], ALU.mult))
                then(nc.vector.tensor_reduce(out, aw[:].rearrange("p (h d) -> p h d", h=H0), AX.X, ALU.add))
            then(nc.vector.tensor_tensor(bias3[:, :, 4 * D:], bias3[:, :, 4 * D:], lnb3[:], ALU.add))
            flat = bias3[:].rearrange("p l n -> p (l n)")
            then(nc.vector.tensor_copy(rest[:], flat))
            for c in range(3):
                then(nc.vector.tensor_copy(part[:, c], rest[:]))
                then(nc.vector.tensor_tensor(rest[:], rest[:], part[:, c], ALU.subtract))
            then(nc.vector.tensor_scalar(picked[:], part[:, 0], ident[0:3, 0:1], None, ALU.mult))
            for c in range(1, 3):
                then(nc.vector.scalar_tensor_tensor(out=picked[:], in0=part[:, c], scalar=ident[0:3, c:c + 1],
                                                    in1=picked[:], op0=ALU.mult, op1=ALU.add))
            then(nc.vector.tensor_copy(bias_b[0:3, :], picked[:]))
            dve.wait_ge(pe_made, 1)
            for l in range(LAYERS):
                then(nc.vector.tensor_tensor(b1col[:, l], b1col[:, l], psum[:, 0, 2 * l:2 * l + 2], ALU.add))
                then(nc.vector.tensor_scalar(w1[:, l], w1[:, l], g1col[:, l:l + 1], None, ALU.mult))

        @block.tensor
        def _(pe):
            pe.wait_ge(loaded, 16 * (len(loads) + 1))
            for l in range(LAYERS):
                for c in range(2):
                    mm = nc.tensor.matmul(psum[:, 0, 2 * l + c:2 * l + c + 1], w1[:, l, c * D:(c + 1) * D],
                                          b1lncol[:, l:l + 1], start=True, stop=True)
            mm.then_inc(pe_made, 1)


def guess_root(core, nc, act, st, prefix, var, guess):
    logged, guessed, refined = (core.sem(f"{prefix}_{n}") for n in ("logged", "guessed", "refined"))
    log = core.sb(f"{prefix}_log", [P, var.shape[-1]])
    first = isinstance(st.index, int) and st.index == 0
    if not first:
        act.wait_ge(guessed, st.done() - 1)
    nc.scalar.activation(log[:], var, ACT.Ln, bias=core.sb("ln_eps", [P, 1])[:, 0:1]).then_inc(logged, 1)
    act.wait_ge(logged, st.done())
    if not first:
        act.wait_ge(refined, st.done(3) - 3)
    nc.scalar.activation(guess[:], log[:], ACT.Exp, scale=-0.5).then_inc(guessed, 1)


def refine_root(core, nc, dve, st, prefix, var, guess, rs):
    guessed, refined = core.sem(f"{prefix}_guessed"), core.sem(f"{prefix}_refined")
    square, off, shifted = (core.sb(f"{prefix}_{n}", [P, var.shape[-1]]) for n in ("square", "off", "shifted"))
    nc.vector.tensor_scalar(shifted[:], var, LN_EPS, None, ALU.add).then_inc(core.sem(f"{prefix}_var_shifted"), 1)
    dve.wait_ge(guessed, st.done())
    nc.vector.tensor_tensor(square[:], guess[:], guess[:], ALU.mult).then_inc(refined, 1)
    dve.wait_ge(core.sem(f"{prefix}_var_shifted"), st.done())
    dve.wait_ge(refined, st.done(3) - 2)
    nc.vector.scalar_tensor_tensor(out=off[:], in0=square[:], scalar=-0.5, in1=shifted[:], op0=ALU.mult,
                                   op1=ALU.mult).then_inc(refined, 1)
    dve.wait_ge(refined, st.done(3) - 1)
    nc.vector.scalar_tensor_tensor(out=rs[:], in0=off[:], scalar=1.5, in1=guess[:], op0=ALU.add,
                                   op1=ALU.mult).then_inc(refined, 1)
    dve.wait_ge(refined, st.done(3))


def match_edges(core, nc, dve, st, prefix, ids, rows, match):
    for t in range(TE):
        nc.vector.tensor_scalar(match[:, st.slot, t], rows[:, st.slot, t * P:(t + 1) * P],
                                ids[:, st.slot, t:t + 1], None, ALU.is_equal).then_inc(core.sem(f"{prefix}_matched"), 1)


def pick_targets(core, nc, dve, st, prefix, ids, match, target):
    later, trash = core.sb("later", [P, P]), core.sb("trash", [P, 1])
    scratch, lone, moved, others = (core.sb("pick_scratch", [P, TE, P]), core.sb("pick_lone", [P, TE]),
                                    core.sb("pick_moved", [P, TE]), core.sb("pick_others", [P, TE]))
    matched, counted = core.sem(f"{prefix}_matched"), core.sem(f"{prefix}_counted")
    chained, picked, added = core.sem(f"{prefix}_chained"), core.sem(f"{prefix}_picked"), core.sems(f"{prefix}_added")
    k = st.slot
    dve.wait_ge(matched, st.done(TE))
    for t in range(TE):
        nc.vector.tensor_tensor_reduce(out=scratch[:, t], in0=match[:, k, t], in1=later[:], scale=1.0, scalar=0.0,
                                       op0=ALU.mult, op1=ALU.add, accum_out=others[:, t:t + 1]).then_inc(counted, 1)
    dve.wait_ge(counted, st.done(TE))
    nc.vector.tensor_scalar(lone[:], others[:], 0.0, None, ALU.is_equal).then_inc(chained, 1)
    nc.vector.tensor_scalar(moved[:], ids[:, k, 0:TE], trash[:, 0:1], None, ALU.subtract).then_inc(chained, 1)
    dve.wait_ge(chained, st.done(3) - 1)
    nc.vector.tensor_tensor(moved[:], moved[:], lone[:], ALU.mult).then_inc(chained, 1)
    dve.wait_ge(chained, st.done(3))
    if st.reused:
        dve.wait_ge(added[k], st.landed_before(16 * TE))
    nc.vector.tensor_scalar(target[:, k], moved[:], trash[:, 0:1], None, ALU.add).then_inc(picked, 1)


def gather_and_add(core, nc, pool, steps, layer, prefix, lag, source, table, zeroed, zero_parts, ends, rows_in,
                   users, sums, target):
    ends_landed, gathered = core.place_sems(f"{prefix}_ends_landed"), core.place_sems(f"{prefix}_gathered")
    added = core.sems(f"{prefix}_added")
    rows_used, uses = core.sem(users[0]), users[1]
    summed, picked = core.sem(f"{prefix}_summed"), core.sem(f"{prefix}_picked")

    def gather(st, t):
        k = st.place
        if t == 0:
            counts = held(core, pool, st.place_landed(), *[st.turn_before(uses)] * st.place_reused)
            pool.wait_ge(ends_landed[k], counts[0])
            if st.place_reused:
                pool.wait_ge(rows_used, counts[1])
        for c in (t, TE + t):
            nc.gpsimd.indirect_dma_start(
                rows_in[:, k, c], None, source, bass.IndirectOffsetOnAxis(ap=ends[:, k, c:c + 1].bitcast(U32), axis=0)
            ).then_inc(gathered[k], 16)

    def add(st, t):
        k = st.slot
        if t == 0:
            if isinstance(st.index, int) and st.index == 0:
                pool.wait_ge(zeroed, 16 * zero_parts)
            done, previous = held(core, pool, st.done(), st.landed(16 * TE) if k == 1 else st.landed_before(16 * TE))
            pool.wait_ge(summed, done)
            pool.wait_ge(picked, done)
            pool.wait_ge(added[1 - k], previous)
        else:
            previous, = held(core, pool, st.landed_before(16 * TE) + 16 * t)
            pool.wait_ge(added[k], previous)
        nc.gpsimd.indirect_dma_start(
            table, bass.IndirectOffsetOnAxis(ap=target[:, k, t:t + 1].bitcast(U32), axis=0), sums[:, k, t], None,
            compute_op=ALU.add).then_inc(added[k], 16)

    stages = []
    for t in range(TE):
        stages += [(0, lambda st, t=t: gather(st, t)), (-lag, lambda st, t=t: add(st, t))]
    run_steps(pool, steps, stages, layer)
    end = last_step(steps, layer)
    for k in range(2):
        pool.wait_ge(added[k], end.landed(16 * TE))


def l0_edge_phase(core, w, steps, x, table, to_zero):
    nc, psum = core.nc, core.psum
    ident = core.sb("ident", [P, P])
    w0, wi, ae = core.sb("w0_ext", [P, D + H0]), core.sb("w0_src", [P, H0]), core.sb("a_edge", [P, H0])
    ends, ids = core.sb("ends", [P, TURN, 2 * TE], I32), core.sb("ids", [P, 2, TE])
    equal_rows = core.sb("equal_rows", [P, 2, TE * P], I32)
    attr = core.sb("attr", [P, 2, TE * P])
    x_in = core.sb("rows_in", [P, TURN, 2 * TE, D])
    n_in, x_t = core.sb("normed", [P, 2, 2 * TE, D]), core.sb("rows_t", [P, 2, 2 * TE * P])
    stats, mv = core.sb("e_stats", [P, 2 * TE, 6]), core.sb("e_mv", [P, 2, 2 * TE, 2])
    guess, rs = core.sb("e_guess", [P, 2 * TE]), core.sb("e_rs", [P, 2 * TE])
    match = core.sb("match", [P, 2, TE, P])
    target = core.sb("target", [P, 2, TE], I32)
    logit, leaky = core.sb("logit", [P, 2, TE, H0]), core.sb("leaky", [P, TE, H0])
    top, centred = core.sb("top", [P, TE]), core.sb("centred", [P, 2, TE, H0])
    grown, total = core.sb("grown", [P, 2, TE, H0]), core.sb("total", [P, TE])
    share = core.sb("share", [P, TE, H0])
    msg, sums = core.sb("msg0", [P, 2, TE, D]), core.sb("sums0", [P, 2, TE, D])

    ps_t = lambda k: psum[:, k]
    ps_w = lambda k: psum[:, 2 + k].rearrange("p (t n) -> p t n", t=TE)
    ps_m = lambda k: psum[:, 4 + k, 0:TE * D].rearrange("p (t n) -> p t n", t=TE)

    ends_landed, rows_landed = core.place_sems("e0_ends_landed"), core.sems("e0_rows_landed")
    attr_landed, gathered, added = core.sems("e0_attr_landed"), core.place_sems("e0_gathered"), core.sems("e0_added")
    (cast, stated, aggregated, normed, turned, relued, projected, logits_out, matched,
     picked, chain, centre_done, exped, weighed, merged, summed) = (
        core.sem("e0_" + n) for n in
        ("cast", "stated", "aggregated", "normed", "turned", "relued",
         "projected", "logits_out", "matched", "picked", "softmaxed", "centred", "exped", "weighed", "merged",
         "summed"))

    with nc.Block() as block:
        @block.sync
        def _(sp):
            zeroed = core.sem("zeroed_1")

            def load(st):
                if st.place_reused:
                    used, previous = held(core, sp, st.place_landed_before(16 * 2 * TE), st.turn_before())
                    sp.wait_ge(gathered[st.place], used)
                    sp.wait_ge(cast, previous)
                sp.dma_start(ends[:, st.place], w["ends"][st.index]).then_inc(ends_landed[st.place], 16)

            def load_rows(st):
                k = st.slot
                if st.reused:
                    before, = held(core, sp, st.before(TE))
                    sp.wait_ge(matched, before)
                sp.dma_start(equal_rows[:, k], w["src_rows"][st.index].partition_broadcast(P)).then_inc(rows_landed[k], 16)
                if st.reused:
                    before, = held(core, sp, st.before())
                    sp.wait_ge(projected, before)
                sp.dma_start(attr[0:FE, k], w["attr_T"][:, bass.ds(st.index * (TE * P), TE * P)]).then_inc(attr_landed[k], 16)

            def zero(st):
                sp.dma_start(to_zero[st.index], core.sb("zeros", [P, to_zero.shape[-1]])[:]).then_inc(zeroed, 16)

            run_steps(sp, steps, [(2, load), (0, load_rows), (0, zero)])

        @block.gpsimd
        def _(pool):
            gather_and_add(core, nc, pool, steps, 0, "e0", 3, x, table, core.sem("zeroed_0"), 8, ends, x_in,
                           ("e0_normed", 2 * TE), sums, target)

        @block.vector
        def _(dve):
            def statistics(st):
                k = st.slot
                dve.wait_ge(ends_landed[st.place], st.place_landed())
                if st.reused:
                    dve.wait_ge(picked, st.before())
                nc.vector.tensor_copy(ids[:, k], ends[:, st.place, 0:TE]).then_inc(cast, 1)
                dve.wait_ge(gathered[st.place], st.place_landed(16 * 2 * TE))
                for c in range(2 * TE):
                    nc.vector.bn_stats(stats[:, c], x_in[:, st.place, c]).then_inc(stated, 1)
                all_stated, = held(core, dve, st.done(2 * TE))
                dve.wait_ge(stated, all_stated)
                for c in range(2 * TE):
                    nc.vector.bn_aggr(mv[:, k, c], stats[:, c]).then_inc(aggregated, 1)

            def normalise(st):
                k = st.slot
                dve.wait_ge(aggregated, st.done(2 * TE))
                refine_root(core, nc, dve, st, "e0", mv[:, k, :, 1], guess, rs)
                if st.reused:
                    dve.wait_ge(turned, st.before())
                for c in range(2 * TE):
                    nc.vector.tensor_scalar(n_in[:, k, c], x_in[:, st.place, c], mv[:, k, c, 0:1], rs[:, c:c + 1],
                                            ALU.subtract, ALU.mult).then_inc(normed, 1)

            def centre(st):
                k = st.slot
                dve.wait_ge(logits_out, st.done())
                nc.vector.scalar_tensor_tensor(out=leaky[:], in0=logit[:, k], scalar=ALPHA, in1=logit[:, k],
                                               op0=ALU.mult, op1=ALU.max).then_inc(chain, 1)
                dve.wait_ge(chain, st.done(5) - 4)
                nc.vector.tensor_reduce(top[:], leaky[:], AX.X, ALU.max).then_inc(chain, 1)
                dve.wait_ge(chain, st.done(5) - 3)
                nc.vector.tensor_tensor(centred[:, k], leaky[:], over_lanes(top[:], H0), ALU.subtract).then_inc(centre_done, 1)

            def weigh(st):
                k = st.slot
                dve.wait_ge(exped, st.done())
                nc.vector.tensor_reduce(total[:], grown[:, k], AX.X, ALU.add).then_inc(chain, 1)
                dve.wait_ge(chain, st.done(5) - 2)
                nc.vector.reciprocal(total[:], total[:]).then_inc(chain, 1)
                dve.wait_ge(cast, st.done())
                dve.wait_ge(rows_landed[k], st.landed())
                if st.reused:
                    dve.wait_ge(merged, st.before())
                match_edges(core, nc, dve, st, "e0", ids, equal_rows, match)
                dve.wait_ge(chain, st.done(5) - 1)
                nc.vector.tensor_tensor(share[:], grown[:, k], over_lanes(total[:], H0), ALU.mult).then_inc(chain, 1)
                dve.wait_ge(chain, st.done(5))
                nc.vector.tensor_tensor(msg[:, k].rearrange("p t (h d) -> p t h d", h=H0),
                                        ps_w(k)[:, :, 0:D].rearrange("p t (h d) -> p t h d", h=H0),
                                        over_lanes(share[:], D0), ALU.mult).then_inc(weighed, 1)
                pick_targets(core, nc, dve, st, "e0", ids, match, target)

            run_steps(dve, steps, [(0, statistics), (-1, centre), (0, normalise), (-1, weigh)])

        @block.scalar
        def _(act):
            act.preload_act_table_set(EXP_AND_LN)

            def root(st):
                act.wait_ge(aggregated, st.done(2 * TE))
                guess_root(core, nc, act, st, "e0", mv[:, st.slot, :, 1], guess)

            def relu_turned(st):
                act.wait_ge(turned, st.done())
                if st.reused:
                    act.wait_ge(projected, st.before())
                nc.scalar.activation(x_t[:, st.slot], ps_t(st.slot), ACT.Relu).then_inc(relued, 1)

            def logits(st):
                act.wait_ge(projected, st.done())
                nc.scalar.copy(logit[:, st.slot], ps_w(st.slot)[:, :, D:D + H0]).then_inc(logits_out, 1)

            def exp(st):
                act.wait_ge(centre_done, st.done())
                nc.scalar.activation(grown[:, st.slot], centred[:, st.slot], ACT.Exp).then_inc(exped, 1)

            def sums_out(st):
                act.wait_ge(merged, st.done())
                if st.reused:
                    act.wait_ge(added[st.slot], st.landed_before(16 * TE))
                nc.scalar.copy(sums[:, st.slot], ps_m(st.slot)).then_inc(summed, 1)

            run_steps(act, steps, [(0, root), (-1, exp), (0, relu_turned), (-1, sums_out), (0, logits)])

        @block.tensor
        def _(pe):
            def turn(st):
                k = st.slot
                pe.wait_ge(normed, st.done(2 * TE))
                if st.reused:
                    pe.wait_ge(relued, st.before())
                for c in range(2 * TE):
                    mm = nc.tensor.transpose(ps_t(k)[:, c * P:(c + 1) * P], n_in[:, k, c], ident[:])
                mm.then_inc(turned, 1)

            def project(st):
                k = st.slot
                pe.wait_ge(relued, st.done())
                pe.wait_ge(attr_landed[k], st.landed())
                if st.reused:
                    pe.wait_ge(weighed, st.before())
                    pe.wait_ge(logits_out, st.before())
                for t in range(TE):
                    nc.tensor.matmul(ps_w(k)[:, t, 0:D + H0], x_t[:, k, (TE + t) * P:(TE + t + 1) * P], w0[:],
                                     start=True, stop=False)
                    nc.tensor.matmul(ps_w(k)[:, t, D:D + H0], x_t[:, k, t * P:(t + 1) * P], wi[:],
                                     start=False, stop=False)
                    mm = nc.tensor.matmul(ps_w(k)[:, t, D:D + H0], attr[:, k, t * P:(t + 1) * P], ae[:],
                                          start=False, stop=True)
                mm.then_inc(projected, 1)

            def merge(st):
                k = st.slot
                pe.wait_ge(weighed, st.done())
                pe.wait_ge(matched, st.done(TE))
                if st.reused:
                    pe.wait_ge(summed, st.before())
                for t in range(TE):
                    mm = nc.tensor.matmul(ps_m(k)[:, t], match[:, k, t], msg[:, k, t], start=True, stop=True)
                mm.then_inc(merged, 1)

            run_steps(pe, steps, [(0, turn), (-1, merge), (0, project)])


def l0_node_phase(core, w, steps, x, table, x1_table, h_table):
    nc, psum = core.nc, core.psum
    ident, wemb = core.sb("ident", [P, P]), core.sb("wemb", [P, D])
    node = lambda name: core.sb(name, [P, 2, TN, D])
    o_in, x_in, low, e_low, high = node("n_a"), node("n_b"), node("n_c"), node("n_d"), node("n_e")
    x1, n1, n1t, h_out, lift = node("n_f"), node("n_g"), node("n_h"), node("n_i"), node("n_j")
    stats, mv = core.sb("n_stats", [P, TN, 6]), core.sb("n_mv", [P, 2, TN, 2])
    guess, rs = core.sb("n_guess", [P, TN]), core.sb("n_rs", [P, TN])
    ps_t = lambda k: psum[:, k].rearrange("p (t n) -> p t n", t=TN)
    ps_h = lambda k: psum[:, 2 + k].rearrange("p (t n) -> p t n", t=TN)
    per_step = lambda t: t[0:steps * TN * P, :].rearrange("(s p j) d -> s p j d", p=P, j=TN)

    o_landed, x_landed = core.sems("n0_o_landed"), core.sems("n0_x_landed")
    x1_stored, h_stored = core.sems("n0_x1_stored"), core.sems("n0_h_stored")
    lowed, lifted, highed, exped, x1_made, stated, aggregated, normed, turned, relued, embedded, h_made = (
        core.sem("n0_" + n) for n in ("lowed", "lifted", "highed", "exped", "x1_made", "stated", "aggregated",
                                      "normed", "turned", "relued", "embedded", "h_made"))

    with nc.Block() as block:
        @block.sync
        def _(sp):
            def load(st):
                k = st.slot
                if st.reused:
                    before, = held(core, sp, st.before())
                    sp.wait_ge(highed, before)
                    sp.wait_ge(lowed, before)
                    sp.wait_ge(lifted, before)
                sp.dma_start(o_in[:, k], per_step(table)[st.index]).then_inc(o_landed[k], 16)
                sp.dma_start(x_in[:, k], per_step(x)[st.index]).then_inc(x_landed[k], 16)

            def store(st):
                k = st.slot
                ready, = held(core, sp, st.done())
                sp.wait_ge(x1_made, ready)
                sp.dma_start(per_step(x1_table)[st.index], x1[:, k]).then_inc(x1_stored[k], 16)

            def store_h(st):
                k = st.slot
                ready, = held(core, sp, st.done())
                sp.wait_ge(h_made, ready)
                sp.dma_start(per_step(h_table)[st.index], h_out[:, k]).then_inc(h_stored[k], 16)

            run_steps(sp, steps, [(0, store), (4, load), (-3, store_h)])
            end = last_step(steps, 0)
            for k in range(2):
                sp.wait_ge(x1_stored[k], end.landed())
                sp.wait_ge(h_stored[k], end.landed())

        @block.vector
        def _(dve):
            def statistics(st):
                k = st.slot
                dve.wait_ge(exped, st.done())
                dve.wait_ge(highed, st.done())
                if st.reused:
                    dve.wait_ge(normed, st.before(TN))
                    dve.wait_ge(x1_stored[k], st.landed_before())
                nc.vector.scalar_tensor_tensor(out=x1[:, k], in0=e_low[:, k], scalar=-1.0, in1=high[:, k],
                                               op0=ALU.add, op1=ALU.add).then_inc(x1_made, 1)
                dve.wait_ge(x1_made, st.done())
                for j in range(TN):
                    nc.vector.bn_stats(stats[:, j], x1[:, k, j]).then_inc(stated, 1)
                all_stated, = held(core, dve, st.done(TN))
                dve.wait_ge(stated, all_stated)
                for j in range(TN):
                    nc.vector.bn_aggr(mv[:, k, j], stats[:, j]).then_inc(aggregated, 1)

            def normalise(st):
                k = st.slot
                dve.wait_ge(aggregated, st.done(TN))
                refine_root(core, nc, dve, st, "n0", mv[:, k, :, 1], guess, rs)
                if st.reused:
                    dve.wait_ge(turned, st.before())
                for j in range(TN):
                    nc.vector.tensor_scalar(n1[:, k, j], x1[:, k, j], mv[:, k, j, 0:1], rs[:, j:j + 1],
                                            ALU.subtract, ALU.mult).then_inc(normed, 1)

            run_steps(dve, steps, [(0, statistics), (-1, normalise)])

        @block.gpsimd
        def _(pool):
            def residual(st):
                k = st.slot
                pool.wait_ge(lifted, st.done())
                pool.wait_ge(x_landed[k], st.landed())
                if st.reused:
                    pool.wait_ge(x1_made, st.before())
                nc.gpsimd.tensor_tensor(high[:, k], lift[:, k], x_in[:, k], ALU.add).then_inc(highed, 1)

            run_steps(pool, steps, [(2, residual)])

        @block.scalar
        def _(act):
            act.preload_act_table_set(EXP_AND_LN)

            def split(st):
                k = st.slot
                act.wait_ge(o_landed[k], st.landed())
                if st.reused:
                    act.wait_ge(exped, st.before())
                    act.wait_ge(highed, st.before())
                nc.scalar.activation(low[:, k], o_in[:, k], ACT.Relu, scale=-1.0).then_inc(lowed, 1)
                nc.scalar.activation(lift[:, k], o_in[:, k], ACT.Relu).then_inc(lifted, 1)
                act.wait_ge(lowed, st.done())
                if st.reused:
                    act.wait_ge(x1_made, st.before())
                nc.scalar.activation(e_low[:, k], low[:, k], ACT.Exp, scale=-1.0).then_inc(exped, 1)

            def root(st):
                act.wait_ge(aggregated, st.done(TN))
                guess_root(core, nc, act, st, "n0", mv[:, st.slot, :, 1], guess)

            def relu_turned(st):
                act.wait_ge(turned, st.done())
                if st.reused:
                    act.wait_ge(embedded, st.before())
                nc.scalar.activation(n1t[:, st.slot], ps_t(st.slot), ACT.Relu).then_inc(relued, 1)

            def h_ready(st):
                act.wait_ge(embedded, st.done())
                if st.reused:
                    act.wait_ge(h_stored[st.slot], st.landed_before())
                nc.scalar.copy(h_out[:, st.slot], ps_h(st.slot)).then_inc(h_made, 1)

            run_steps(act, steps, [(0, root), (2, split), (-1, relu_turned), (-2, h_ready)])

        @block.tensor
        def _(pe):
            def turn(st):
                k = st.slot
                pe.wait_ge(normed, st.done(TN))
                if st.reused:
                    pe.wait_ge(relued, st.before())
                for j in range(TN):
                    mm = nc.tensor.transpose(ps_t(k)[:, j], n1[:, k, j], ident[:])
                mm.then_inc(turned, 1)

            def embed(st):
                k = st.slot
                pe.wait_ge(relued, st.done())
                if st.reused:
                    pe.wait_ge(h_made, st.before())
                for j in range(TN):
                    mm = nc.tensor.matmul(ps_h(k)[:, j], n1t[:, k, j], wemb[:], start=True, stop=True)
                mm.then_inc(embedded, 1)

            run_steps(pe, steps, [(-1, turn), (-2, embed)])


def l1_edge_phase(core, w, steps, layer, h_table, table, to_zero):
    nc, psum = core.nc, core.psum
    ident, ones = core.sb("ident", [P, P]), core.sb("ones", [P, P], BF16)
    wkvq = core.sb("wkvq", [P, LAYERS, 3 * D])[:, layer]
    bias = core.sb("bias_b", [P, LAYERS * 5 * D], BF16)[:].rearrange("p (l n) -> p l n", l=LAYERS)[:, layer]
    ends, ids = core.sb("ends", [P, TURN, 2 * TE], I32), core.sb("ids", [P, 2, TE])
    equal_rows = core.sb("equal_rows", [P, 2, TE * P], I32)
    h_in, h_t = core.sb("rows_in", [P, TURN, 2 * TE, D]), core.sb("rows_t", [P, 2, 2 * TE * P])
    match = core.sb("match", [P, 2, TE, P])
    target = core.sb("target", [P, 2, TE], I32)
    q, prod = core.sb("q", [P, 2, TE, D]), core.sb("prod", [P, TE, D])
    score, clipped = core.sb("score", [P, TE, H1]), core.sb("clipped", [P, 2, TE, H1])
    msg, sums = core.sb("msg1", [P, 2, TE, MW]), core.sb("sums1", [P, 2, TE, MW])

    ps_t = lambda k: psum[:, k]
    ps_kv = lambda k: psum[:, 2 + k].rearrange("p (t n) -> p t n", t=TE)
    ps_q = lambda k: psum[:, 4 + k, 0:TE * D].rearrange("p (t n) -> p t n", t=TE)
    ps_m = lambda k: psum[:, 6 + k, 0:TE * MW].rearrange("p (t n) -> p t n", t=TE)

    ends_landed, rows_landed = core.place_sems("e1_ends_landed"), core.sems("e1_rows_landed")
    gathered, added = core.place_sems("e1_gathered"), core.sems("e1_added")
    (cast, turned, turned_out, queried, projected, q_out, matched, picked, multiplied, scored, clip_done, exped, weighed,
     merged, summed) = (core.sem("e1_" + n) for n in
                        ("cast", "turned", "turned_out", "queried", "projected", "q_out", "matched", "picked",
                         "multiplied", "scored", "clipped", "exped", "weighed", "merged", "summed"))

    with nc.Block() as block:
        @block.sync
        def _(sp):
            zeroed = core.sem(f"zeroed_{layer + 2}")

            def load(st):
                if st.place_reused:
                    used, previous = held(core, sp, st.place_landed_before(16 * 2 * TE), st.turn_before())
                    sp.wait_ge(gathered[st.place], used)
                    sp.wait_ge(cast, previous)
                sp.dma_start(ends[:, st.place], w["ends"][st.index]).then_inc(ends_landed[st.place], 16)

            def load_rows(st):
                k = st.slot
                if st.reused:
                    before, = held(core, sp, st.before(TE))
                    sp.wait_ge(matched, before)
                sp.dma_start(equal_rows[:, k], w["dst_rows"][st.index].partition_broadcast(P)).then_inc(rows_landed[k], 16)

            def zero(st):
                sp.dma_start(to_zero[st.index], core.sb("zeros", [P, to_zero.shape[-1]])[:]).then_inc(zeroed, 16)

            run_steps(sp, steps, [(2, load), (0, load_rows)] + [(0, zero)] * (to_zero is not None), layer)

        @block.gpsimd
        def _(pool):
            gather_and_add(core, nc, pool, steps, layer, "e1", 3, h_table, table,
                           core.sem(f"zeroed_{layer + 1}"), steps, ends, h_in, ("e1_turned", 1),
                           sums, target)

        @block.vector
        def _(dve):
            def message(st):
                k = st.slot
                dve.wait_ge(ends_landed[st.place], st.place_landed())
                if st.reused:
                    dve.wait_ge(picked, st.before())
                nc.vector.tensor_copy(ids[:, k], ends[:, st.place, TE:]).then_inc(cast, 1)
                dve.wait_ge(cast, st.done())
                dve.wait_ge(rows_landed[k], st.landed())
                if st.reused:
                    dve.wait_ge(merged, st.before())
                match_edges(core, nc, dve, st, "e1", ids, equal_rows, match)
                dve.wait_ge(q_out, st.done())
                dve.wait_ge(projected, st.done())
                nc.vector.tensor_tensor(prod[:], ps_kv(k)[:, :, 0:D], q[:, k], ALU.mult).then_inc(multiplied, 1)
                dve.wait_ge(multiplied, st.done())
                nc.vector.tensor_reduce(score[:], prod[:].rearrange("p t (h d) -> p t h d", h=H1), AX.X,
                                        ALU.add).then_inc(scored, 1)
                dve.wait_ge(scored, st.done())
                nc.vector.tensor_scalar(clipped[:, k], score[:], CLIP * SCALE, -CLIP * SCALE, ALU.min,
                                        ALU.max).then_inc(clip_done, 1)
                dve.wait_ge(exped, st.done())
                nc.vector.tensor_tensor(msg[:, k, :, 0:D].rearrange("p t (h d) -> p t h d", h=H1),
                                        ps_kv(k)[:, :, D:].rearrange("p t (h d) -> p t h d", h=H1),
                                        over_lanes(msg[:, k, :, D:], D1), ALU.mult).then_inc(weighed, 1)
                pick_targets(core, nc, dve, st, "e1", ids, match, target)

            run_steps(dve, steps, [(0, message)], layer)

        @block.scalar
        def _(act):
            def turned_to_sbuf(st):
                act.wait_ge(turned, st.done())
                if st.reused:
                    act.wait_ge(projected, st.before())
                nc.scalar.copy(h_t[:, st.slot], ps_t(st.slot)).then_inc(turned_out, 1)

            def q_to_sbuf(st):
                act.wait_ge(queried, st.done())
                if st.reused:
                    act.wait_ge(multiplied, st.before())
                nc.scalar.copy(q[:, st.slot], ps_q(st.slot)).then_inc(q_out, 1)

            def exp(st):
                act.wait_ge(clip_done, st.done())
                if st.reused:
                    act.wait_ge(merged, st.before())
                nc.scalar.activation(msg[:, st.slot, :, D:], clipped[:, st.slot], ACT.Exp,
                                     scale=1.0 / SCALE).then_inc(exped, 1)

            def sums_out(st):
                act.wait_ge(merged, st.done())
                if st.reused:
                    act.wait_ge(added[st.slot], st.landed_before(16 * TE))
                nc.scalar.copy(sums[:, st.slot], ps_m(st.slot)).then_inc(summed, 1)

            run_steps(act, steps, [(0, turned_to_sbuf), (0, q_to_sbuf), (0, exp), (-1, sums_out)], layer)

        @block.tensor
        def _(pe):
            def turn(st):
                k = st.slot
                pe.wait_ge(gathered[st.place], st.place_landed(16 * 2 * TE))
                if st.reused:
                    pe.wait_ge(turned_out, st.before())
                for c in range(2 * TE):
                    mm = nc.tensor.transpose(ps_t(k)[:, c * P:(c + 1) * P], h_in[:, st.place, c], ident[:])
                mm.then_inc(turned, 1)

            def merge(st):
                k = st.slot
                pe.wait_ge(weighed, st.done())
                pe.wait_ge(matched, st.done(TE))
                pe.wait_ge(exped, st.done())
                if st.reused:
                    pe.wait_ge(summed, st.before())
                for t in range(TE):
                    mm = nc.tensor.matmul(ps_m(k)[:, t], match[:, k, t], msg[:, k, t], start=True, stop=True)
                mm.then_inc(merged, 1)

            def project(st):
                k = st.slot
                pe.wait_ge(turned_out, st.done())
                if st.reused:
                    pe.wait_ge(weighed, st.before())
                    pe.wait_ge(q_out, st.before())
                nc.tensor.matmul(ps_q(k), ones[:], over_tiles(bias[:, 2 * D:3 * D], TE), start=True, stop=False)
                for t in range(TE):
                    mm = nc.tensor.matmul(ps_q(k)[:, t], h_t[:, k, (TE + t) * P:(TE + t + 1) * P], wkvq[:, 2 * D:],
                                          start=False, stop=(t == TE - 1))
                mm.then_inc(queried, 1)
                nc.tensor.matmul(ps_kv(k), ones[:], over_tiles(bias[:, 0:2 * D], TE), start=True, stop=False)
                for t in range(TE):
                    mm = nc.tensor.matmul(ps_kv(k)[:, t], h_t[:, k, t * P:(t + 1) * P], wkvq[:, 0:2 * D],
                                          start=False, stop=(t == TE - 1))
                mm.then_inc(projected, 1)

            run_steps(pe, steps, [(0, turn), (0, project), (-1, merge)], layer)


def l1_node_phase(core, w, steps, layer, table, h_table, x1_table, out):
    nc, psum = core.nc, core.psum
    ident, eps, ones = core.sb("ident", [P, P]), core.sb("ln_eps", [P, 1]), core.sb("ones", [P, P], BF16)
    wo = core.sb("wo", [P, LAYERS, D])[:, layer]
    w1 = core.sb("w1", [P, LAYERS, 2 * D])[:, layer]
    w2 = core.sb("w2", [P, LAYERS, 2, D])[:, layer]
    b1col = core.sb("b1_col", [P, LAYERS, 2])[:, layer]
    g1rows, g2rows, b2rows = (core.sb(f"{n}_rows", [P, LAYERS, D])[:, layer] for n in ("ln1_g", "ln2_g", "ln2_b"))
    bias = core.sb("bias_b", [P, LAYERS * 5 * D], BF16)[:].rearrange("p (l n) -> p l n", l=LAYERS)[:, layer]
    last = layer == LAYERS - 1

    node = lambda name: core.sb(name, [P, 2, TN, D])
    h_in, att, att_t, r1, n1, n1t = node("n_a"), node("n_b"), node("n_c"), node("n_d"), node("n_e"), node("n_f")
    n2, h_out, x1_in, h1, r2 = node("n_g"), node("n_h"), node("n_i"), node("n_j"), node("n_k")
    agg = core.sb("agg", [P, 2, TN, MW])
    hidden = core.sb("hidden", [P, 2, 2, TN * P])
    z = core.sb("z", [P, TN, H1])
    rz = core.sb("rz", [P, 2, TN, H1])
    stats, mv = core.sb("n_stats", [P, TN, 6]), core.sb("n_mv", [P, 2, TN, 2])
    sd, rs = core.sb("n_sd", [P, TN]), core.sb("n_rs", [P, TN])
    stats2, mv2 = core.sb("n_stats2", [P, TN, 6]), core.sb("n_mv2", [P, 2, TN, 2])
    sd2, rs2, shift2 = core.sb("n_sd2", [P, TN]), core.sb("n_rs2", [P, 2, TN]), core.sb("n_shift2", [P, 2, TN])

    by_tile = lambda b: psum[:, b].rearrange("p (t n) -> p t n", t=TN)
    ps_at = by_tile(0)
    ps_nt = by_tile(1)
    ps_o = lambda k: by_tile(2 + k)
    ps_h = lambda c: psum[:, 4 + c]
    ps_f = lambda k: by_tile(6 + k)
    per_step = lambda t: t[0:steps * TN * P, :].rearrange("(s p j) d -> s p j d", p=P, j=TN)

    agg_landed, h_landed, x1_landed = core.sems("n1_agg_landed"), core.sems("n1_h_landed"), core.sems("n1_x1_landed")
    stored = core.sems("n1_stored")
    (z_made, rz_made, att_made, att_turned, att_out, o_made, r_made, stated, aggregated, rooted, inverted, normed,
     n1_turned, n1_out, up, relued, ffn_made, carried, r2_made, stated2, aggregated2, rooted2, inverted2, shifted2, normed2, scaled,
     h_made) = (core.sem("n1_" + n) for n in
                ("z_made", "rz_made", "att_made", "att_turned", "att_out", "o_made", "r_made", "stated",
                 "aggregated", "rooted", "inverted", "normed", "n1_turned", "n1_out", "up", "relued", "ffn_made",
                 "carried", "r2_made", "stated2", "aggregated2", "rooted2", "inverted2", "shifted2", "normed2", "scaled", "h_made"))

    with nc.Block() as block:
        @block.sync
        def _(sp):
            def load(st):
                k = st.slot
                if st.reused:
                    before, = held(core, sp, st.before())
                    sp.wait_ge(att_made, before)
                sp.dma_start(agg[:, k], per_step(table)[st.index]).then_inc(agg_landed[k], 16)

            def load_h(st):
                k = st.slot
                if st.reused:
                    before, = held(core, sp, st.before())
                    sp.wait_ge(r_made, before)
                sp.dma_start(h_in[:, k], per_step(h_table)[st.index]).then_inc(h_landed[k], 16)

            def store(st):
                k = st.slot
                ready, = held(core, sp, st.done())
                sp.wait_ge(h_made, ready)
                if not last:
                    sp.dma_start(per_step(h_table)[st.index], h_out[:, k]).then_inc(stored[k], 16)
                elif isinstance(st.index, int) and (st.index + 1) * TN * P > out.shape[0]:
                    rows = out.shape[0] - st.index * TN * P
                    sp.dma_start(out[st.index * TN * P:, :].rearrange("(p j) d -> p j d", j=TN),
                                 h_out[0:rows // TN, k]).then_inc(stored[k], 16)
                else:
                    whole = out[0:out.shape[0] // (TN * P) * (TN * P), :]
                    sp.dma_start(whole.rearrange("(s p j) d -> s p j d", p=P, j=TN)[st.index],
                                 h_out[:, k]).then_inc(stored[k], 16)

            def load_x1(st):
                k = st.slot
                if not (isinstance(st.pair, int) and st.pair == 0):
                    before, = held(core, sp, st.before())
                    sp.wait_ge(h_made, before)
                sp.dma_start(x1_in[:, k], per_step(x1_table)[st.index]).then_inc(x1_landed[k], 16)

            run_steps(sp, steps, [(3, load), (2, load_h), (-4, store)] + [(-2, load_x1)] * last, layer)
            end = last_step(steps, layer)
            for k in range(2):
                sp.wait_ge(stored[k], end.landed())

        @block.gpsimd
        def _(pool):
            def attend(st):
                k = st.slot
                pool.wait_ge(agg_landed[k], st.landed())
                pool.wait_ge(rz_made, st.done())
                if st.reused:
                    pool.wait_ge(att_turned, st.before())
                nc.gpsimd.tensor_tensor(att[:, k].rearrange("p j (h d) -> p j h d", h=H1),
                                        agg[:, k, :, 0:D].rearrange("p j (h d) -> p j h d", h=H1),
                                        over_lanes(rz[:, k], D1), ALU.mult).then_inc(att_made, 1)

            def carry(st):
                k = st.slot
                pool.wait_ge(normed, st.done(TN))
                if st.reused:
                    pool.wait_ge(r2_made, st.before())
                nc.gpsimd.tensor_tensor(h1[:, k], n1[:, k], over_tiles(g1rows, TN), ALU.mult).then_inc(carried, 1)

            def finish(st):
                k = st.slot
                pool.wait_ge(normed2, st.done(TN))
                if st.reused:
                    pool.wait_ge(stored[k], st.landed_before())
                nc.gpsimd.tensor_tensor(h_out[:, k], n2[:, k], over_tiles(g2rows, TN), ALU.mult).then_inc(scaled, 1)
                pool.wait_ge(scaled, st.done())
                nc.gpsimd.tensor_tensor(h_out[:, k], h_out[:, k], over_tiles(b2rows, TN), ALU.add).then_inc(
                    scaled if last else h_made, 1)

            def finish_last(st):
                k = st.slot
                pool.wait_ge(normed2, st.done(TN))
                if st.reused:
                    pool.wait_ge(stored[k], st.landed_before())
                base = st.index * 2 + layer * steps
                nc.gpsimd.tensor_tensor(h_out[:, k], n2[:, k], over_tiles(g2rows, TN), ALU.mult).then_inc(scaled, 1)
                pool.wait_ge(scaled, base + 1)
                nc.gpsimd.tensor_tensor(h_out[:, k], h_out[:, k], over_tiles(b2rows, TN), ALU.add).then_inc(scaled, 1)
                pool.wait_ge(scaled, base + 2)
                pool.wait_ge(x1_landed[k], (st.pair + 1) * 16)
                nc.gpsimd.tensor_tensor(h_out[:, k], h_out[:, k], x1_in[:, k], ALU.add).then_inc(h_made, 1)

            run_steps(pool, steps, [(-1, carry), (2, attend), (-3, finish_last if last else finish)], layer)

        @block.vector
        def _(dve):
            def weights_inverse(st):
                k = st.slot
                dve.wait_ge(agg_landed[k], st.landed())
                nc.vector.tensor_scalar(z[:], agg[:, k, :, D:], Z_EPS, None, ALU.add).then_inc(z_made, 1)
                dve.wait_ge(z_made, st.done())
                if st.reused:
                    dve.wait_ge(att_made, st.before())
                nc.vector.reciprocal(rz[:, k], z[:]).then_inc(rz_made, 1)
                dve.wait_ge(rz_made, st.done())

            def residual(st):
                k = st.slot
                dve.wait_ge(o_made, st.done())
                dve.wait_ge(h_landed[k], st.landed())
                if st.reused:
                    dve.wait_ge(normed, st.before(TN))
                nc.vector.tensor_tensor(r1[:, k], ps_o(k), h_in[:, k], ALU.add).then_inc(r_made, 1)
                dve.wait_ge(r_made, st.done())
                for j in range(TN):
                    nc.vector.bn_stats(stats[:, j], r1[:, k, j]).then_inc(stated, 1)
                all_stated, = held(core, dve, st.done(TN))
                dve.wait_ge(stated, all_stated)
                for j in range(TN):
                    nc.vector.bn_aggr(mv[:, k, j], stats[:, j]).then_inc(aggregated, 1)

            def normalise(st):
                k = st.slot
                dve.wait_ge(aggregated, st.done(TN))
                dve.wait_ge(rooted, st.done())
                nc.vector.reciprocal(rs[:], sd[:]).then_inc(inverted, 1)
                dve.wait_ge(inverted, st.done())
                if st.reused:
                    dve.wait_ge(n1_turned, st.before())
                    dve.wait_ge(carried, st.before())
                for j in range(TN):
                    nc.vector.tensor_scalar(n1[:, k, j], r1[:, k, j], mv[:, k, j, 0:1], rs[:, j:j + 1],
                                            ALU.subtract, ALU.mult).then_inc(normed, 1)

            def statistics2(st):
                k = st.slot
                dve.wait_ge(ffn_made, st.done())
                dve.wait_ge(carried, st.done())
                if st.reused:
                    dve.wait_ge(normed2, st.before(TN))
                nc.vector.tensor_tensor(r2[:, k], ps_f(k), h1[:, k], ALU.add).then_inc(r2_made, 1)
                dve.wait_ge(r2_made, st.done())
                for j in range(TN):
                    nc.vector.bn_stats(stats2[:, j], r2[:, k, j]).then_inc(stated2, 1)
                if st.reused:
                    all_stated, used = held(core, dve, st.done(TN), st.before())
                    dve.wait_ge(shifted2, used)
                else:
                    all_stated, = held(core, dve, st.done(TN))
                dve.wait_ge(stated2, all_stated)
                for j in range(TN):
                    nc.vector.bn_aggr(mv2[:, k, j], stats2[:, j]).then_inc(aggregated2, 1)

            def shift(st):
                k = st.slot
                dve.wait_ge(aggregated2, st.done(TN))
                dve.wait_ge(rooted2, st.done())
                if st.reused:
                    dve.wait_ge(normed2, st.before(TN))
                nc.vector.reciprocal(rs2[:, k], sd2[:]).then_inc(inverted2, 1)
                dve.wait_ge(inverted2, st.done())
                nc.vector.scalar_tensor_tensor(out=shift2[:, k], in0=mv2[:, k, :, 0], scalar=-1.0, in1=rs2[:, k],
                                               op0=ALU.mult, op1=ALU.mult).then_inc(shifted2, 1)

            run_steps(dve, steps, [(0, residual), (2, weights_inverse), (-3, shift), (0, normalise), (-2, statistics2)],
                      layer)

        @block.scalar
        def _(act):
            def n1_to_sbuf(st):
                act.wait_ge(n1_turned, st.done())
                if st.reused:
                    act.wait_ge(up, st.before())
                nc.scalar.copy(n1t[:, st.slot], ps_nt).then_inc(n1_out, 1)

            def att_to_sbuf(st):
                act.wait_ge(att_turned, st.done())
                if st.reused:
                    act.wait_ge(o_made, st.before())
                nc.scalar.copy(att_t[:, st.slot], ps_at).then_inc(att_out, 1)

            def root(st):
                act.wait_ge(aggregated, st.done(TN))
                if st.reused:
                    act.wait_ge(inverted, st.done() - 1)
                nc.scalar.activation(sd[:], mv[:, st.slot, :, 1], ACT.Sqrt, bias=eps[:, 0:1]).then_inc(rooted, 1)

            def relu(st):
                act.wait_ge(up, st.done())
                if st.reused:
                    act.wait_ge(ffn_made, st.before())
                for c in range(2):
                    nc.scalar.activation(hidden[:, st.slot, c], ps_h(c), ACT.Relu,
                                         bias=b1col[:, c:c + 1]).then_inc(relued, 1)

            def root2(st):
                act.wait_ge(aggregated2, st.done(TN))
                if st.reused:
                    act.wait_ge(inverted2, st.done() - 1)
                nc.scalar.activation(sd2[:], mv2[:, st.slot, :, 1], ACT.Sqrt, bias=eps[:, 0:1]).then_inc(rooted2, 1)

            def normalise2(st):
                k = st.slot
                act.wait_ge(shifted2, st.done())
                if st.reused:
                    act.wait_ge(h_made, st.before())
                for j in range(TN):
                    nc.scalar.activation(n2[:, k, j], r2[:, k, j], ACT.Identity, bias=shift2[:, k, j:j + 1],
                                         scale=rs2[:, k, j:j + 1]).then_inc(normed2, 1)

            run_steps(act, steps, [(-2, relu), (-1, n1_to_sbuf), (1, att_to_sbuf), (-3, root2), (0, root),
                                   (-3, normalise2)], layer)

        @block.tensor
        def _(pe):
            def turn_n1(st):
                pe.wait_ge(normed, st.done(TN))
                if st.reused:
                    pe.wait_ge(n1_out, st.done() - 1)
                for j in range(TN):
                    mm = nc.tensor.transpose(ps_nt[:, j], n1[:, st.slot, j], ident[:])
                mm.then_inc(n1_turned, 1)

            def turn_att(st):
                pe.wait_ge(att_made, st.done())
                if st.reused:
                    pe.wait_ge(att_out, st.done() - 1)
                for j in range(TN):
                    mm = nc.tensor.transpose(ps_at[:, j], att[:, st.slot, j], ident[:])
                mm.then_inc(att_turned, 1)

            def output(st):
                k = st.slot
                pe.wait_ge(att_out, st.done())
                if st.reused:
                    pe.wait_ge(r_made, st.before())
                nc.tensor.matmul(ps_o(k), ones[:], over_tiles(bias[:, 3 * D:4 * D], TN), start=True, stop=False)
                for j in range(TN):
                    mm = nc.tensor.matmul(ps_o(k)[:, j], att_t[:, k, j], wo, start=False, stop=(j == TN - 1))
                mm.then_inc(o_made, 1)

            def widen(st):
                k = st.slot
                pe.wait_ge(n1_out, st.done())
                if st.reused:
                    pe.wait_ge(relued, (st.done() - 1) * 2)
                for c in range(2):
                    mm = nc.tensor.matmul(ps_h(c), w1[:, c * D:(c + 1) * D], n1t[:, k].rearrange("p j n -> p (j n)"),
                                          start=True, stop=True)
                mm.then_inc(up, 1)

            def narrow(st):
                k = st.slot
                pe.wait_ge(relued, st.done(2))
                if st.reused:
                    pe.wait_ge(r2_made, st.before())
                nc.tensor.matmul(ps_f(k), ones[:], over_tiles(bias[:, 4 * D:], TN), start=True, stop=False)
                for j in range(TN):
                    for c in range(2):
                        mm = nc.tensor.matmul(ps_f(k)[:, j], hidden[:, k, c, j * P:(j + 1) * P], w2[:, c],
                                              start=False, stop=(c == 1 and j == TN - 1))
                mm.then_inc(ffn_made, 1)

            run_steps(pe, steps, [(0, output), (-1, turn_n1), (1, turn_att), (-2, narrow), (-1, widen)], layer)


def build(nc, w, out):
    node_rows = w["x"].shape[0]
    node_steps, edge_steps = node_rows // (TN * P), w["ends"].shape[0]
    assert node_steps % 2 == 0 and edge_steps % 2 == 0
    scratch = lambda name, rows, cols: nc.dram_tensor(name, (rows, cols), F32).ap()
    sums0 = scratch("l0_sums", node_rows + P, D)
    zero_width = -(-(node_rows + P) * MW // (P * edge_steps))
    flat1 = [nc.dram_tensor(f"l1_sums_{l}", (edge_steps * P * zero_width,), F32).ap() for l in range(LAYERS)]
    sums1 = [t[0:(node_rows + P) * MW].rearrange("(r d) -> r d", d=MW) for t in flat1]
    to_zero = [t.rearrange("(s p n) -> s p n", p=P, n=zero_width) for t in flat1] + [None]
    x1_table, h_table = scratch("x1_table", node_rows, D), scratch("h_table", node_rows, D)
    with ExitStack() as ctx:
        core = Core(nc, ctx)
        core.psum = ctx.enter_context(nc.psum_tensor("psum", [P, 8, 512], F32))
        setup_phase(core, w, sums0, node_rows, zero_width)
        l0_edge_phase(core, w, edge_steps, w["x"], sums0, to_zero[0])
        l0_node_phase(core, w, node_steps, w["x"], sums0, x1_table, h_table)
        for layer in range(LAYERS):
            l1_edge_phase(core, w, edge_steps, layer, h_table, sums1[layer], to_zero[layer + 1])
            l1_node_phase(core, w, node_steps, layer, sums1[layer], h_table, x1_table, out)


def kernel(**inputs):
    import numpy as _np
    import concourse.bacc as _bacc
    from concourse import mybir as _mybir
    from concourse.bass_utils import run_bass_kernel_spmd as _run

    a = {k: _np.asarray(v) for k, v in inputs.items()}
    nodes, edges = a["x"].shape[0], a["src"].shape[0]
    node_steps = -(-nodes // (TN * P * 2)) * 2
    edge_steps = -(-edges // (TE * P * 2)) * 2
    rows, slots = node_steps * TN * P, edge_steps * TE * P
    assert rows > nodes
    src = _np.full(slots, nodes, _np.int32)
    src[:edges] = a["src"]
    dst = _np.full(slots, nodes, _np.int32)
    dst[:edges] = a["dst"]
    x = _np.zeros((rows, D), _np.float32)
    x[:nodes] = a["x"]
    attr_t = _np.zeros((FE, slots), _np.float32)
    attr_t[:, :edges] = a["edge_attr_16"].T
    by_partition = lambda v: v.reshape(edge_steps, TE, P).transpose(0, 2, 1)
    arrays = {
        "x": x, "attr_T": attr_t,
        "ends": _np.concatenate([by_partition(src), by_partition(dst)], axis=2),
        "src_rows": src.reshape(edge_steps, TE * P), "dst_rows": dst.reshape(edge_steps, TE * P),
        "a_T": a["L0_gnn_a"].T, "ln1_g_T": a["L1_gnn_ln1_g"].T, "ln1_b_T": a["L1_gnn_ln1_b"].T,
        "b1_T": a["L1_gnn_b1"].reshape(LAYERS, 2, P).transpose(2, 0, 1).reshape(P, LAYERS * 2),
    }
    for name in ("L0_gnn_W", "L0_gnn_a", "L1_gnn_Wemb", "L1_gnn_Wq", "L1_gnn_bq", "L1_gnn_Wk", "L1_gnn_bk", "L1_gnn_Wv",
                 "L1_gnn_bv", "L1_gnn_Wo", "L1_gnn_bo", "L1_gnn_ln1_g", "L1_gnn_ln1_b", "L1_gnn_W1", "L1_gnn_W2", "L1_gnn_b2",
                 "L1_gnn_ln2_g", "L1_gnn_ln2_b"):
        arrays[name] = a[name]
    nc = _bacc.Bacc("TRN2", target_bir_lowering=False, num_devices=1)
    given, w = {}, {}
    for name, v in arrays.items():
        v = _np.ascontiguousarray(v)
        given[f"in_{name}"] = v
        w[name] = nc.dram_tensor(f"in_{name}", v.shape, _mybir.dt.from_np(v.dtype), kind="ExternalInput").ap()
    out = nc.dram_tensor("out", (nodes, D), _mybir.dt.float32, kind="ExternalOutput").ap()
    build(nc, w, out)
    r = _run(nc, [given], core_ids=[0])
    return r.results[0]["out"]
```

```python
from contextlib import ExitStack

import numpy as np
import concourse.bass as bass
from concourse import mybir

P = 128
TE = 2
TN = 4
TURN = 4
D = 128
H0, D0 = 4, 32
FE = 16
H1, D1 = 8, 16
MW = D + H1
LAYERS = 3
ALPHA = 0.2
LN_EPS = 1e-5
Z_EPS = 1e-6
CLIP = 5.0
EXP_AND_LN = "natural_log_exp_and_others"
SCALE = float(np.sqrt(D1))

ALU = mybir.AluOpType
ACT = mybir.ActivationFunctionType
AX = mybir.AxisListType
F32 = mybir.dt.float32
BF16 = mybir.dt.bfloat16
I32 = mybir.dt.int32
U32 = mybir.dt.uint32


class Step:

    def __init__(self, turn, place, steps, layer):
        self.turn, self.place, self.steps, self.layer = turn, place, steps, layer
        self.slot = place % 2
        self.pair = turn * 2 + place // 2
        self.index = turn * TURN + place
        self.reused = not (isinstance(turn, int) and turn == 0 and place < 2 and layer == 0)
        self.first = isinstance(turn, int) and turn == 0 and place == 0 and layer == 0
        self.place_reused = not (isinstance(turn, int) and turn == 0 and layer == 0)

    def done(self, n=1):
        return (self.index + (self.layer * self.steps + 1)) * n

    def before(self, n=1):
        return (self.index + (self.layer * self.steps - 1)) * n

    def landed(self, n=16):
        return (self.pair + (self.layer * self.steps // 2 + 1)) * n

    def landed_before(self, n=16):
        return (self.pair + self.layer * self.steps // 2) * n

    def landed_two_before(self, n=16):
        return self.landed_before(n) - n

    def turn_before(self, n=1):
        return self.before(n) - 2 * n

    def place_landed(self, n=16):
        return (self.turn + (self.layer * ((self.steps - self.place + TURN - 1) // TURN) + 1)) * n

    def place_landed_before(self, n=16):
        return (self.turn + self.layer * ((self.steps - self.place + TURN - 1) // TURN)) * n


def last_step(steps, layer):
    return Step((steps - 1) // TURN, (steps - 1) % TURN, steps, layer)


def run_steps(engine, steps, stages, layer=0):
    least, most = min(a for a, _ in stages), max(a for a, _ in stages)
    first, last = -most, steps - least
    start = -((least - TURN) // TURN) * TURN
    end = start + (steps - most - start) // TURN * TURN

    def plain(rounds):
        for r in rounds:
            for ahead, emit in stages:
                if 0 <= r + ahead < steps:
                    emit(Step((r + ahead) // TURN, (r + ahead) % TURN, steps, layer))

    if end - start < 2 * TURN:
        plain(range(first, last))
        return
    plain(range(first, start))
    with engine.Fori(start // TURN, end // TURN) as turn:
        for r in range(TURN):
            for ahead, emit in stages:
                emit(Step(turn + (r + ahead) // TURN, (r + ahead) % TURN, steps, layer))
    plain(range(end, last))


class Core:

    def __init__(self, nc, ctx):
        self.nc, self.ctx, self.kept = nc, ctx, {}

    def sb(self, name, shape, dt=F32):
        if name not in self.kept:
            self.kept[name] = self.ctx.enter_context(self.nc.sbuf_tensor(name, shape, dt))
        return self.kept[name]

    def sem(self, name):
        if name not in self.kept:
            self.kept[name] = self.ctx.enter_context(self.nc.semaphore(name))
        return self.kept[name]

    def count(self, engine, n, value):
        if isinstance(value, int):
            return value
        key = f"count_{engine.engine.name}_{n}"
        if key not in self.kept:
            self.kept[key] = engine.alloc_register(key)
        engine.reg_mov(self.kept[key], value)
        return self.kept[key]

    def sems(self, name):
        return [self.sem(f"{name}_{k}") for k in range(2)]

    def place_sems(self, name):
        return [self.sem(f"{name}_{k}") for k in range(TURN)]


def held(core, engine, *counts):
    kept = [core.count(engine, n, v) for n, v in enumerate(counts)]
    engine.wait_ge(core.sem("consts_made"), 5)
    return kept


def over_tiles(row, tiles):
    return row.unsqueeze(1).to_broadcast([P, tiles, row.shape[-1]])


def over_lanes(heads, width):
    return heads.unsqueeze(len(heads.shape)).to_broadcast([*heads.shape, width])


def setup_phase(core, w, trash_row, zero_width, zero_parts):
    nc = core.nc
    psum = core.psum
    loaded = core.sem("weights_loaded")
    pool_made, dve_made, pe_made = core.sem("consts_made"), core.sem("prep_dve"), core.sem("prep_pe")
    ident, later, trash_i = core.sb("ident", [P, P]), core.sb("later", [P, P]), core.sb("trash_i", [P, 1], I32)
    trash, eps, ones = core.sb("trash", [P, 1]), core.sb("ln_eps", [P, 1]), core.sb("ones", [P, P], BF16)
    w0, wi = core.sb("w0_ext", [P, D + H0]), core.sb("w0_src", [P, H0])
    a_rows = core.sb("a_rows", [P, H0, 2 * D0 + FE])
    ae, attr = core.sb("a_edge", [P, H0]), core.sb("attr", [P, 2, TE * P])
    aw = core.sb("a_times_w", [P, D])
    wemb = core.sb("wemb", [P, D])
    wkvq = core.sb("wkvq", [P, LAYERS, 3 * D])
    wo = core.sb("wo", [P, LAYERS, D])
    w1 = core.sb("w1", [P, LAYERS, 2 * D])
    w2 = core.sb("w2", [P, LAYERS, 2, D])
    g1col, b1lncol = core.sb("ln1_g_col", [P, LAYERS]), core.sb("ln1_b_col", [P, LAYERS])
    b1col = core.sb("b1_col", [P, LAYERS, 2])
    g1rows, g2rows, b2rows = (core.sb(f"{n}_rows", [P, LAYERS, D]) for n in ("ln1_g", "ln2_g", "ln2_b"))
    bo_cols, bo_rows = core.sb("bo_cols", [P, LAYERS, 3]), core.sb("bo_rows", [P, LAYERS, D])
    nb = 5 * D
    bias3 = core.sb("bias3", [3, LAYERS, nb])
    lnb3 = core.sb("lnb3", [3, LAYERS, D])
    part = core.sb("bias_part", [3, 3, LAYERS * nb], BF16)
    rest = core.sb("bias_rest", [3, LAYERS * nb])
    picked = core.sb("bias_picked", [3, LAYERS * nb])
    bias_b = core.sb("bias_b", [P, LAYERS * nb], BF16)
    zeros = core.sb("zeros", [P, zero_width])

    loads = [(w0[:, 0:D], w["L0_gnn_W"]), (wemb[:], w["L1_gnn_Wemb"]),
             (a_rows[:].rearrange("p h a -> p (h a)"), w["L0_gnn_a"].rearrange("h a -> (h a)").partition_broadcast(P)),
             (wkvq[:, :, 0:D], w["L1_gnn_Wk"].rearrange("l p n -> p l n")),
             (wkvq[:, :, D:2 * D], w["L1_gnn_Wv"].rearrange("l p n -> p l n")),
             (wkvq[:, :, 2 * D:], w["L1_gnn_Wq"].rearrange("l p n -> p l n")),
             (wo[:], w["L1_gnn_Wo"].rearrange("l p n -> p l n")),
             (w1[:], w["L1_gnn_W1"].rearrange("l p n -> p l n")),
             (g1col[:], w["ln1_g_T"]), (b1lncol[:], w["ln1_b_T"]), (b1col[:].rearrange("p l c -> p (l c)"), w["b1_T"]),
             (bo_cols[:], w["bo_T"]),
             (bo_rows[:].rearrange("p l n -> p (l n)"), w["L1_gnn_bo"].rearrange("l n -> (l n)").partition_broadcast(P)),
             (g1rows[:].rearrange("p l n -> p (l n)"), w["L1_gnn_ln1_g"].rearrange("l n -> (l n)").partition_broadcast(P)),
             (g2rows[:].rearrange("p l n -> p (l n)"), w["L1_gnn_ln2_g"].rearrange("l n -> (l n)").partition_broadcast(P)),
             (b2rows[:].rearrange("p l n -> p (l n)"), w["L1_gnn_ln2_b"].rearrange("l n -> (l n)").partition_broadcast(P)),
             (lnb3[:].rearrange("p l n -> p (l n)"), w["L1_gnn_ln1_b"].rearrange("l n -> (l n)").partition_broadcast(3))]
    loads += [(w2[:, l], w["L1_gnn_W2"][l].rearrange("(c p) n -> p c n", p=P)) for l in range(LAYERS)]
    loads += [(bias3[:, :, c * D:(c + 1) * D], w[f"L1_gnn_{b}"].partition_broadcast(3))
              for c, b in enumerate(("bk", "bv", "bq", "bo", "b2"))]

    with nc.Block() as block:
        @block.scalar
        def _(act):
            act.wait_ge(dve_made, 1)
            for c in range(zero_parts.shape[0]):
                act.dma_start(zero_parts[c], zeros[:, 0:zero_parts.shape[-1]]).then_inc(core.sem("zeroed_0"), 16)

        @block.sync
        def _(sp):
            for dst, src in loads:
                sp.dma_start(dst, src).then_inc(loaded, 16)
            sp.wait_ge(dve_made, 5)
            sp.dma_start(ae[0:FE, :], w["a_T"][2 * D0:, :]).then_inc(loaded, 16)

        @block.gpsimd
        def _(pool):
            nc.gpsimd.memset(ident[:], 0.0).then_inc(pool_made, 1)
            nc.gpsimd.memset(later[:], 1.0).then_inc(pool_made, 1)
            pool.wait_ge(pool_made, 2)
            nc.gpsimd.affine_select(out=ident[:], in_=ident[:], compare_op=ALU.not_equal, fill=1.0, base=0,
                                    pattern=[[-1, P]], channel_multiplier=1).then_inc(pool_made, 1)
            nc.gpsimd.affine_select(out=later[:], in_=later[:], compare_op=ALU.is_gt, fill=0.0, base=0,
                                    pattern=[[1, P]], channel_multiplier=-1).then_inc(pool_made, 1)
            nc.gpsimd.iota(trash_i[:], [[0, 1]], base=trash_row, channel_multiplier=1).then_inc(pool_made, 1)

        @block.vector
        def _(dve):
            made = [0]

            def then(instruction):
                instruction.then_inc(dve_made, 1)
                made[0] += 1
                dve.wait_ge(dve_made, made[0])

            then(nc.vector.memset(zeros[:], 0.0))
            then(nc.vector.memset(eps[:], LN_EPS))
            then(nc.vector.memset(ones[:], 1.0))
            then(nc.vector.memset(bias_b[:], 0.0))
            then(nc.vector.memset(ae[:], 0.0))
            then(nc.vector.memset(attr[:], 0.0))
            dve.wait_ge(pool_made, 5)
            then(nc.vector.tensor_copy(trash[:], trash_i[:]))
            dve.wait_ge(loaded, 16 * (len(loads) + 1))
            w_heads = w0[:, 0:D].rearrange("p (h d) -> p h d", h=H0)
            for out, lo in ((wi[:], 0), (w0[:, D:D + H0], D0)):
                then(nc.vector.tensor_tensor(aw[:].rearrange("p (h d) -> p h d", h=H0), w_heads,
                                             a_rows[:, :, lo:lo + D0], ALU.mult))
                then(nc.vector.tensor_reduce(out, aw[:].rearrange("p (h d) -> p h d", h=H0), AX.X, ALU.add))
            then(nc.vector.tensor_tensor(bias3[:, :, 4 * D:], bias3[:, :, 4 * D:], lnb3[:], ALU.add))
            dve.wait_ge(pe_made, 1)
            for l in range(LAYERS):
                then(nc.vector.tensor_tensor(bias3[:, l, 0:3 * D], bias3[:, l, 0:3 * D], psum[0:3, 1 + l, 0:3 * D],
                                             ALU.subtract))
            for l in range(LAYERS - 1):
                then(nc.vector.tensor_tensor(b2rows[:, l], b2rows[:, l], bo_rows[:, l + 1], ALU.add))
            flat = bias3[:].rearrange("p l n -> p (l n)")
            then(nc.vector.tensor_copy(rest[:], flat))
            for c in range(3):
                then(nc.vector.tensor_copy(part[:, c], rest[:]))
                then(nc.vector.tensor_tensor(rest[:], rest[:], part[:, c], ALU.subtract))
            then(nc.vector.tensor_scalar(picked[:], part[:, 0], ident[0:3, 0:1], None, ALU.mult))
            for c in range(1, 3):
                then(nc.vector.scalar_tensor_tensor(out=picked[:], in0=part[:, c], scalar=ident[0:3, c:c + 1],
                                                    in1=picked[:], op0=ALU.mult, op1=ALU.add))
            then(nc.vector.tensor_copy(bias_b[0:3, :], picked[:]))
            for l in range(LAYERS):
                then(nc.vector.tensor_tensor(b1col[:, l], b1col[:, l], psum[:, 0, 2 * l:2 * l + 2], ALU.add))
                then(nc.vector.tensor_scalar(w1[:, l], w1[:, l], g1col[:, l:l + 1], None, ALU.mult))

        @block.tensor
        def _(pe):
            pe.wait_ge(loaded, 16 * (len(loads) + 1))
            for l in range(LAYERS):
                nc.tensor.matmul(psum[0:3, 1 + l, 0:3 * D], bo_cols[:, l], wkvq[:, l], start=True, stop=True)
            for l in range(LAYERS):
                for c in range(2):
                    mm = nc.tensor.matmul(psum[:, 0, 2 * l + c:2 * l + c + 1], w1[:, l, c * D:(c + 1) * D],
                                          b1lncol[:, l:l + 1], start=True, stop=True)
            mm.then_inc(pe_made, 1)


def guess_root(core, nc, act, st, prefix, var, guess):
    logged, guessed, refined = (core.sem(f"{prefix}_{n}") for n in ("logged", "guessed", "refined"))
    log = core.sb(f"{prefix}_log", [P, var.shape[-1]])
    if not st.first:
        act.wait_ge(guessed, st.done() - 1)
    nc.scalar.activation(log[:], var, ACT.Ln, bias=core.sb("ln_eps", [P, 1])[:, 0:1]).then_inc(logged, 1)
    act.wait_ge(logged, st.done())
    if not st.first:
        act.wait_ge(refined, st.done(3) - 3)
    nc.scalar.activation(guess[:], log[:], ACT.Exp, scale=-0.5).then_inc(guessed, 1)


def refine_root(core, nc, dve, st, prefix, var, guess, rs, stage):
    guessed, refined = core.sem(f"{prefix}_guessed"), core.sem(f"{prefix}_refined")
    square, off, shifted = (core.sb(f"{prefix}_{n}", [P, var.shape[-1]]) for n in ("square", "off", "shifted"))
    if stage == 0:
        nc.vector.tensor_scalar(shifted[:], var, LN_EPS, None, ALU.add).then_inc(core.sem(f"{prefix}_var_shifted"), 1)
    elif stage == 1:
        dve.wait_ge(guessed, st.done())
        nc.vector.tensor_tensor(square[:], guess[:], guess[:], ALU.mult).then_inc(refined, 1)
    elif stage == 2:
        dve.wait_ge(core.sem(f"{prefix}_var_shifted"), st.done())
        dve.wait_ge(refined, st.done(3) - 2)
        nc.vector.scalar_tensor_tensor(out=off[:], in0=square[:], scalar=-0.5, in1=shifted[:], op0=ALU.mult,
                                       op1=ALU.mult).then_inc(refined, 1)
    else:
        dve.wait_ge(refined, st.done(3) - 1)
        nc.vector.scalar_tensor_tensor(out=rs[:], in0=off[:], scalar=1.5, in1=guess[:], op0=ALU.add,
                                       op1=ALU.mult).then_inc(refined, 1)


def match_edges(core, nc, dve, st, prefix, ids, rows, match):
    for t in range(TE):
        nc.vector.tensor_scalar(match[:, st.slot, t], rows[:, st.slot, t * P:(t + 1) * P],
                                ids[:, st.place, t:t + 1], None, ALU.is_equal).then_inc(core.sem(f"{prefix}_matched"), 1)


def count_later(core, nc, dve, st, prefix, match):
    later, others = core.sb("later", [P, P]), core.sb("pick_others", [P, TE])
    scratch = core.sb("pick_scratch", [P, TE, P])
    dve.wait_ge(core.sem(f"{prefix}_matched"), st.done(TE))
    if not st.first:
        dve.wait_ge(core.sem(f"{prefix}_chained"), st.done(3) - 3)
    for t in range(TE):
        nc.vector.tensor_tensor_reduce(out=scratch[:, t], in0=match[:, st.slot, t], in1=later[:], scale=1.0, scalar=0.0,
                                       op0=ALU.mult, op1=ALU.add, accum_out=others[:, t:t + 1]
                                       ).then_inc(core.sem(f"{prefix}_counted"), 1)


def pick_targets(core, nc, dve, st, prefix, ids, target):
    trash = core.sb("trash", [P, 1])
    lone, moved, others = (core.sb("pick_lone", [P, TE]), core.sb("pick_moved", [P, TE]),
                           core.sb("pick_others", [P, TE]))
    counted, chained, picked = (core.sem(f"{prefix}_{n}") for n in ("counted", "chained", "picked"))
    if not st.first:
        dve.wait_ge(picked, st.done() - 1)
    nc.vector.tensor_scalar(moved[:], ids[:, st.place, 0:TE], trash[:, 0:1], None, ALU.subtract).then_inc(chained, 1)
    dve.wait_ge(counted, st.done(TE))
    nc.vector.tensor_scalar(lone[:], others[:], 0.0, None, ALU.is_equal).then_inc(chained, 1)
    dve.wait_ge(chained, st.done(3) - 1)
    nc.vector.tensor_tensor(moved[:], moved[:], lone[:], ALU.mult).then_inc(chained, 1)
    dve.wait_ge(chained, st.done(3))
    if st.place_reused:
        dve.wait_ge(core.sems(f"{prefix}_added")[st.slot], st.landed_two_before(16 * TE))
    nc.vector.tensor_scalar(target[:, st.place], moved[:], trash[:, 0:1], None, ALU.add).then_inc(picked, 1)


def gather_and_add(core, nc, pool, steps, layer, prefix, lag, source, table, zeroed, zero_parts, ends, rows_in,
                   users, sums, target):
    ends_landed, gathered = core.place_sems(f"{prefix}_ends_landed"), core.place_sems(f"{prefix}_gathered")
    added = core.sems(f"{prefix}_added")
    rows_used, uses = core.sem(users[0]), users[1]
    summed, picked = core.sem(f"{prefix}_summed"), core.sem(f"{prefix}_picked")

    def gather(st, t):
        k = st.place
        if t == 0:
            counts = held(core, pool, st.place_landed(), *[st.turn_before(uses)] * st.place_reused)
            pool.wait_ge(ends_landed[k], counts[0])
            if st.place_reused:
                pool.wait_ge(rows_used, counts[1])
        for c in (t, TE + t):
            nc.gpsimd.indirect_dma_start(
                rows_in[:, k, c], None, source, bass.IndirectOffsetOnAxis(ap=ends[:, k, c:c + 1].bitcast(U32), axis=0)
            ).then_inc(gathered[k], 16)

    def add(st, t):
        k = st.slot
        if t == 0:
            if isinstance(st.index, int) and st.index == 0:
                pool.wait_ge(zeroed, 16 * zero_parts)
            done, previous = held(core, pool, st.done(), st.landed(16 * TE) if k == 1 else st.landed_before(16 * TE))
            pool.wait_ge(summed, done)
            pool.wait_ge(picked, done)
            pool.wait_ge(added[1 - k], previous)
        else:
            previous, = held(core, pool, st.landed_before(16 * TE) + 16 * t)
            pool.wait_ge(added[k], previous)
        nc.gpsimd.indirect_dma_start(
            table, bass.IndirectOffsetOnAxis(ap=target[:, st.place, t:t + 1].bitcast(U32), axis=0), sums[:, st.place, t], None,
            compute_op=ALU.add).then_inc(added[k], 16)

    stages = []
    for t in range(TE):
        stages += [(0, lambda st, t=t: gather(st, t)), (-lag, lambda st, t=t: add(st, t))]
    run_steps(pool, steps, stages, layer)
    end = last_step(steps, layer)
    for k in range(2):
        pool.wait_ge(added[k], end.landed(16 * TE))


def l0_edge_phase(core, w, steps, x, table, zero_parts, to_zero):
    nc, psum = core.nc, core.psum
    ident = core.sb("ident", [P, P])
    w0, wi, ae = core.sb("w0_ext", [P, D + H0]), core.sb("w0_src", [P, H0]), core.sb("a_edge", [P, H0])
    ends, ids = core.sb("ends", [P, TURN, 2 * TE], I32), core.sb("ids", [P, TURN, TE])
    equal_rows = core.sb("equal_rows", [P, 2, TE * P], I32)
    attr = core.sb("attr", [P, 2, TE * P])
    x_in = core.sb("rows_in", [P, TURN, 2 * TE, D])
    n_in, x_t = core.sb("normed", [P, 2, 2 * TE, D]), core.sb("rows_t", [P, 2, 2 * TE * P])
    stats, mv = core.sb("e_stats", [P, 2 * TE, 6]), core.sb("e_mv", [P, 2, 2 * TE, 2])
    guess, rs = core.sb("e_guess", [P, 2 * TE]), core.sb("e_rs", [P, 2 * TE])
    match = core.sb("match", [P, 2, TE, P])
    target = core.sb("target", [P, TURN, TE], I32)
    logit, leaky = core.sb("logit", [P, 2, TE, H0]), core.sb("leaky", [P, TE, H0])
    top, centred = core.sb("top", [P, TE]), core.sb("centred", [P, 2, TE, H0])
    grown, total = core.sb("grown", [P, 2, TE, H0]), core.sb("total", [P, TE])
    share = core.sb("share", [P, TE, H0])
    msg, sums = core.sb("msg0", [P, 2, TE, D]), core.sb("sums0", [P, TURN, TE, D])

    ps_t = lambda k: psum[:, k]
    ps_w = lambda k: psum[:, 2 + k].rearrange("p (t n) -> p t n", t=TE)
    ps_m = lambda k: psum[:, 4 + k, 0:TE * D].rearrange("p (t n) -> p t n", t=TE)

    ends_landed, rows_landed = core.place_sems("e0_ends_landed"), core.sems("e0_rows_landed")
    attr_landed, gathered, added = core.sems("e0_attr_landed"), core.place_sems("e0_gathered"), core.sems("e0_added")
    (cast, stated, aggregated, normed, turned, relued, projected, logits_out, matched,
     picked, chain, centre_done, exped, weighed, merged, summed) = (
        core.sem("e0_" + n) for n in
        ("cast", "stated", "aggregated", "normed", "turned", "relued",
         "projected", "logits_out", "matched", "picked", "softmaxed", "centred", "exped", "weighed", "merged",
         "summed"))

    zeros = core.sb("zeros", [P, to_zero.shape[-1]])

    with nc.Block() as block:
        @block.sync
        def _(sp):
            zeroed = core.sem("zeroed_1")

            def load(st):
                if st.place_reused:
                    used, previous = held(core, sp, st.place_landed_before(16 * 2 * TE), st.turn_before())
                    sp.wait_ge(gathered[st.place], used)
                    sp.wait_ge(cast, previous)
                sp.dma_start(ends[:, st.place], w["ends"][st.index]).then_inc(ends_landed[st.place], 16)

            def load_rows(st):
                k = st.slot
                if st.reused:
                    before, = held(core, sp, st.before(TE))
                    sp.wait_ge(matched, before)
                sp.dma_start(equal_rows[:, k], w["src_rows"][st.index].partition_broadcast(P)).then_inc(rows_landed[k], 16)
                if st.reused:
                    before, = held(core, sp, st.before())
                    sp.wait_ge(projected, before)
                sp.dma_start(attr[0:FE, k], w["attr_T"][:, bass.ds(st.index * (TE * P), TE * P)]).then_inc(attr_landed[k], 16)

            def zero(st):
                sp.dma_start(to_zero[st.index], zeros[:]).then_inc(zeroed, 16)

            run_steps(sp, steps, [(2, load), (0, load_rows), (0, zero)])

        @block.gpsimd
        def _(pool):
            gather_and_add(core, nc, pool, steps, 0, "e0", 4, x, table, core.sem("zeroed_0"), zero_parts, ends, x_in,
                           ("e0_normed", 2 * TE), sums, target)

        @block.vector
        def _(dve):
            def statistics(st):
                dve.wait_ge(ends_landed[st.place], st.place_landed())
                if st.place_reused:
                    dve.wait_ge(picked, st.turn_before())
                nc.vector.tensor_copy(ids[:, st.place], ends[:, st.place, 0:TE]).then_inc(cast, 1)
                dve.wait_ge(gathered[st.place], st.place_landed(16 * 2 * TE))
                for c in range(2 * TE):
                    nc.vector.bn_stats(stats[:, c], x_in[:, st.place, c]).then_inc(stated, 1)

            def moments(st):
                all_stated, = held(core, dve, st.done(2 * TE))
                dve.wait_ge(stated, all_stated)
                for c in range(2 * TE):
                    nc.vector.bn_aggr(mv[:, st.slot, c], stats[:, c]).then_inc(aggregated, 1)

            def refine(stage, st):
                if stage == 0:
                    dve.wait_ge(aggregated, st.done(2 * TE))
                refine_root(core, nc, dve, st, "e0", mv[:, st.slot, :, 1], guess, rs, stage)

            def normalise(st):
                k = st.slot
                dve.wait_ge(core.sem("e0_refined"), st.done(3))
                if st.reused:
                    dve.wait_ge(turned, st.before())
                for c in range(2 * TE):
                    nc.vector.tensor_scalar(n_in[:, k, c], x_in[:, st.place, c], mv[:, k, c, 0:1], rs[:, c:c + 1],
                                            ALU.subtract, ALU.mult).then_inc(normed, 1)

            def leak(st):
                dve.wait_ge(logits_out, st.done())
                nc.vector.scalar_tensor_tensor(out=leaky[:], in0=logit[:, st.slot], scalar=ALPHA, in1=logit[:, st.slot],
                                               op0=ALU.mult, op1=ALU.max).then_inc(chain, 1)

            def find_top(st):
                dve.wait_ge(chain, st.done(5) - 4)
                nc.vector.tensor_reduce(top[:], leaky[:], AX.X, ALU.max).then_inc(chain, 1)

            def centre(st):
                dve.wait_ge(chain, st.done(5) - 3)
                nc.vector.tensor_tensor(centred[:, st.slot], leaky[:], over_lanes(top[:], H0),
                                        ALU.subtract).then_inc(centre_done, 1)

            def find_matches(st):
                dve.wait_ge(cast, st.done())
                dve.wait_ge(rows_landed[st.slot], st.landed())
                if st.reused:
                    dve.wait_ge(merged, st.before())
                match_edges(core, nc, dve, st, "e0", ids, equal_rows, match)

            def sum_heads(st):
                dve.wait_ge(exped, st.done())
                nc.vector.tensor_reduce(total[:], grown[:, st.slot], AX.X, ALU.add).then_inc(chain, 1)

            def invert(st):
                dve.wait_ge(chain, st.done(5) - 2)
                nc.vector.reciprocal(total[:], total[:]).then_inc(chain, 1)

            def divide(st):
                dve.wait_ge(chain, st.done(5) - 1)
                nc.vector.tensor_tensor(share[:], grown[:, st.slot], over_lanes(total[:], H0), ALU.mult).then_inc(chain, 1)

            def weigh(st):
                k = st.slot
                dve.wait_ge(chain, st.done(5))
                nc.vector.tensor_tensor(msg[:, k].rearrange("p t (h d) -> p t h d", h=H0),
                                        ps_w(k)[:, :, 0:D].rearrange("p t (h d) -> p t h d", h=H0),
                                        over_lanes(share[:], D0), ALU.mult).then_inc(weighed, 1)

            refinements = [lambda st, n=n: refine(n, st) for n in range(4)]
            run_steps(dve, steps, [
                (0, statistics), (-2, leak), (0, moments), (-2, find_top), (0, refinements[0]), (-2, centre),
                (-2, find_matches), (0, refinements[1]), (-2, sum_heads), (0, refinements[2]), (-2, invert),
                (0, refinements[3]), (-2, divide), (-2, lambda st: count_later(core, nc, dve, st, "e0", match)),
                (-2, weigh), (0, normalise), (-2, lambda st: pick_targets(core, nc, dve, st, "e0", ids, target))])

        @block.scalar
        def _(act):
            act.preload_act_table_set(EXP_AND_LN)

            def root(st):
                act.wait_ge(aggregated, st.done(2 * TE))
                guess_root(core, nc, act, st, "e0", mv[:, st.slot, :, 1], guess)

            def relu_turned(st):
                act.wait_ge(turned, st.done())
                if st.reused:
                    act.wait_ge(projected, st.before())
                nc.scalar.activation(x_t[:, st.slot], ps_t(st.slot), ACT.Relu).then_inc(relued, 1)

            def logits(st):
                act.wait_ge(projected, st.done())
                nc.scalar.copy(logit[:, st.slot], ps_w(st.slot)[:, :, D:D + H0]).then_inc(logits_out, 1)

            def exp(st):
                act.wait_ge(centre_done, st.done())
                nc.scalar.activation(grown[:, st.slot], centred[:, st.slot], ACT.Exp).then_inc(exped, 1)

            def sums_out(st):
                act.wait_ge(merged, st.done())
                if st.place_reused:
                    act.wait_ge(added[st.slot], st.landed_two_before(16 * TE))
                nc.scalar.copy(sums[:, st.place], ps_m(st.slot)).then_inc(summed, 1)

            run_steps(act, steps, [(0, root), (-2, exp), (-1, logits), (0, relu_turned), (-2, sums_out)])

        @block.tensor
        def _(pe):
            def turn(st):
                k = st.slot
                pe.wait_ge(normed, st.done(2 * TE))
                if st.reused:
                    pe.wait_ge(relued, st.before())
                for c in range(2 * TE):
                    mm = nc.tensor.transpose(ps_t(k)[:, c * P:(c + 1) * P], n_in[:, k, c], ident[:])
                mm.then_inc(turned, 1)

            def project(st):
                k = st.slot
                pe.wait_ge(relued, st.done())
                pe.wait_ge(attr_landed[k], st.landed())
                if st.reused:
                    pe.wait_ge(weighed, st.before())
                    pe.wait_ge(logits_out, st.before())
                for t in range(TE):
                    nc.tensor.matmul(ps_w(k)[:, t, 0:D + H0], x_t[:, k, (TE + t) * P:(TE + t + 1) * P], w0[:],
                                     start=True, stop=False)
                    nc.tensor.matmul(ps_w(k)[:, t, D:D + H0], x_t[:, k, t * P:(t + 1) * P], wi[:],
                                     start=False, stop=False)
                    mm = nc.tensor.matmul(ps_w(k)[:, t, D:D + H0], attr[:, k, t * P:(t + 1) * P], ae[:],
                                          start=False, stop=True)
                mm.then_inc(projected, 1)

            def merge(st):
                k = st.slot
                pe.wait_ge(weighed, st.done())
                pe.wait_ge(matched, st.done(TE))
                if st.reused:
                    pe.wait_ge(summed, st.before())
                for t in range(TE):
                    mm = nc.tensor.matmul(ps_m(k)[:, t], match[:, k, t], msg[:, k, t], start=True, stop=True)
                mm.then_inc(merged, 1)

            run_steps(pe, steps, [(0, turn), (-2, merge), (0, project)])


def l0_node_phase(core, w, steps, x, table, x1_table, h_table):
    nc, psum = core.nc, core.psum
    ident, wemb, ones = core.sb("ident", [P, P]), core.sb("wemb", [P, D]), core.sb("ones", [P, P], BF16)
    bo_row = core.sb("bias_b", [P, LAYERS * 5 * D], BF16)[:, 3 * D:4 * D]
    last_shift = core.sb("ln2_b_rows", [P, LAYERS, D])[:, LAYERS - 1]
    node = lambda name: core.sb(name, [P, 2, TN, D])
    o_in, x_in, low, e_low, high = node("n_a"), node("n_b"), node("n_c"), node("n_d"), node("n_e")
    x1, n1, n1t, h_out, lift = node("n_f"), node("n_g"), node("n_h"), node("n_i"), node("n_j")
    kept, x1_kept = node("n_k"), core.sem("n0_x1_kept")
    stats, mv = core.sb("n_stats", [P, TN, 6]), core.sb("n_mv", [P, 2, TN, 2])
    guess, rs = core.sb("n_guess", [P, TN]), core.sb("n_rs", [P, TN])
    ps_t = lambda k: psum[:, k].rearrange("p (t n) -> p t n", t=TN)
    ps_h = lambda k: psum[:, 2 + k].rearrange("p (t n) -> p t n", t=TN)
    per_step = lambda t: t[0:steps * TN * P, :].rearrange("(s p j) d -> s p j d", p=P, j=TN)

    o_landed, x_landed = core.sems("n0_o_landed"), core.sems("n0_x_landed")
    x1_stored, h_stored = core.sems("n0_x1_stored"), core.sems("n0_h_stored")
    lowed, lifted, highed, exped, x1_made, stated, aggregated, normed, turned, relued, embedded, h_made = (
        core.sem("n0_" + n) for n in ("lowed", "lifted", "highed", "exped", "x1_made", "stated", "aggregated",
                                      "normed", "turned", "relued", "embedded", "h_made"))

    with nc.Block() as block:
        @block.sync
        def _(sp):
            def load(st):
                k = st.slot
                if st.reused:
                    before, = held(core, sp, st.before())
                    sp.wait_ge(highed, before)
                    sp.wait_ge(lowed, before)
                    sp.wait_ge(lifted, before)
                sp.dma_start(o_in[:, k], per_step(table)[st.index]).then_inc(o_landed[k], 16)
                sp.dma_start(x_in[:, k], per_step(x)[st.index]).then_inc(x_landed[k], 16)

            def store(st):
                k = st.slot
                ready, = held(core, sp, st.done())
                sp.wait_ge(x1_kept, ready)
                sp.dma_start(per_step(x1_table)[st.index], kept[:, k]).then_inc(x1_stored[k], 16)

            def store_h(st):
                k = st.slot
                ready, = held(core, sp, st.done())
                sp.wait_ge(h_made, ready)
                sp.dma_start(per_step(h_table)[st.index], h_out[:, k]).then_inc(h_stored[k], 16)

            run_steps(sp, steps, [(-3, store_h), (0, store), (4, load)])
            end = last_step(steps, 0)
            for k in range(2):
                sp.wait_ge(x1_stored[k], end.landed())
                sp.wait_ge(h_stored[k], end.landed())

        @block.vector
        def _(dve):
            def add(st):
                k = st.slot
                dve.wait_ge(exped, st.done())
                dve.wait_ge(highed, st.done())
                if st.reused:
                    dve.wait_ge(normed, st.before(TN))
                    dve.wait_ge(x1_kept, st.before())
                nc.vector.scalar_tensor_tensor(out=x1[:, k], in0=e_low[:, k], scalar=-1.0, in1=high[:, k],
                                               op0=ALU.add, op1=ALU.add).then_inc(x1_made, 1)

            def statistics(st):
                k = st.slot
                dve.wait_ge(x1_made, st.done())
                for j in range(TN):
                    nc.vector.bn_stats(stats[:, j], x1[:, k, j]).then_inc(stated, 1)

            def moments(st):
                k = st.slot
                all_stated, = held(core, dve, st.done(TN))
                dve.wait_ge(stated, all_stated)
                for j in range(TN):
                    nc.vector.bn_aggr(mv[:, k, j], stats[:, j]).then_inc(aggregated, 1)

            def normalise(st):
                k = st.slot
                dve.wait_ge(core.sem("n0_refined"), st.done(3))
                if st.reused:
                    dve.wait_ge(turned, st.before())
                for j in range(TN):
                    nc.vector.tensor_scalar(n1[:, k, j], x1[:, k, j], mv[:, k, j, 0:1], rs[:, j:j + 1],
                                            ALU.subtract, ALU.mult).then_inc(normed, 1)

            def refine(stage, st):
                if stage == 0:
                    dve.wait_ge(aggregated, st.done(TN))
                refine_root(core, nc, dve, st, "n0", mv[:, st.slot, :, 1], guess, rs, stage)

            refinements = [lambda st, n=n: refine(n, st) for n in range(4)]
            run_steps(dve, steps, [(-1, refinements[0]), (-1, refinements[1]), (0, add), (-1, refinements[2]),
                                   (0, statistics), (-1, refinements[3]), (0, moments), (-1, normalise)])

        @block.gpsimd
        def _(pool):
            def residual(st):
                k = st.slot
                pool.wait_ge(lifted, st.done())
                pool.wait_ge(x_landed[k], st.landed())
                if st.reused:
                    pool.wait_ge(x1_made, st.before())
                nc.gpsimd.tensor_tensor(high[:, k], lift[:, k], x_in[:, k], ALU.add).then_inc(highed, 1)

            def keep(st):
                k = st.slot
                pool.wait_ge(x1_made, st.done())
                if st.reused:
                    pool.wait_ge(x1_stored[k], st.landed_before())
                nc.gpsimd.tensor_tensor(kept[:, k], x1[:, k], over_tiles(last_shift, TN), ALU.add).then_inc(x1_kept, 1)

            run_steps(pool, steps, [(0, keep), (2, residual)])

        @block.scalar
        def _(act):
            act.preload_act_table_set(EXP_AND_LN)

            def split(st):
                k = st.slot
                act.wait_ge(o_landed[k], st.landed())
                if st.reused:
                    act.wait_ge(exped, st.before())
                    act.wait_ge(highed, st.before())
                nc.scalar.activation(low[:, k], o_in[:, k], ACT.Relu, scale=-1.0).then_inc(lowed, 1)
                nc.scalar.activation(lift[:, k], o_in[:, k], ACT.Relu).then_inc(lifted, 1)
                act.wait_ge(lowed, st.done())
                if st.reused:
                    act.wait_ge(x1_made, st.before())
                nc.scalar.activation(e_low[:, k], low[:, k], ACT.Exp, scale=-1.0).then_inc(exped, 1)

            def root(st):
                act.wait_ge(aggregated, st.done(TN))
                guess_root(core, nc, act, st, "n0", mv[:, st.slot, :, 1], guess)

            def relu_turned(st):
                act.wait_ge(turned, st.done())
                if st.reused:
                    act.wait_ge(embedded, st.before())
                nc.scalar.activation(n1t[:, st.slot], ps_t(st.slot), ACT.Relu).then_inc(relued, 1)

            def h_ready(st):
                act.wait_ge(embedded, st.done())
                if st.reused:
                    act.wait_ge(h_stored[st.slot], st.landed_before())
                nc.scalar.copy(h_out[:, st.slot], ps_h(st.slot)).then_inc(h_made, 1)

            run_steps(act, steps, [(0, root), (2, split), (-1, relu_turned), (-2, h_ready)])

        @block.tensor
        def _(pe):
            def turn(st):
                k = st.slot
                pe.wait_ge(normed, st.done(TN))
                if st.reused:
                    pe.wait_ge(relued, st.before())
                for j in range(TN):
                    mm = nc.tensor.transpose(ps_t(k)[:, j], n1[:, k, j], ident[:])
                mm.then_inc(turned, 1)

            def embed(st):
                k = st.slot
                pe.wait_ge(relued, st.done())
                if st.reused:
                    pe.wait_ge(h_made, st.before())
                nc.tensor.matmul(ps_h(k), ones[:], over_tiles(bo_row, TN), start=True, stop=False)
                for j in range(TN):
                    mm = nc.tensor.matmul(ps_h(k)[:, j], n1t[:, k, j], wemb[:], start=False, stop=(j == TN - 1))
                mm.then_inc(embedded, 1)

            run_steps(pe, steps, [(-1, turn), (-2, embed)])


def l1_edge_phase(core, w, steps, layer, h_table, table, to_zero):
    nc, psum = core.nc, core.psum
    ident, ones = core.sb("ident", [P, P]), core.sb("ones", [P, P], BF16)
    wkvq = core.sb("wkvq", [P, LAYERS, 3 * D])[:, layer]
    bias = core.sb("bias_b", [P, LAYERS * 5 * D], BF16)[:].rearrange("p (l n) -> p l n", l=LAYERS)[:, layer]
    ends, ids = core.sb("ends", [P, TURN, 2 * TE], I32), core.sb("ids", [P, TURN, TE])
    equal_rows = core.sb("equal_rows", [P, 2, TE * P], I32)
    h_in, h_t = core.sb("rows_in", [P, TURN, 2 * TE, D]), core.sb("rows_t", [P, 2, 2 * TE * P])
    match = core.sb("match", [P, 2, TE, P])
    target = core.sb("target", [P, TURN, TE], I32)
    q, prod = core.sb("q", [P, 2, TE, D]), core.sb("prod", [P, TE, D])
    score, clipped = core.sb("score", [P, TE, H1]), core.sb("clipped", [P, 2, TE, H1])
    msg, sums = core.sb("msg1", [P, 2, TE, MW]), core.sb("sums1", [P, TURN, TE, MW])

    ps_t = lambda k: psum[:, k]
    ps_kv = lambda k: psum[:, 2 + k].rearrange("p (t n) -> p t n", t=TE)
    ps_q = lambda k: psum[:, 4 + k, 0:TE * D].rearrange("p (t n) -> p t n", t=TE)
    ps_m = lambda k: psum[:, 6 + k, 0:TE * MW].rearrange("p (t n) -> p t n", t=TE)

    ends_landed, rows_landed = core.place_sems("e1_ends_landed"), core.sems("e1_rows_landed")
    gathered, added = core.place_sems("e1_gathered"), core.sems("e1_added")
    (cast, turned, turned_out, queried, projected, q_out, matched, picked, multiplied, scored, clip_done, exped, weighed,
     merged, summed) = (core.sem("e1_" + n) for n in
                        ("cast", "turned", "turned_out", "queried", "projected", "q_out", "matched", "picked",
                         "multiplied", "scored", "clipped", "exped", "weighed", "merged", "summed"))

    with nc.Block() as block:
        @block.sync
        def _(sp):
            zeroed = core.sem(f"zeroed_{layer + 2}")

            def load(st):
                if st.place_reused:
                    used, previous = held(core, sp, st.place_landed_before(16 * 2 * TE), st.turn_before())
                    sp.wait_ge(gathered[st.place], used)
                    sp.wait_ge(cast, previous)
                sp.dma_start(ends[:, st.place], w["ends"][st.index]).then_inc(ends_landed[st.place], 16)

            def load_rows(st):
                k = st.slot
                if st.reused:
                    before, = held(core, sp, st.before(TE))
                    sp.wait_ge(matched, before)
                sp.dma_start(equal_rows[:, k], w["dst_rows"][st.index].partition_broadcast(P)).then_inc(rows_landed[k], 16)

            def zero(st):
                sp.dma_start(to_zero[st.index], core.sb("zeros", [P, to_zero.shape[-1]])[:]).then_inc(zeroed, 16)

            run_steps(sp, steps, [(2, load), (0, load_rows)] + [(0, zero)] * (to_zero is not None), layer)

        @block.gpsimd
        def _(pool):
            gather_and_add(core, nc, pool, steps, layer, "e1", 3, h_table, table,
                           core.sem(f"zeroed_{layer + 1}"), steps, ends, h_in, ("e1_turned", 1),
                           sums, target)

        @block.vector
        def _(dve):
            def message(st):
                k = st.slot
                dve.wait_ge(ends_landed[st.place], st.place_landed())
                if st.place_reused:
                    dve.wait_ge(picked, st.turn_before())
                nc.vector.tensor_copy(ids[:, st.place], ends[:, st.place, TE:]).then_inc(cast, 1)
                dve.wait_ge(cast, st.done())
                dve.wait_ge(rows_landed[k], st.landed())
                if st.reused:
                    dve.wait_ge(merged, st.before())
                match_edges(core, nc, dve, st, "e1", ids, equal_rows, match)
                dve.wait_ge(q_out, st.done())
                dve.wait_ge(projected, st.done())
                nc.vector.tensor_tensor(prod[:], ps_kv(k)[:, :, 0:D], q[:, k], ALU.mult).then_inc(multiplied, 1)
                dve.wait_ge(multiplied, st.done())
                nc.vector.tensor_reduce(score[:], prod[:].rearrange("p t (h d) -> p t h d", h=H1), AX.X,
                                        ALU.add).then_inc(scored, 1)
                dve.wait_ge(scored, st.done())
                nc.vector.tensor_scalar(clipped[:, k], score[:], CLIP * SCALE, -CLIP * SCALE, ALU.min,
                                        ALU.max).then_inc(clip_done, 1)
                dve.wait_ge(exped, st.done())
                nc.vector.tensor_tensor(msg[:, k, :, 0:D].rearrange("p t (h d) -> p t h d", h=H1),
                                        ps_kv(k)[:, :, D:].rearrange("p t (h d) -> p t h d", h=H1),
                                        over_lanes(msg[:, k, :, D:], D1), ALU.mult).then_inc(weighed, 1)
                count_later(core, nc, dve, st, "e1", match)
                pick_targets(core, nc, dve, st, "e1", ids, target)

            run_steps(dve, steps, [(0, message)], layer)

        @block.scalar
        def _(act):
            def turned_to_sbuf(st):
                act.wait_ge(turned, st.done())
                if st.reused:
                    act.wait_ge(projected, st.before())
                nc.scalar.copy(h_t[:, st.slot], ps_t(st.slot)).then_inc(turned_out, 1)

            def q_to_sbuf(st):
                act.wait_ge(queried, st.done())
                if st.reused:
                    act.wait_ge(multiplied, st.before())
                nc.scalar.copy(q[:, st.slot], ps_q(st.slot)).then_inc(q_out, 1)

            def exp(st):
                act.wait_ge(clip_done, st.done())
                if st.reused:
                    act.wait_ge(merged, st.before())
                nc.scalar.activation(msg[:, st.slot, :, D:], clipped[:, st.slot], ACT.Exp,
                                     scale=1.0 / SCALE).then_inc(exped, 1)

            def sums_out(st):
                act.wait_ge(merged, st.done())
                if st.place_reused:
                    act.wait_ge(added[st.slot], st.landed_two_before(16 * TE))
                nc.scalar.copy(sums[:, st.place], ps_m(st.slot)).then_inc(summed, 1)

            run_steps(act, steps, [(0, turned_to_sbuf), (0, q_to_sbuf), (0, exp), (-1, sums_out)], layer)

        @block.tensor
        def _(pe):
            def turn(st):
                k = st.slot
                pe.wait_ge(gathered[st.place], st.place_landed(16 * 2 * TE))
                if st.reused:
                    pe.wait_ge(turned_out, st.before())
                for c in range(2 * TE):
                    mm = nc.tensor.transpose(ps_t(k)[:, c * P:(c + 1) * P], h_in[:, st.place, c], ident[:])
                mm.then_inc(turned, 1)

            def merge(st):
                k = st.slot
                pe.wait_ge(weighed, st.done())
                pe.wait_ge(matched, st.done(TE))
                pe.wait_ge(exped, st.done())
                if st.reused:
                    pe.wait_ge(summed, st.before())
                for t in range(TE):
                    mm = nc.tensor.matmul(ps_m(k)[:, t], match[:, k, t], msg[:, k, t], start=True, stop=True)
                mm.then_inc(merged, 1)

            def project(st):
                k = st.slot
                pe.wait_ge(turned_out, st.done())
                if st.reused:
                    pe.wait_ge(weighed, st.before())
                    pe.wait_ge(q_out, st.before())
                nc.tensor.matmul(ps_q(k), ones[:], over_tiles(bias[:, 2 * D:3 * D], TE), start=True, stop=False)
                for t in range(TE):
                    mm = nc.tensor.matmul(ps_q(k)[:, t], h_t[:, k, (TE + t) * P:(TE + t + 1) * P], wkvq[:, 2 * D:],
                                          start=False, stop=(t == TE - 1))
                mm.then_inc(queried, 1)
                nc.tensor.matmul(ps_kv(k), ones[:], over_tiles(bias[:, 0:2 * D], TE), start=True, stop=False)
                for t in range(TE):
                    mm = nc.tensor.matmul(ps_kv(k)[:, t], h_t[:, k, t * P:(t + 1) * P], wkvq[:, 0:2 * D],
                                          start=False, stop=(t == TE - 1))
                mm.then_inc(projected, 1)

            run_steps(pe, steps, [(0, turn), (0, project), (-1, merge)], layer)


def l1_node_phase(core, w, steps, layer, table, h_table, x1_table, out):
    nc, psum = core.nc, core.psum
    ident, eps, ones = core.sb("ident", [P, P]), core.sb("ln_eps", [P, 1]), core.sb("ones", [P, P], BF16)
    wo = core.sb("wo", [P, LAYERS, D])[:, layer]
    w1 = core.sb("w1", [P, LAYERS, 2 * D])[:, layer]
    w2 = core.sb("w2", [P, LAYERS, 2, D])[:, layer]
    b1col = core.sb("b1_col", [P, LAYERS, 2])[:, layer]
    g1rows, g2rows, b2rows = (core.sb(f"{n}_rows", [P, LAYERS, D])[:, layer] for n in ("ln1_g", "ln2_g", "ln2_b"))
    bias = core.sb("bias_b", [P, LAYERS * 5 * D], BF16)[:].rearrange("p (l n) -> p l n", l=LAYERS)[:, layer]
    last = layer == LAYERS - 1

    node = lambda name: core.sb(name, [P, 2, TN, D])
    h_in, att, att_t, r1, n1, n1t = node("n_a"), node("n_b"), node("n_c"), node("n_d"), node("n_e"), node("n_f")
    n2, h_out, x1_in, h1, r2 = node("n_g"), node("n_h"), node("n_i"), node("n_j"), node("n_k")
    agg = core.sb("agg", [P, 2, TN, MW])
    hidden = core.sb("hidden", [P, 2, 2, TN * P])
    z = core.sb("z", [P, TN, H1])
    rz = core.sb("rz", [P, 2, TN, H1])
    stats, mv = core.sb("n_stats", [P, TN, 6]), core.sb("n_mv", [P, 2, TN, 2])
    sd, rs = core.sb("n_sd", [P, TN]), core.sb("n_rs", [P, TN])
    stats2, mv2 = core.sb("n_stats2", [P, TN, 6]), core.sb("n_mv2", [P, 2, TN, 2])
    sd2, rs2, shift2 = core.sb("n_sd2", [P, TN]), core.sb("n_rs2", [P, 2, TN]), core.sb("n_shift2", [P, 2, TN])

    by_tile = lambda b: psum[:, b].rearrange("p (t n) -> p t n", t=TN)
    ps_at = by_tile(0)
    ps_nt = by_tile(1)
    ps_o = lambda k: by_tile(2 + k)
    ps_h = lambda c: psum[:, 4 + c]
    ps_f = lambda k: by_tile(6 + k)
    per_step = lambda t: t[0:steps * TN * P, :].rearrange("(s p j) d -> s p j d", p=P, j=TN)

    agg_landed, h_landed, x1_landed = core.sems("n1_agg_landed"), core.sems("n1_h_landed"), core.sems("n1_x1_landed")
    stored = core.sems("n1_stored")
    (z_made, rz_made, att_made, att_turned, att_out, o_made, r_made, stated, aggregated, rooted, inverted, normed,
     n1_turned, n1_out, up, relued, ffn_made, carried, r2_made, stated2, aggregated2, rooted2, inverted2, shifted2, normed2, scaled,
     h_made) = (core.sem("n1_" + n) for n in
                ("z_made", "rz_made", "att_made", "att_turned", "att_out", "o_made", "r_made", "stated",
                 "aggregated", "rooted", "inverted", "normed", "n1_turned", "n1_out", "up", "relued", "ffn_made",
                 "carried", "r2_made", "stated2", "aggregated2", "rooted2", "inverted2", "shifted2", "normed2", "scaled", "h_made"))

    with nc.Block() as block:
        @block.sync
        def _(sp):
            def load(st):
                k = st.slot
                if st.reused:
                    before, = held(core, sp, st.before())
                    sp.wait_ge(att_made, before)
                sp.dma_start(agg[:, k], per_step(table)[st.index]).then_inc(agg_landed[k], 16)

            def load_h(st):
                k = st.slot
                if st.reused:
                    before, = held(core, sp, st.before())
                    sp.wait_ge(r_made, before)
                sp.dma_start(h_in[:, k], per_step(h_table)[st.index]).then_inc(h_landed[k], 16)

            def store(st):
                k = st.slot
                ready, = held(core, sp, st.done())
                sp.wait_ge(h_made, ready)
                if not last:
                    sp.dma_start(per_step(h_table)[st.index], h_out[:, k]).then_inc(stored[k], 16)
                elif isinstance(st.index, int) and (st.index + 1) * TN * P > out.shape[0]:
                    rows = out.shape[0] - st.index * TN * P
                    sp.dma_start(out[st.index * TN * P:, :].rearrange("(p j) d -> p j d", j=TN),
                                 h_out[0:rows // TN, k]).then_inc(stored[k], 16)
                else:
                    whole = out[0:out.shape[0] // (TN * P) * (TN * P), :]
                    sp.dma_start(whole.rearrange("(s p j) d -> s p j d", p=P, j=TN)[st.index],
                                 h_out[:, k]).then_inc(stored[k], 16)

            def load_x1(st):
                k = st.slot
                if not (isinstance(st.pair, int) and st.pair == 0):
                    before, = held(core, sp, st.before())
                    sp.wait_ge(h_made, before)
                sp.dma_start(x1_in[:, k], per_step(x1_table)[st.index]).then_inc(x1_landed[k], 16)

            run_steps(sp, steps, [(3, load), (2, load_h), (-5, store)] + [(-3, load_x1)] * last, layer)
            end = last_step(steps, layer)
            for k in range(2):
                sp.wait_ge(stored[k], end.landed())

        @block.gpsimd
        def _(pool):
            def attend(st):
                k = st.slot
                pool.wait_ge(agg_landed[k], st.landed())
                pool.wait_ge(rz_made, st.done())
                if st.reused:
                    pool.wait_ge(att_turned, st.before())
                nc.gpsimd.tensor_tensor(att[:, k].rearrange("p j (h d) -> p j h d", h=H1),
                                        agg[:, k, :, 0:D].rearrange("p j (h d) -> p j h d", h=H1),
                                        over_lanes(rz[:, k], D1), ALU.mult).then_inc(att_made, 1)

            def carry(st):
                k = st.slot
                pool.wait_ge(normed, st.done(TN))
                if st.reused:
                    pool.wait_ge(r2_made, st.before())
                nc.gpsimd.tensor_tensor(h1[:, k], n1[:, k], over_tiles(g1rows, TN), ALU.mult).then_inc(carried, 1)

            def finish(st):
                k = st.slot
                pool.wait_ge(normed2, st.done(TN))
                if st.reused:
                    pool.wait_ge(stored[k], st.landed_before())
                nc.gpsimd.tensor_tensor(h_out[:, k], n2[:, k], over_tiles(g2rows, TN), ALU.mult).then_inc(scaled, 1)
                pool.wait_ge(scaled, st.done())
                nc.gpsimd.tensor_tensor(h_out[:, k], h_out[:, k], over_tiles(b2rows, TN), ALU.add).then_inc(h_made, 1)

            def finish_last(st):
                k = st.slot
                pool.wait_ge(normed2, st.done(TN))
                if st.reused:
                    pool.wait_ge(stored[k], st.landed_before())
                nc.gpsimd.tensor_tensor(h_out[:, k], n2[:, k], over_tiles(g2rows, TN), ALU.mult).then_inc(scaled, 1)
                pool.wait_ge(scaled, st.done())
                pool.wait_ge(x1_landed[k], (st.pair + 1) * 16)
                nc.gpsimd.tensor_tensor(h_out[:, k], h_out[:, k], x1_in[:, k], ALU.add).then_inc(h_made, 1)

            run_steps(pool, steps, [(-1, carry), (2, attend), (-4, finish_last if last else finish)], layer)

        @block.vector
        def _(dve):
            def add1(st):
                k = st.slot
                dve.wait_ge(o_made, st.done())
                dve.wait_ge(h_landed[k], st.landed())
                if st.reused:
                    dve.wait_ge(normed, st.before(TN))
                nc.vector.tensor_tensor(r1[:, k], ps_o(k), h_in[:, k], ALU.add).then_inc(r_made, 1)

            def add2(st):
                k = st.slot
                dve.wait_ge(ffn_made, st.done())
                dve.wait_ge(carried, st.done())
                if st.reused:
                    dve.wait_ge(normed2, st.before(TN))
                nc.vector.tensor_tensor(r2[:, k], ps_f(k), h1[:, k], ALU.add).then_inc(r2_made, 1)

            def statistics1(st):
                dve.wait_ge(r_made, st.done())
                for j in range(TN):
                    nc.vector.bn_stats(stats[:, j], r1[:, st.slot, j]).then_inc(stated, 1)

            def statistics2(st):
                dve.wait_ge(r2_made, st.done())
                for j in range(TN):
                    nc.vector.bn_stats(stats2[:, j], r2[:, st.slot, j]).then_inc(stated2, 1)

            def moments1(st):
                all_stated, = held(core, dve, st.done(TN))
                dve.wait_ge(stated, all_stated)
                for j in range(TN):
                    nc.vector.bn_aggr(mv[:, st.slot, j], stats[:, j]).then_inc(aggregated, 1)

            def moments2(st):
                if not st.first:
                    all_stated, used = held(core, dve, st.done(TN), st.done() - 1)
                    dve.wait_ge(shifted2, used)
                else:
                    all_stated, = held(core, dve, st.done(TN))
                dve.wait_ge(stated2, all_stated)
                for j in range(TN):
                    nc.vector.bn_aggr(mv2[:, st.slot, j], stats2[:, j]).then_inc(aggregated2, 1)

            def weights(st):
                dve.wait_ge(agg_landed[st.slot], st.landed())
                if not st.first:
                    dve.wait_ge(rz_made, st.done() - 1)
                nc.vector.tensor_scalar(z[:], agg[:, st.slot, :, D:], Z_EPS, None, ALU.add).then_inc(z_made, 1)

            def invert1(st):
                dve.wait_ge(rooted, st.done())
                if not st.first:
                    dve.wait_ge(normed, (st.done() - 1) * TN)
                nc.vector.reciprocal(rs[:], sd[:]).then_inc(inverted, 1)

            def invert2(st):
                dve.wait_ge(rooted2, st.done())
                if st.reused:
                    dve.wait_ge(normed2, st.before(TN))
                nc.vector.reciprocal(rs2[:, st.slot], sd2[:]).then_inc(inverted2, 1)

            def invert_weights(st):
                dve.wait_ge(z_made, st.done())
                if st.reused:
                    dve.wait_ge(att_made, st.before())
                nc.vector.reciprocal(rz[:, st.slot], z[:]).then_inc(rz_made, 1)

            def shift(st):
                k = st.slot
                dve.wait_ge(aggregated2, st.done(TN))
                dve.wait_ge(inverted2, st.done())
                nc.vector.scalar_tensor_tensor(out=shift2[:, k], in0=mv2[:, k, :, 0], scalar=-1.0, in1=rs2[:, k],
                                               op0=ALU.mult, op1=ALU.mult).then_inc(shifted2, 1)

            def normalise(st):
                k = st.slot
                dve.wait_ge(aggregated, st.done(TN))
                dve.wait_ge(inverted, st.done())
                if st.reused:
                    dve.wait_ge(n1_turned, st.before())
                    dve.wait_ge(carried, st.before())
                for j in range(TN):
                    nc.vector.tensor_scalar(n1[:, k, j], r1[:, k, j], mv[:, k, j, 0:1], rs[:, j:j + 1],
                                            ALU.subtract, ALU.mult).then_inc(normed, 1)

            run_steps(dve, steps, [(0, add1), (-3, add2), (0, statistics1), (-3, statistics2), (0, moments1),
                                   (-3, moments2), (2, weights), (0, invert1), (-3, invert2), (2, invert_weights),
                                   (-3, shift), (0, normalise)], layer)

        @block.scalar
        def _(act):
            def n1_to_sbuf(st):
                act.wait_ge(n1_turned, st.done())
                if st.reused:
                    act.wait_ge(up, st.before())
                nc.scalar.copy(n1t[:, st.slot], ps_nt).then_inc(n1_out, 1)

            def att_to_sbuf(st):
                act.wait_ge(att_turned, st.done())
                if st.reused:
                    act.wait_ge(o_made, st.before())
                nc.scalar.copy(att_t[:, st.slot], ps_at).then_inc(att_out, 1)

            def root(st):
                act.wait_ge(aggregated, st.done(TN))
                if not st.first:
                    act.wait_ge(inverted, st.done() - 1)
                nc.scalar.activation(sd[:], mv[:, st.slot, :, 1], ACT.Sqrt, bias=eps[:, 0:1]).then_inc(rooted, 1)

            def relu(st):
                act.wait_ge(up, st.done())
                if st.reused:
                    act.wait_ge(ffn_made, st.before())
                for c in range(2):
                    nc.scalar.activation(hidden[:, st.slot, c], ps_h(c), ACT.Relu,
                                         bias=b1col[:, c:c + 1]).then_inc(relued, 1)

            def root2(st):
                act.wait_ge(aggregated2, st.done(TN))
                if not st.first:
                    act.wait_ge(inverted2, st.done() - 1)
                nc.scalar.activation(sd2[:], mv2[:, st.slot, :, 1], ACT.Sqrt, bias=eps[:, 0:1]).then_inc(rooted2, 1)

            def normalise2(st):
                k = st.slot
                act.wait_ge(shifted2, st.done())
                if st.reused:
                    act.wait_ge(h_made, st.before())
                for j in range(TN):
                    nc.scalar.activation(n2[:, k, j], r2[:, k, j], ACT.Identity, bias=shift2[:, k, j:j + 1],
                                         scale=rs2[:, k, j:j + 1]).then_inc(normed2, 1)

            run_steps(act, steps, [(-2, relu), (-1, n1_to_sbuf), (1, att_to_sbuf), (-4, normalise2), (0, root),
                                   (-3, root2)], layer)

        @block.tensor
        def _(pe):
            def turn_n1(st):
                pe.wait_ge(normed, st.done(TN))
                if not st.first:
                    pe.wait_ge(n1_out, st.done() - 1)
                for j in range(TN):
                    mm = nc.tensor.transpose(ps_nt[:, j], n1[:, st.slot, j], ident[:])
                mm.then_inc(n1_turned, 1)

            def turn_att(st):
                pe.wait_ge(att_made, st.done())
                if not st.first:
                    pe.wait_ge(att_out, st.done() - 1)
                for j in range(TN):
                    mm = nc.tensor.transpose(ps_at[:, j], att[:, st.slot, j], ident[:])
                mm.then_inc(att_turned, 1)

            def output(st):
                k = st.slot
                pe.wait_ge(att_out, st.done())
                if st.reused:
                    pe.wait_ge(r_made, st.before())
                for j in range(TN):
                    mm = nc.tensor.matmul(ps_o(k)[:, j], att_t[:, k, j], wo, start=True, stop=True)
                mm.then_inc(o_made, 1)

            def widen(st):
                k = st.slot
                pe.wait_ge(n1_out, st.done())
                if not st.first:
                    pe.wait_ge(relued, (st.done() - 1) * 2)
                for c in range(2):
                    mm = nc.tensor.matmul(ps_h(c), w1[:, c * D:(c + 1) * D], n1t[:, k].rearrange("p j n -> p (j n)"),
                                          start=True, stop=True)
                mm.then_inc(up, 1)

            def narrow(st):
                k = st.slot
                pe.wait_ge(relued, st.done(2))
                if st.reused:
                    pe.wait_ge(r2_made, st.before())
                nc.tensor.matmul(ps_f(k), ones[:], over_tiles(bias[:, 4 * D:], TN), start=True, stop=False)
                for j in range(TN):
                    for c in range(2):
                        mm = nc.tensor.matmul(ps_f(k)[:, j], hidden[:, k, c, j * P:(j + 1) * P], w2[:, c],
                                              start=False, stop=(c == 1 and j == TN - 1))
                mm.then_inc(ffn_made, 1)

            run_steps(pe, steps, [(0, output), (-1, turn_n1), (1, turn_att), (-2, narrow), (-1, widen)], layer)


def build(nc, w, out):
    node_rows = w["x"].shape[0]
    node_steps, edge_steps = node_rows // (TN * P), w["ends"].shape[0]
    assert node_steps % 2 == 0 and edge_steps % 2 == 0
    scratch = lambda name, rows, cols: nc.dram_tensor(name, (rows, cols), F32).ap()
    sums0 = scratch("l0_sums", node_rows + P, D)
    zero_width = -(-(node_rows + P) * MW // (P * edge_steps))
    flat1 = [nc.dram_tensor(f"l1_sums_{l}", (edge_steps * P * zero_width,), F32).ap() for l in range(LAYERS)]
    sums1 = [t[0:(node_rows + P) * MW].rearrange("(r d) -> r d", d=MW) for t in flat1]
    to_zero = [t.rearrange("(s p n) -> s p n", p=P, n=zero_width) for t in flat1] + [None]
    x1_table, h_table = scratch("x1_table", node_rows, D), scratch("h_table", node_rows, D)
    with ExitStack() as ctx:
        core = Core(nc, ctx)
        core.psum = ctx.enter_context(nc.psum_tensor("psum", [P, 8, 512], F32))
        cells = (node_rows + P) * D
        parts = next(c for c in range(-(-cells // (P * zero_width)), cells) if cells % (P * c) == 0)
        setup_phase(core, w, node_rows, zero_width,
                    sums0.rearrange("r d -> (r d)").rearrange("(c p n) -> c p n", c=parts, p=P))
        l0_edge_phase(core, w, edge_steps, w["x"], sums0, parts, to_zero[0])
        l0_node_phase(core, w, node_steps, w["x"], sums0, x1_table, h_table)
        for layer in range(LAYERS):
            l1_edge_phase(core, w, edge_steps, layer, h_table, sums1[layer], to_zero[layer + 1])
            l1_node_phase(core, w, node_steps, layer, sums1[layer], h_table, x1_table, out)


def kernel(**inputs):
    import numpy as _np
    import concourse.bacc as _bacc
    from concourse import mybir as _mybir
    from concourse.bass_utils import run_bass_kernel_spmd as _run

    a = {k: _np.asarray(v) for k, v in inputs.items()}
    nodes, edges = a["x"].shape[0], a["src"].shape[0]
    node_steps = -(-nodes // (TN * P * 2)) * 2
    edge_steps = -(-edges // (TE * P * 2)) * 2
    rows, slots = node_steps * TN * P, edge_steps * TE * P
    assert rows > nodes
    src = _np.full(slots, nodes, _np.int32)
    src[:edges] = a["src"]
    dst = _np.full(slots, nodes, _np.int32)
    dst[:edges] = a["dst"]
    x = _np.zeros((rows, D), _np.float32)
    x[:nodes] = a["x"]
    attr_t = _np.zeros((FE, slots), _np.float32)
    attr_t[:, :edges] = a["edge_attr_16"].T
    by_partition = lambda v: v.reshape(edge_steps, TE, P).transpose(0, 2, 1)
    arrays = {
        "x": x, "attr_T": attr_t,
        "ends": _np.concatenate([by_partition(src), by_partition(dst)], axis=2),
        "src_rows": src.reshape(edge_steps, TE * P), "dst_rows": dst.reshape(edge_steps, TE * P),
        "a_T": a["L0_gnn_a"].T, "ln1_g_T": a["L1_gnn_ln1_g"].T, "ln1_b_T": a["L1_gnn_ln1_b"].T,
        "bo_T": _np.repeat(a["L1_gnn_bo"].T[:, :, None], 3, axis=2),
        "b1_T": a["L1_gnn_b1"].reshape(LAYERS, 2, P).transpose(2, 0, 1).reshape(P, LAYERS * 2),
    }
    for name in ("L0_gnn_W", "L0_gnn_a", "L1_gnn_Wemb", "L1_gnn_Wq", "L1_gnn_bq", "L1_gnn_Wk", "L1_gnn_bk", "L1_gnn_Wv",
                 "L1_gnn_bv", "L1_gnn_Wo", "L1_gnn_bo", "L1_gnn_ln1_g", "L1_gnn_ln1_b", "L1_gnn_W1", "L1_gnn_W2", "L1_gnn_b2",
                 "L1_gnn_ln2_g", "L1_gnn_ln2_b"):
        arrays[name] = a[name]
    nc = _bacc.Bacc("TRN2", target_bir_lowering=False, num_devices=1)
    given, w = {}, {}
    for name, v in arrays.items():
        v = _np.ascontiguousarray(v)
        given[f"in_{name}"] = v
        w[name] = nc.dram_tensor(f"in_{name}", v.shape, _mybir.dt.from_np(v.dtype), kind="ExternalInput").ap()
    out = nc.dram_tensor("out", (nodes, D), _mybir.dt.float32, kind="ExternalOutput").ap()
    build(nc, w, out)
    r = _run(nc, [given], core_ids=[0])
    return r.results[0]["out"]
```
